# Optimizing a Trainium2 kernel written in Bass

```python
import numpy as np
import jax
import jax.numpy as jnp

def _softmax(x, axis=-1):
    return jax.nn.softmax(x, axis=axis)

def _gelu(x):
    return jax.nn.gelu(x, approximate=True)

def _silu(x):
    return jax.nn.silu(x)

def _sigmoid(x):
    return jax.nn.sigmoid(x)

def _layernorm(x, axis=-1, eps=1e-05):
    m = jnp.mean(x, axis=axis, keepdims=True)
    v = jnp.var(x, axis=axis, keepdims=True)
    return (x - m) / jnp.sqrt(v + eps)

def _scatter_add(tgt, idx, src, axis=0):
    return tgt.at[idx].add(src)

def _segment_sum(src, seg, n):
    return jax.ops.segment_sum(src, seg, n)
kernel_name = 'mk_xattn_seq_d4_seqx_r8_efdb36'

def setup_inputs(seed: int=0):
    np.random.seed(seed)
    _w = jnp.asarray

    def _rec_inputs():
        import jax
        import jax.numpy as jnp
        _rk = jax.random.key(seed)
        x = -0.0005146 + 1 * jax.random.normal(jax.random.fold_in(_rk, 1), (4, 256, 256), jnp.float32)
        _lenS = 256 - jax.random.randint(jax.random.fold_in(_rk, 7), (4,), 0, max(1, 256 // 4) + 1, jnp.int32)
        _lenS2 = 64 - jax.random.randint(jax.random.fold_in(_rk, 8), (4,), 0, max(1, 64 // 4) + 1, jnp.int32)
        _ctx_2048P = jax.random.normal(jax.random.fold_in(_rk, 11), (4, 16, 256), jnp.float32)
        _ctx_2048c = jax.random.dirichlet(jax.random.fold_in(_rk, 511), 0.3 * jnp.ones((16,), jnp.float32), (4, 64))
        _ctx_2048t = jnp.einsum('bsk,bkd->bsd', _ctx_2048c, _ctx_2048P)
        _ctx_2048t = _ctx_2048t * jax.lax.rsqrt(jnp.mean(jnp.square(_ctx_2048t)) + 1e-12) * 0.953939
        ctx_2048 = -0.000392918 + 0.999932 * (_ctx_2048t + 0.3 * jax.random.normal(jax.random.fold_in(_rk, 611), (4, 64, 256), jnp.float32))
        _validS = jnp.arange(256)[None, :] < _lenS[:, None]
        _validS2 = jnp.arange(64)[None, :] < _lenS2[:, None]
        _causal = jnp.tril(jnp.ones((256, 256), dtype=bool))
        mask_BxS2_ik0 = jnp.where(jnp.broadcast_to(_validS2[:, :], (4, 64)), 0, 1).astype(jnp.int32)
        mask_Bx1xSxS2_ff0 = jnp.where(jnp.ones((4, 1, 256, 64), dtype=bool), 0.0, -1000000000.0).astype(jnp.float32)
        mask_BxS2_bf1 = jnp.ones((4, 64), dtype=bool)
        return (x, ctx_2048, mask_BxS2_ik0, mask_Bx1xSxS2_ff0, mask_BxS2_bf1)
    x, ctx_2048, mask_BxS2_ik0, mask_Bx1xSxS2_ff0, mask_BxS2_bf1 = _rec_inputs()

    def _L0_xattn_setup():
        import jax, jax.numpy as jnp
        import numpy as np
        B, P, K, H, NH = (4, 256, 32, 256, 16)
        DH = H // NH
        EPS = 1e-06

        def rmsnorm(x, w):
            var = jnp.mean(jnp.square(x), axis=-1, keepdims=True)
            return x * jax.lax.rsqrt(var + EPS) * w
        key = jax.random.key(seed)
        ks = jax.random.split(key, 12)
        s = 0.02
        return {'x': jax.random.normal(ks[0], (B, P, H), jnp.float32), 'latents': jax.random.normal(ks[1], (B, K, H), jnp.float32), 'attention_mask': jax.random.randint(ks[2], (B, P), 0, 2, jnp.int32), 'q_w': s * jax.random.normal(ks[3], (H, H), jnp.float32), 'q_b': jnp.zeros((H,), jnp.float32), 'kv_w': s * jax.random.normal(ks[4], (H, 2 * H), jnp.float32), 'kv_b': jnp.zeros((2 * H,), jnp.float32), 'out_w': s * jax.random.normal(ks[5], (H, H), jnp.float32), 'out_b': jnp.zeros((H,), jnp.float32), 'postnorm_w': jnp.ones((H,), jnp.float32), 'mlp_w1': s * jax.random.normal(ks[6], (H, 4 * H), jnp.float32), 'mlp_b1': jnp.zeros((4 * H,), jnp.float32), 'mlp_w2': s * jax.random.normal(ks[7], (4 * H, H), jnp.float32), 'mlp_b2': jnp.zeros((H,), jnp.float32)}
    _L0_xattn_all = _L0_xattn_setup()
    _L0_xattn_in = {k: v for k, v in _L0_xattn_all.items() if k in ('q_w', 'q_b', 'kv_w', 'kv_b', 'out_w', 'out_b', 'postnorm_w', 'mlp_w1', 'mlp_b1', 'mlp_w2', 'mlp_b2')}
    del _L0_xattn_all

    def _L1_xattn_setup():
        import jax, jax.numpy as jnp
        import numpy as np
        H = 256
        NH = 32
        KVH = 8
        HD = H // NH
        GROUPS = NH // KVH
        EPS = 1e-06
        B, L, S = (4, 128, 128)

        def _gqa_forward(hidden_state, encoder_hidden_state, encoder_attention_mask, Wq, bq, Wk, bk, Wv, bv, Wo, bo, gamma, beta):
            b, l, _ = hidden_state.shape
            s = encoder_hidden_state.shape[1]
            q = hidden_state @ Wq + bq
            k = encoder_hidden_state @ Wk + bk
            v = encoder_hidden_state @ Wv + bv
            q = q.reshape(b, l, KVH, GROUPS, HD).transpose(0, 2, 3, 1, 4)
            k = k.reshape(b, s, KVH, HD).transpose(0, 2, 1, 3)
            v = v.reshape(b, s, KVH, HD).transpose(0, 2, 1, 3)
            scale = 1.0 / jnp.sqrt(jnp.asarray(HD, q.dtype))
            scores = jnp.einsum('bkgld,bksd->bkgls', q, k) * scale
            scores = scores + encoder_attention_mask[:, :, None, :, :]
            attn = jax.nn.softmax(scores, axis=-1)
            out = jnp.einsum('bkgls,bksd->bkgld', attn, v)
            out = out.transpose(0, 3, 1, 2, 4).reshape(b, l, H)
            out = out @ Wo + bo
            x = out + hidden_state
            mu = jnp.mean(x, axis=-1, keepdims=True)
            var = jnp.var(x, axis=-1, keepdims=True)
            return (x - mu) * jax.lax.rsqrt(var + EPS) * gamma + beta
        key = jax.random.key(seed)
        ks = jax.random.split(key, 12)
        sd = 0.02
        return {'hidden_state': jax.random.normal(ks[0], (B, L, H), jnp.float32), 'encoder_hidden_state': jax.random.normal(ks[1], (B, S, H), jnp.float32), 'encoder_attention_mask': jnp.zeros((B, 1, L, S), jnp.float32), 'Wq': jax.random.normal(ks[2], (H, H), jnp.float32) * sd, 'bq': jnp.zeros((H,), jnp.float32), 'Wk': jax.random.normal(ks[3], (H, KVH * HD), jnp.float32) * sd, 'bk': jnp.zeros((KVH * HD,), jnp.float32), 'Wv': jax.random.normal(ks[4], (H, KVH * HD), jnp.float32) * sd, 'bv': jnp.zeros((KVH * HD,), jnp.float32), 'Wo': jax.random.normal(ks[5], (H, H), jnp.float32) * sd, 'bo': jnp.zeros((H,), jnp.float32), 'gamma': jnp.ones((H,), jnp.float32), 'beta': jnp.zeros((H,), jnp.float32)}
    _L1_xattn_all = _L1_xattn_setup()
    _L1_xattn_in = {k: v for k, v in _L1_xattn_all.items() if k in ('Wq', 'bq', 'Wk', 'bk', 'Wv', 'bv', 'Wo', 'bo', 'gamma', 'beta')}
    del _L1_xattn_all

    def _L2_xattn_setup():
        import jax, jax.numpy as jnp
        import numpy as np
        B, Q, S1, S2 = (4, 32, 256, 256)
        D, H, K, F = (256, 16, 128, 1024)
        LN_EPS = 1e-05

        def _layer_norm(x, scale, offset):
            mu = jnp.mean(x, axis=-1, keepdims=True)
            var = jnp.var(x, axis=-1, keepdims=True)
            return (x - mu) * jax.lax.rsqrt(var + LN_EPS) * scale + offset

        def _cross_attention(q_in, kv_in, wq, bq, wk, bk, wv, bv, wo, bo, bias_k, bias_v):
            b, q_len, _ = q_in.shape
            t = kv_in.shape[1]
            qh = (q_in @ wq + bq).reshape(b, q_len, H, K)
            kh = (kv_in @ wk + bk).reshape(b, t, H, K)
            vh = (kv_in @ wv + bv).reshape(b, t, H, K)
            kh = jnp.concatenate([kh, jnp.broadcast_to(bias_k, (b, 1, H, K))], axis=1)
            vh = jnp.concatenate([vh, jnp.broadcast_to(bias_v, (b, 1, H, K))], axis=1)
            scale = jnp.sqrt(jnp.asarray(K, q_in.dtype))
            logits = jnp.einsum('bqhk,bthk->bhqt', qh, kh) / scale
            weights = jax.nn.softmax(logits, axis=-1)
            ctx = jnp.einsum('bhqt,bthk->bqhk', weights, vh).reshape(b, q_len, H * K)
            return ctx @ wo + bo

        def _forward(x, xf_1, xf_2, ln1_scale, ln1_offset, wq1, bq1, wk1, bk1, wv1, bv1, wo1, bo1, bias_k1, bias_v1, ln2_scale, ln2_offset, wq2, bq2, wk2, bk2, wv2, bv2, wo2, bo2, bias_k2, bias_v2, ln_mlp_scale, ln_mlp_offset, w_fc1, b_fc1, w_fc2, b_fc2):
            res = x
            h = _layer_norm(x, ln1_scale, ln1_offset)
            x = res + _cross_attention(h, xf_1, wq1, bq1, wk1, bk1, wv1, bv1, wo1, bo1, bias_k1, bias_v1)
            res = x
            h = _layer_norm(x, ln2_scale, ln2_offset)
            x = res + _cross_attention(h, xf_2, wq2, bq2, wk2, bk2, wv2, bv2, wo2, bo2, bias_k2, bias_v2)
            h = _layer_norm(x, ln_mlp_scale, ln_mlp_offset)
            h = jax.nn.gelu(h @ w_fc1 + b_fc1, approximate=False) @ w_fc2 + b_fc2
            return x + h
        key = jax.random.key(seed)
        ks = iter(jax.random.split(key, 64))

        def rn(shape, s=0.02):
            return jax.random.normal(next(ks), shape, jnp.float32) * s
        inp = {'x': rn((B, Q, D), 1.0), 'xf_1': rn((B, S1, D), 1.0), 'xf_2': rn((B, S2, D), 1.0)}
        for i in (1, 2):
            inp[f'ln{i}_scale'] = jnp.ones((D,), jnp.float32)
            inp[f'ln{i}_offset'] = jnp.zeros((D,), jnp.float32)
            inp[f'wq{i}'] = rn((D, H * K))
            inp[f'bq{i}'] = jnp.zeros((H * K,), jnp.float32)
            inp[f'wk{i}'] = rn((D, H * K))
            inp[f'bk{i}'] = jnp.zeros((H * K,), jnp.float32)
            inp[f'wv{i}'] = rn((D, H * K))
            inp[f'bv{i}'] = jnp.zeros((H * K,), jnp.float32)
            inp[f'wo{i}'] = rn((H * K, D))
            inp[f'bo{i}'] = jnp.zeros((D,), jnp.float32)
            inp[f'bias_k{i}'] = rn((1, 1, H, K))
            inp[f'bias_v{i}'] = rn((1, 1, H, K))
        inp['ln_mlp_scale'] = jnp.ones((D,), jnp.float32)
        inp['ln_mlp_offset'] = jnp.zeros((D,), jnp.float32)
        inp['w_fc1'] = rn((D, F))
        inp['b_fc1'] = jnp.zeros((F,), jnp.float32)
        inp['w_fc2'] = rn((F, D))
        inp['b_fc2'] = jnp.zeros((D,), jnp.float32)
        return inp
    _L2_xattn_all = _L2_xattn_setup()
    _L2_xattn_in = {k: v for k, v in _L2_xattn_all.items() if k in ('ln1_scale', 'ln1_offset', 'wq1', 'bq1', 'wk1', 'bk1', 'wv1', 'bv1', 'wo1', 'bo1', 'bias_k1', 'bias_v1', 'ln2_scale', 'ln2_offset', 'wq2', 'bq2', 'wk2', 'bk2', 'wv2', 'bv2', 'wo2', 'bo2', 'bias_k2', 'bias_v2', 'ln_mlp_scale', 'ln_mlp_offset', 'w_fc1', 'b_fc1', 'w_fc2', 'b_fc2')}
    del _L2_xattn_all

    def _L3_xattn_setup():
        import jax, jax.numpy as jnp
        import numpy as np
        D = 256
        H = 16
        HD = D // H
        INNER = 4 * D
        EPS = 1e-05

        def layer_norm(x, w, b):
            mu = jnp.mean(x, axis=-1, keepdims=True)
            var = jnp.mean(jnp.square(x - mu), axis=-1, keepdims=True)
            return (x - mu) * jax.lax.rsqrt(var + EPS) * w + b
        key = jax.random.key(seed)
        ks = jax.random.split(key, 12)
        B, LQ, LK = (4, 128, 256)
        std = 0.02
        inp = {'hidden_states': jax.random.normal(ks[0], (B, LQ, D), jnp.float32), 'encoder_hidden_states': jax.random.normal(ks[1], (B, LK, D), jnp.float32), 'encoder_attention_mask': jnp.ones((B, LK), dtype=bool), 'ln1_w': jnp.ones((D,), jnp.float32), 'ln1_b': jnp.zeros((D,), jnp.float32), 'q_w': jax.random.normal(ks[2], (D, D), jnp.float32) * std, 'q_b': jnp.zeros((D,), jnp.float32), 'k_w': jax.random.normal(ks[3], (D, D), jnp.float32) * std, 'k_b': jnp.zeros((D,), jnp.float32), 'v_w': jax.random.normal(ks[4], (D, D), jnp.float32) * std, 'v_b': jnp.zeros((D,), jnp.float32), 'cproj_w': jax.random.normal(ks[5], (D, D), jnp.float32) * std, 'cproj_b': jnp.zeros((D,), jnp.float32), 'ln2_w': jnp.ones((D,), jnp.float32), 'ln2_b': jnp.zeros((D,), jnp.float32), 'fc_w': jax.random.normal(ks[6], (D, INNER), jnp.float32) * std, 'fc_b': jnp.zeros((INNER,), jnp.float32), 'proj_w': jax.random.normal(ks[7], (INNER, D), jnp.float32) * std, 'proj_b': jnp.zeros((D,), jnp.float32)}
        return inp
    _L3_xattn_all = _L3_xattn_setup()
    _L3_xattn_in = {k: v for k, v in _L3_xattn_all.items() if k in ('ln1_w', 'ln1_b', 'q_w', 'q_b', 'k_w', 'k_b', 'v_w', 'v_b', 'cproj_w', 'cproj_b', 'ln2_w', 'ln2_b', 'fc_w', 'fc_b', 'proj_w', 'proj_b')}
    del _L3_xattn_all
    return {'x': x, 'ctx_2048': ctx_2048, 'mask_BxS2_ik0': mask_BxS2_ik0, 'mask_Bx1xSxS2_ff0': mask_Bx1xSxS2_ff0, 'mask_BxS2_bf1': mask_BxS2_bf1, 'L0_xattn_q_w': _L0_xattn_in['q_w'], 'L0_xattn_q_b': _L0_xattn_in['q_b'], 'L0_xattn_kv_w': _L0_xattn_in['kv_w'], 'L0_xattn_kv_b': _L0_xattn_in['kv_b'], 'L0_xattn_out_w': _L0_xattn_in['out_w'], 'L0_xattn_out_b': _L0_xattn_in['out_b'], 'L0_xattn_postnorm_w': _L0_xattn_in['postnorm_w'], 'L0_xattn_mlp_w1': _L0_xattn_in['mlp_w1'], 'L0_xattn_mlp_b1': _L0_xattn_in['mlp_b1'], 'L0_xattn_mlp_w2': _L0_xattn_in['mlp_w2'], 'L0_xattn_mlp_b2': _L0_xattn_in['mlp_b2'], 'L1_xattn_Wq': _L1_xattn_in['Wq'], 'L1_xattn_bq': _L1_xattn_in['bq'], 'L1_xattn_Wk': _L1_xattn_in['Wk'], 'L1_xattn_bk': _L1_xattn_in['bk'], 'L1_xattn_Wv': _L1_xattn_in['Wv'], 'L1_xattn_bv': _L1_xattn_in['bv'], 'L1_xattn_Wo': _L1_xattn_in['Wo'], 'L1_xattn_bo': _L1_xattn_in['bo'], 'L1_xattn_gamma': _L1_xattn_in['gamma'], 'L1_xattn_beta': _L1_xattn_in['beta'], 'L2_xattn_ln1_scale': _L2_xattn_in['ln1_scale'], 'L2_xattn_ln1_offset': _L2_xattn_in['ln1_offset'], 'L2_xattn_wq1': _L2_xattn_in['wq1'], 'L2_xattn_bq1': _L2_xattn_in['bq1'], 'L2_xattn_wk1': _L2_xattn_in['wk1'], 'L2_xattn_bk1': _L2_xattn_in['bk1'], 'L2_xattn_wv1': _L2_xattn_in['wv1'], 'L2_xattn_bv1': _L2_xattn_in['bv1'], 'L2_xattn_wo1': _L2_xattn_in['wo1'], 'L2_xattn_bo1': _L2_xattn_in['bo1'], 'L2_xattn_bias_k1': _L2_xattn_in['bias_k1'], 'L2_xattn_bias_v1': _L2_xattn_in['bias_v1'], 'L2_xattn_ln2_scale': _L2_xattn_in['ln2_scale'], 'L2_xattn_ln2_offset': _L2_xattn_in['ln2_offset'], 'L2_xattn_wq2': _L2_xattn_in['wq2'], 'L2_xattn_bq2': _L2_xattn_in['bq2'], 'L2_xattn_wk2': _L2_xattn_in['wk2'], 'L2_xattn_bk2': _L2_xattn_in['bk2'], 'L2_xattn_wv2': _L2_xattn_in['wv2'], 'L2_xattn_bv2': _L2_xattn_in['bv2'], 'L2_xattn_wo2': _L2_xattn_in['wo2'], 'L2_xattn_bo2': _L2_xattn_in['bo2'], 'L2_xattn_bias_k2': _L2_xattn_in['bias_k2'], 'L2_xattn_bias_v2': _L2_xattn_in['bias_v2'], 'L2_xattn_ln_mlp_scale': _L2_xattn_in['ln_mlp_scale'], 'L2_xattn_ln_mlp_offset': _L2_xattn_in['ln_mlp_offset'], 'L2_xattn_w_fc1': _L2_xattn_in['w_fc1'], 'L2_xattn_b_fc1': _L2_xattn_in['b_fc1'], 'L2_xattn_w_fc2': _L2_xattn_in['w_fc2'], 'L2_xattn_b_fc2': _L2_xattn_in['b_fc2'], 'L3_xattn_ln1_w': _L3_xattn_in['ln1_w'], 'L3_xattn_ln1_b': _L3_xattn_in['ln1_b'], 'L3_xattn_q_w': _L3_xattn_in['q_w'], 'L3_xattn_q_b': _L3_xattn_in['q_b'], 'L3_xattn_k_w': _L3_xattn_in['k_w'], 'L3_xattn_k_b': _L3_xattn_in['k_b'], 'L3_xattn_v_w': _L3_xattn_in['v_w'], 'L3_xattn_v_b': _L3_xattn_in['v_b'], 'L3_xattn_cproj_w': _L3_xattn_in['cproj_w'], 'L3_xattn_cproj_b': _L3_xattn_in['cproj_b'], 'L3_xattn_ln2_w': _L3_xattn_in['ln2_w'], 'L3_xattn_ln2_b': _L3_xattn_in['ln2_b'], 'L3_xattn_fc_w': _L3_xattn_in['fc_w'], 'L3_xattn_fc_b': _L3_xattn_in['fc_b'], 'L3_xattn_proj_w': _L3_xattn_in['proj_w'], 'L3_xattn_proj_b': _L3_xattn_in['proj_b']}

def reference(x, ctx_2048, mask_BxS2_ik0, mask_Bx1xSxS2_ff0, mask_BxS2_bf1, L0_xattn_q_w, L0_xattn_q_b, L0_xattn_kv_w, L0_xattn_kv_b, L0_xattn_out_w, L0_xattn_out_b, L0_xattn_postnorm_w, L0_xattn_mlp_w1, L0_xattn_mlp_b1, L0_xattn_mlp_w2, L0_xattn_mlp_b2, L1_xattn_Wq, L1_xattn_bq, L1_xattn_Wk, L1_xattn_bk, L1_xattn_Wv, L1_xattn_bv, L1_xattn_Wo, L1_xattn_bo, L1_xattn_gamma, L1_xattn_beta, L2_xattn_ln1_scale, L2_xattn_ln1_offset, L2_xattn_wq1, L2_xattn_bq1, L2_xattn_wk1, L2_xattn_bk1, L2_xattn_wv1, L2_xattn_bv1, L2_xattn_wo1, L2_xattn_bo1, L2_xattn_bias_k1, L2_xattn_bias_v1, L2_xattn_ln2_scale, L2_xattn_ln2_offset, L2_xattn_wq2, L2_xattn_bq2, L2_xattn_wk2, L2_xattn_bk2, L2_xattn_wv2, L2_xattn_bv2, L2_xattn_wo2, L2_xattn_bo2, L2_xattn_bias_k2, L2_xattn_bias_v2, L2_xattn_ln_mlp_scale, L2_xattn_ln_mlp_offset, L2_xattn_w_fc1, L2_xattn_b_fc1, L2_xattn_w_fc2, L2_xattn_b_fc2, L3_xattn_ln1_w, L3_xattn_ln1_b, L3_xattn_q_w, L3_xattn_q_b, L3_xattn_k_w, L3_xattn_k_b, L3_xattn_v_w, L3_xattn_v_b, L3_xattn_cproj_w, L3_xattn_cproj_b, L3_xattn_ln2_w, L3_xattn_ln2_b, L3_xattn_fc_w, L3_xattn_fc_b, L3_xattn_proj_w, L3_xattn_proj_b):
    import jax
    import jax.numpy as jnp

    def _L0_xattn_ref(x, latents, attention_mask, q_w, q_b, kv_w, kv_b, out_w, out_b, postnorm_w, mlp_w1, mlp_b1, mlp_w2, mlp_b2):
        import jax, jax.numpy as jnp
        import numpy as np
        B, P, K, H, NH = (4, 256, 32, 256, 16)
        DH = H // NH
        EPS = 1e-06

        def rmsnorm(x, w):
            var = jnp.mean(jnp.square(x), axis=-1, keepdims=True)
            return x * jax.lax.rsqrt(var + EPS) * w
        b, p, _ = x.shape
        k_len = latents.shape[1]
        residual = latents
        h = jnp.concatenate([x, latents], axis=1)
        q = (latents @ q_w + q_b).reshape(b, k_len, NH, DH)
        kv = (h @ kv_w + kv_b).reshape(b, p + k_len, NH, DH, 2)
        kmat, v = (kv[..., 0], kv[..., 1])
        attn = jnp.einsum('bkhd,bnhd->bhkn', q, kmat) / DH
        full_mask = jnp.concatenate([attention_mask.astype(bool), jnp.ones((b, k_len), bool)], axis=-1)
        attn = jnp.where(full_mask[:, None, None, :], attn, -jnp.inf)
        attn = jax.nn.softmax(attn.astype(jnp.float32), axis=-1).astype(q.dtype)
        attn_out = jnp.einsum('bhkn,bnhd->bkhd', attn, v).reshape(b, k_len, H)
        attn_out = attn_out @ out_w + out_b + residual
        out = rmsnorm(attn_out, postnorm_w)
        out = jax.nn.gelu(out @ mlp_w1 + mlp_b1) @ mlp_w2 + mlp_b2
        return out + residual

    def _L1_xattn_ref(hidden_state, encoder_hidden_state, encoder_attention_mask, Wq, bq, Wk, bk, Wv, bv, Wo, bo, gamma, beta):
        import jax, jax.numpy as jnp
        import numpy as np
        H = 256
        NH = 32
        KVH = 8
        HD = H // NH
        GROUPS = NH // KVH
        EPS = 1e-06
        B, L, S = (4, 128, 128)

        def _gqa_forward(hidden_state, encoder_hidden_state, encoder_attention_mask, Wq, bq, Wk, bk, Wv, bv, Wo, bo, gamma, beta):
            b, l, _ = hidden_state.shape
            s = encoder_hidden_state.shape[1]
            q = hidden_state @ Wq + bq
            k = encoder_hidden_state @ Wk + bk
            v = encoder_hidden_state @ Wv + bv
            q = q.reshape(b, l, KVH, GROUPS, HD).transpose(0, 2, 3, 1, 4)
            k = k.reshape(b, s, KVH, HD).transpose(0, 2, 1, 3)
            v = v.reshape(b, s, KVH, HD).transpose(0, 2, 1, 3)
            scale = 1.0 / jnp.sqrt(jnp.asarray(HD, q.dtype))
            scores = jnp.einsum('bkgld,bksd->bkgls', q, k) * scale
            scores = scores + encoder_attention_mask[:, :, None, :, :]
            attn = jax.nn.softmax(scores, axis=-1)
            out = jnp.einsum('bkgls,bksd->bkgld', attn, v)
            out = out.transpose(0, 3, 1, 2, 4).reshape(b, l, H)
            out = out @ Wo + bo
            x = out + hidden_state
            mu = jnp.mean(x, axis=-1, keepdims=True)
            var = jnp.var(x, axis=-1, keepdims=True)
            return (x - mu) * jax.lax.rsqrt(var + EPS) * gamma + beta
        return _gqa_forward(hidden_state, encoder_hidden_state, encoder_attention_mask, Wq, bq, Wk, bk, Wv, bv, Wo, bo, gamma, beta)

    def _L2_xattn_ref(x, xf_1, xf_2, ln1_scale, ln1_offset, wq1, bq1, wk1, bk1, wv1, bv1, wo1, bo1, bias_k1, bias_v1, ln2_scale, ln2_offset, wq2, bq2, wk2, bk2, wv2, bv2, wo2, bo2, bias_k2, bias_v2, ln_mlp_scale, ln_mlp_offset, w_fc1, b_fc1, w_fc2, b_fc2):
        import jax, jax.numpy as jnp
        import numpy as np
        B, Q, S1, S2 = (4, 32, 256, 256)
        D, H, K, F = (256, 16, 128, 1024)
        LN_EPS = 1e-05

        def _layer_norm(x, scale, offset):
            mu = jnp.mean(x, axis=-1, keepdims=True)
            var = jnp.var(x, axis=-1, keepdims=True)
            return (x - mu) * jax.lax.rsqrt(var + LN_EPS) * scale + offset

        def _cross_attention(q_in, kv_in, wq, bq, wk, bk, wv, bv, wo, bo, bias_k, bias_v):
            b, q_len, _ = q_in.shape
            t = kv_in.shape[1]
            qh = (q_in @ wq + bq).reshape(b, q_len, H, K)
            kh = (kv_in @ wk + bk).reshape(b, t, H, K)
            vh = (kv_in @ wv + bv).reshape(b, t, H, K)
            kh = jnp.concatenate([kh, jnp.broadcast_to(bias_k, (b, 1, H, K))], axis=1)
            vh = jnp.concatenate([vh, jnp.broadcast_to(bias_v, (b, 1, H, K))], axis=1)
            scale = jnp.sqrt(jnp.asarray(K, q_in.dtype))
            logits = jnp.einsum('bqhk,bthk->bhqt', qh, kh) / scale
            weights = jax.nn.softmax(logits, axis=-1)
            ctx = jnp.einsum('bhqt,bthk->bqhk', weights, vh).reshape(b, q_len, H * K)
            return ctx @ wo + bo

        def _forward(x, xf_1, xf_2, ln1_scale, ln1_offset, wq1, bq1, wk1, bk1, wv1, bv1, wo1, bo1, bias_k1, bias_v1, ln2_scale, ln2_offset, wq2, bq2, wk2, bk2, wv2, bv2, wo2, bo2, bias_k2, bias_v2, ln_mlp_scale, ln_mlp_offset, w_fc1, b_fc1, w_fc2, b_fc2):
            res = x
            h = _layer_norm(x, ln1_scale, ln1_offset)
            x = res + _cross_attention(h, xf_1, wq1, bq1, wk1, bk1, wv1, bv1, wo1, bo1, bias_k1, bias_v1)
            res = x
            h = _layer_norm(x, ln2_scale, ln2_offset)
            x = res + _cross_attention(h, xf_2, wq2, bq2, wk2, bk2, wv2, bv2, wo2, bo2, bias_k2, bias_v2)
            h = _layer_norm(x, ln_mlp_scale, ln_mlp_offset)
            h = jax.nn.gelu(h @ w_fc1 + b_fc1, approximate=False) @ w_fc2 + b_fc2
            return x + h
        return _forward(x, xf_1, xf_2, ln1_scale, ln1_offset, wq1, bq1, wk1, bk1, wv1, bv1, wo1, bo1, bias_k1, bias_v1, ln2_scale, ln2_offset, wq2, bq2, wk2, bk2, wv2, bv2, wo2, bo2, bias_k2, bias_v2, ln_mlp_scale, ln_mlp_offset, w_fc1, b_fc1, w_fc2, b_fc2)

    def _L3_xattn_ref(hidden_states, encoder_hidden_states, encoder_attention_mask, ln1_w, ln1_b, q_w, q_b, k_w, k_b, v_w, v_b, cproj_w, cproj_b, ln2_w, ln2_b, fc_w, fc_b, proj_w, proj_b):
        import jax, jax.numpy as jnp
        import numpy as np
        D = 256
        H = 16
        HD = D // H
        INNER = 4 * D
        EPS = 1e-05

        def layer_norm(x, w, b):
            mu = jnp.mean(x, axis=-1, keepdims=True)
            var = jnp.mean(jnp.square(x - mu), axis=-1, keepdims=True)
            return (x - mu) * jax.lax.rsqrt(var + EPS) * w + b
        B, LQ, _ = hidden_states.shape
        LK = encoder_hidden_states.shape[1]
        residual = hidden_states
        x = layer_norm(hidden_states, ln1_w, ln1_b)
        q = (x @ q_w + q_b).reshape(B, LQ, H, HD).transpose(0, 2, 1, 3)
        k = (encoder_hidden_states @ k_w + k_b).reshape(B, LK, H, HD).transpose(0, 2, 1, 3)
        v = (encoder_hidden_states @ v_w + v_b).reshape(B, LK, H, HD).transpose(0, 2, 1, 3)
        scale = 1.0 / np.sqrt(HD).astype(np.float32)
        scores = jnp.einsum('bhqd,bhkd->bhqk', q, k) * scale
        mask = encoder_attention_mask[:, None, None, :]
        mask_value = jnp.finfo(scores.dtype).min
        scores = jnp.where(mask, scores, mask_value)
        attn = jax.nn.softmax(scores, axis=-1)
        out = jnp.einsum('bhqk,bhkd->bhqd', attn, v)
        out = out.transpose(0, 2, 1, 3).reshape(B, LQ, D)
        out = out @ cproj_w + cproj_b
        hidden = out + residual
        residual = hidden
        y = layer_norm(hidden, ln2_w, ln2_b)
        y = jax.nn.gelu(y @ fc_w + fc_b, approximate=True)
        y = y @ proj_w + proj_b
        return residual + y
    x = _L0_xattn_ref(ctx_2048, x, mask_BxS2_ik0, L0_xattn_q_w, L0_xattn_q_b, L0_xattn_kv_w, L0_xattn_kv_b, L0_xattn_out_w, L0_xattn_out_b, L0_xattn_postnorm_w, L0_xattn_mlp_w1, L0_xattn_mlp_b1, L0_xattn_mlp_w2, L0_xattn_mlp_b2)
    x = _L1_xattn_ref(x, ctx_2048, mask_Bx1xSxS2_ff0, L1_xattn_Wq, L1_xattn_bq, L1_xattn_Wk, L1_xattn_bk, L1_xattn_Wv, L1_xattn_bv, L1_xattn_Wo, L1_xattn_bo, L1_xattn_gamma, L1_xattn_beta)
    x = _L2_xattn_ref(x, ctx_2048, ctx_2048, L2_xattn_ln1_scale, L2_xattn_ln1_offset, L2_xattn_wq1, L2_xattn_bq1, L2_xattn_wk1, L2_xattn_bk1, L2_xattn_wv1, L2_xattn_bv1, L2_xattn_wo1, L2_xattn_bo1, L2_xattn_bias_k1, L2_xattn_bias_v1, L2_xattn_ln2_scale, L2_xattn_ln2_offset, L2_xattn_wq2, L2_xattn_bq2, L2_xattn_wk2, L2_xattn_bk2, L2_xattn_wv2, L2_xattn_bv2, L2_xattn_wo2, L2_xattn_bo2, L2_xattn_bias_k2, L2_xattn_bias_v2, L2_xattn_ln_mlp_scale, L2_xattn_ln_mlp_offset, L2_xattn_w_fc1, L2_xattn_b_fc1, L2_xattn_w_fc2, L2_xattn_b_fc2)
    x = _L3_xattn_ref(x, ctx_2048, mask_BxS2_bf1, L3_xattn_ln1_w, L3_xattn_ln1_b, L3_xattn_q_w, L3_xattn_q_b, L3_xattn_k_w, L3_xattn_k_b, L3_xattn_v_w, L3_xattn_v_b, L3_xattn_cproj_w, L3_xattn_cproj_b, L3_xattn_ln2_w, L3_xattn_ln2_b, L3_xattn_fc_w, L3_xattn_fc_b, L3_xattn_proj_w, L3_xattn_proj_b)
    return x

_drawn_inputs = setup_inputs


def setup_inputs(seed=0):
    import zlib

    import numpy as np

    out = dict(_drawn_inputs(seed))
    spreads = {'L0_xattn_q_b': (0.0, 0.8),
     'L0_xattn_kv_b': (0.0, 0.8),
     'L0_xattn_out_b': (0.0, 0.692),
     'L0_xattn_postnorm_w': (1.0, 0.6),
     'L0_xattn_mlp_b1': (0.0, 0.1),
     'L0_xattn_mlp_b2': (0.0, 0.1),
     'L1_xattn_bq': (0.0, 0.8),
     'L1_xattn_bk': (0.0, 2.0),
     'L1_xattn_bv': (0.0, 0.267),
     'L1_xattn_bo': (0.0, 0.1),
     'L1_xattn_gamma': (1.0, 0.2),
     'L1_xattn_beta': (0.0, 0.1),
     'L2_xattn_ln1_scale': (1.0, 0.6),
     'L2_xattn_ln1_offset': (0.0, 0.8),
     'L2_xattn_bq1': (0.0, 0.8),
     'L2_xattn_bk1': (0.0, 2.0),
     'L2_xattn_bv1': (0.0, 0.1),
     'L2_xattn_bo1': (0.0, 0.1),
     'L2_xattn_ln2_scale': (1.0, 0.6),
     'L2_xattn_ln2_offset': (0.0, 0.8),
     'L2_xattn_bq2': (0.0, 0.8),
     'L2_xattn_bk2': (0.0, 2.0),
     'L2_xattn_bv2': (0.0, 0.1),
     'L2_xattn_bo2': (0.0, 0.1),
     'L2_xattn_ln_mlp_scale': (1.0, 0.6),
     'L2_xattn_ln_mlp_offset': (0.0, 0.8),
     'L2_xattn_b_fc1': (0.0, 0.1),
     'L2_xattn_b_fc2': (0.0, 0.1),
     'L3_xattn_ln1_w': (1.0, 0.6),
     'L3_xattn_ln1_b': (0.0, 0.8),
     'L3_xattn_q_b': (0.0, 0.8),
     'L3_xattn_k_b': (0.0, 2.0),
     'L3_xattn_v_b': (0.0, 0.276),
     'L3_xattn_cproj_b': (0.0, 0.1),
     'L3_xattn_ln2_w': (1.0, 0.6),
     'L3_xattn_ln2_b': (0.0, 0.733),
     'L3_xattn_fc_b': (0.0, 0.271),
     'L3_xattn_proj_b': (0.0, 0.1)}
    factors = {'L0_xattn_q_w': 8.0,
     'L0_xattn_kv_w': 8.0,
     'L0_xattn_out_w': 8.0,
     'L1_xattn_Wq': 8.0,
     'L1_xattn_Wk': 8.0,
     'L2_xattn_wq1': 8.0,
     'L2_xattn_wk1': 8.0,
     'L2_xattn_bias_k1': 64.0,
     'L2_xattn_bias_v1': 52.283,
     'L2_xattn_wq2': 8.0,
     'L2_xattn_wk2': 8.0,
     'L2_xattn_bias_k2': 64.0,
     'L2_xattn_bias_v2': 64.0,
     'L3_xattn_q_w': 8.0,
     'L3_xattn_k_w': 8.0}
    for name, (base, spread) in spreads.items():
        noise = np.random.default_rng([zlib.crc32(name.encode()), seed]).standard_normal(out[name].shape)
        drawn = base * np.exp(spread * noise) if base else spread * noise
        out[name] = jnp.asarray(drawn.astype(out[name].dtype))
    for name, factor in factors.items():
        out[name] = (out[name] * factor).astype(out[name].dtype)
    return out
```

```python
from contextlib import ExitStack

import concourse.bass as bass
from concourse import mybir

P = 128
B, S, D, T = 4, 256, 256, 64
NQ = B * S // P
NC = D // P
F = 4 * D
NF = F // P
H2, DH2 = 16, 128
NK2 = B * T + 1
KEYS0 = S + T
GROUP = 4
NEG0 = -1.0e30
NEG3 = -3.4028234663852886e38
SCORES, TURNS = (0, 1), (2,)
ALU = mybir.AluOpType
ACT = mybir.ActivationFunctionType
AX = mybir.AxisListType.X
F32 = mybir.dt.float32
I32 = mybir.dt.int32
U8 = mybir.dt.uint8

COLUMNS = [
    ("L0_q_b", 2), ("L0_k_b", 2), ("L0_v_b", 2), ("L0_postnorm_w", 2), ("L0_mlp_b1", 8),
    ("L1_bq", 2), ("L1_bk", 2), ("L1_bv", 2),
    ("L2_ln1_scale", 2), ("L2_ln1_offset", 2), ("L2_bq1", 16), ("L2_bk1", 16), ("L2_bv1", 16),
    ("L2_bias_k1", 16), ("L2_bias_v1", 16),
    ("L2_ln2_scale", 2), ("L2_ln2_offset", 2), ("L2_bq2", 16), ("L2_bk2", 16), ("L2_bv2", 16),
    ("L2_bias_k2", 16), ("L2_bias_v2", 16), ("L2_ln_mlp_scale", 2), ("L2_ln_mlp_offset", 2),
    ("L2_b_fc1", 8),
    ("L3_ln1_w", 2), ("L3_ln1_b", 2), ("L3_q_b", 2), ("L3_k_b", 2), ("L3_v_b", 2),
    ("L3_ln2_w", 2), ("L3_ln2_b", 2), ("L3_fc_b", 8),
]
ROWS = ["L0_out_b", "L0_mlp_b2", "L1_bo", "L1_gamma", "L1_beta", "L2_bo1", "L2_bo2", "L2_b_fc2",
        "L3_cproj_b", "L3_proj_b"]


class Ring:

    def __init__(self, filled, drained):
        self.filled, self.drained = filled, drained
        self.uses = [0] * len(filled)
        self.owed = [0] * len(filled)
        self.order = list(range(len(filled)))
        self.tiles = {}

    def take(self, key, drains=1, among=(0, 1, 2)):
        s = next(x for x in self.order if x in among)
        before = self.owed[s]
        self.order.remove(s)
        self.order.append(s)
        self.uses[s] += 1
        self.owed[s] += drains
        self.tiles[key] = (s, self.uses[s], self.owed[s])
        return s, before

    def slot(self, key):
        return self.tiles[key][0]

    def full(self, key):
        s, n, _ = self.tiles[key]
        return self.filled[s], n

    def empty(self, key):
        s, _, n = self.tiles[key]
        return self.drained[s], n


def build(nc, t, out):
    ctx = ExitStack()
    with ctx:
        def sb(name, shape, dt=F32):
            return ctx.enter_context(nc.sbuf_tensor(name, shape, dt))

        def sem(name):
            return ctx.enter_context(nc.semaphore(name))

        wide_ps = ctx.enter_context(nc.psum_tensor("wide_ps", [P, 3, 1024], F32))
        narrow_ps = ctx.enter_context(nc.psum_tensor("narrow_ps", [P, 2, 512], F32))
        wide = Ring([sem(f"wide{i}_filled") for i in range(3)], [sem(f"wide{i}_drained") for i in range(3)])
        narrow = Ring([sem(f"narrow{i}_filled") for i in range(2)], [sem(f"narrow{i}_drained") for i in range(2)])

        ident = sb("ident", [P, P])
        head16 = sb("head16", [P, 8])
        head8 = sb("head8", [P, 16])
        mhalf = sb("mhalf", [P, 1])
        colraw = sb("colraw", [P, 2, P])
        col = sb("col", [P, 2, P])
        rows = sb("rows", [P, len(ROWS), D])
        mask0 = sb("mask0", [P, B, T])
        mask1 = sb("mask1", [P, NQ, T])
        mask3 = sb("mask3", [P, B, T])
        xq = sb("xq", [P, 4112])
        xA = xq[:, 0:2048].rearrange("p (q d) -> p q d", q=NQ)
        xB = sb("xB", [P, NQ, D])
        xn = sb("xn", [P, NQ, D])
        actT = sb("actT", [P, NC, B * S])
        qT = xq[:, 2048:4096].rearrange("p (c n) -> p c n", c=NC)
        ctxT = sb("ctxT", [P, NC, B * T])
        ctxD = sb("ctxD", [P, NC, B, 2, T])
        stats = sb("stats", [P, NQ, 6])
        mv = sb("mv", [P, NQ, 2])
        veps = sb("veps", [P, NQ])
        rstd = sb("rstd", [P, NQ])
        scoresb = sb("scoresb", [P, 3, 16 * 65])
        probs = sb("probs", [P, 2, 1024])
        mask0i = probs[:, 0, 0:B * T].bitcast(I32)
        mask3i = probs[:, 0, B * T:B * T + B * T // 4].bitcast(U8)
        probsb = sb("probsb", [P, 2, 16])
        probsT = sb("probsT", [P, 2, 1024])
        probsbT = sb("probsbT", [16, 2, P])
        mx = sb("mx", [P, 3, 16])
        sums = sb("sums", [P, 3, 16])
        rcp = sb("rcp", [P, 3, 16])
        wstream = sb("wstream", [P, 8192])
        wsmall = sb("wsmall", [P, 2048])
        wkrep = sb("wkrep", [P, NC, NC, P])
        bvhot = sb("bvhot", [P, H2, H2])
        vwb = sb("vwb", [16, D])
        headbuf = sb("headbuf", [P, 1568])
        heads = headbuf[:].rearrange("p (a n) -> p a n", a=2)
        kT2 = headbuf[:, 0:NC * KEYS0].rearrange("p (c n) -> p c n", c=NC)
        region = sb("region", [P, 16416])

        kbd0 = [region[:, i * 5120:(i + 1) * 5120].rearrange("p (c h k) -> p c h k", c=NC, h=8) for i in range(2)]
        vpad0 = [region[:, 10240 + i * 2560:10240 + (i + 1) * 2560] for i in range(2)]
        w0 = wstream
        q_w0 = w0[:, 0:512].rearrange("p (c n) -> p c n", c=NC)
        kv_w0 = w0[:, 512:1536].rearrange("p (c n two) -> p c two n", c=NC, two=2)
        out_w0 = w0[:, 1536:2048].rearrange("p (c n) -> p c n", c=NC)
        mlp_w1_0 = w0[:, 2048:4096].rearrange("p (c n) -> p c n", c=NC)
        mlp_w2_0 = w0[:, 4096:6144].rearrange("p (c n) -> p c n", c=NF)
        hid = region[:, 0:NF * 1024].rearrange("p (f n) -> p f n", f=NF)
        q_w1 = wsmall[:, 0:512].rearrange("p (c n) -> p c n", c=NC)
        k_w1 = wsmall[:, 512:640].rearrange("p (c n) -> p c n", c=NC)
        v_w1 = wsmall[:, 640:768].rearrange("p (c n) -> p c n", c=NC)
        out_w1 = wsmall[:, 768:1280].rearrange("p (c n) -> p c n", c=NC)
        vpad1 = region[:, 0:8192].rearrange("p (b r n) -> p b r n", b=B, r=16)
        kbd1 = region[:, 8192:16384].rearrange("p (c b h k) -> p c b h k", c=NC, b=B, h=16)
        G = region[:, 0:NC * H2 * NK2].rearrange("p (c h k) -> p c h k", c=NC, h=H2)
        VW = region[:, 8224:8224 + 8192].rearrange("p (b r n) -> p b r n", b=B, r=8)
        cB = xq[:, 0:H2 * NK2].rearrange("p (h k) -> p h k", h=H2)
        wring = [wstream[:, i * 4096:(i + 1) * 4096].rearrange("p (m n) -> p m n", m=4) for i in range(2)]
        fc1_w2 = wstream[:, 0:2048].rearrange("p (c n) -> p c n", c=NC)
        fc2_w2 = wstream[:, 2048:4096].rearrange("p (c n) -> p c n", c=NF)
        fc_w3 = wstream[:, 4096:6144].rearrange("p (c n) -> p c n", c=NC)
        proj_w3 = wstream[:, 6144:8192].rearrange("p (c n) -> p c n", c=NF)
        w3 = [wsmall[:, i * 512:(i + 1) * 512].rearrange("p (c n) -> p c n", c=NC) for i in range(4)]
        kbd3 = region[:, 8192:12288].rearrange("p (c b h k) -> p c b h k", c=NC, b=B, h=8)
        vpad3 = region[:, 12288:16384].rearrange("p (b r n) -> p b r n", b=B, r=8)

        load = {k: sem("loaded_" + k) for k in
                ("x", "ctx", "cols", "rows", "masks", "w0", "mlp0", "w1", "w3", "mlp2", "mlp3")}
        ring_loaded = [sem("ring0_loaded"), sem("ring1_loaded")]
        consts = sem("consts_ready")
        link_dve = sem("dve_step")
        link_pool = sem("pool_step")
        cols_zeroed = sem("cols_zeroed")
        stat_ready = sem("stat_ready")
        rstd_ready = sem("rstd_ready")
        xn_ready = sem("xn_ready")
        x2_ready = sem("x2_ready")
        row_added = sem("row_added")
        vzero = sem("vpad_zeroed")
        kbd_ready = sem("kbd_ready")
        vpad_ready = sem("vpad_ready")
        wk_ready = sem("wk_replicated")
        ctxd_ready = sem("ctx_doubled")
        max_ready = sem("max_ready")
        shifted = sem("scores_shifted")
        exp_done = sem("exp_done")
        rcp_ready = sem("rcp_ready")
        prob_ready = sem("probs_normalized")
        bias_key = sem("bias_key_copied")
        hot_ready = sem("bias_values_spread")
        ring_used = sem("ring_chunk_used")
        stored = sem("out_stored")

        colrow = {}
        n = 0
        for name, k in COLUMNS:
            if n // P != (n + k - 1) // P:
                n = -(-n // P) * P
            colrow[name] = (n, k)
            n += k

        def column(name, i=0):
            r = colrow[name][0] + i
            return col[:, r // P, r % P:r % P + 1]

        def row(name):
            i = ROWS.index(name)
            return rows[:, i, :]

        units0 = [(b, q, r) for b in range(B) for q in range(2) for r in range(8)]
        units1 = [(q, c) for q in range(NQ) for c in range(NC)]
        units2 = [(q,) for q in range(NQ)]
        units3 = [(q,) for q in range(NQ)]
        base = {}
        probcount = [0]
        shiftcount = [0]
        at = 0
        LOADS = {"cols": len(COLUMNS) + 2}
        for name, us in (("0", units0), ("1", units1), ("2a", units2), ("2b", units2), ("3", units3)):
            base[name] = at
            at += len(us)
            for _ in us:
                probcount.append(probcount[-1] + (1 if name in "13" else 2))
                shiftcount.append(shiftcount[-1] + (name != "0"))
        qoff = lambda q: slice(q * P, (q + 1) * P)

        def diagonal(tile, offset, dims, width=None):
            a = tile[:, offset:offset + 1] if len(tile.shape) == 2 else tile[:].rearrange("p a b -> p (a b)")[:, offset:offset + 1]
            return bass.AP(tensor=a.tensor, offset=a.offset, ap=[list(a.ap[0])] + [list(d) for d in dims])

        def colrange(name):
            r, k = colrow[name]
            return col[:, r // P, r % P:r % P + k]

        block = ctx.enter_context(nc.Block())

        @block.tensor
        def _(pe):
            mm = nc.tensor.matmul

            def take_wide(key, drains=1, among=(0, 1, 2)):
                s, before = wide.take(key, drains, among)
                if before:
                    pe.wait_ge(wide.drained[s], before)
                return wide_ps[:, s, :], wide.filled[s]

            def take_narrow(key, drains=1):
                s, before = narrow.take(key, drains)
                if before:
                    pe.wait_ge(narrow.drained[s], before)
                return narrow_ps[:, s, :], narrow.filled[s]

            def turn(key, src, ready=None, drains=1):
                for half in range(2):
                    ps, filled = take_wide((key, half), drains)
                    for j in range(4):
                        q = 4 * half + j
                        if ready:
                            ready(q)
                        for c in range(NC):
                            m = nc.tensor.transpose(ps[:, c * 512 + j * P:c * 512 + (j + 1) * P],
                                                    src[:, q, c * P:(c + 1) * P], ident[:])
                    m.then_inc(filled, 1)

            def norm_turn(k):
                turn(("ln", k), xn, lambda q: pe.wait_ge(xn_ready, k * NQ + q + 1), 2)

            def queries(layer, w, src_key):
                for c in range(NC):
                    ps, filled = take_wide(("q", layer, c))
                    for half in range(2):
                        pe.wait_ge(*wide.empty((src_key, half)))
                        for kc in range(NC):
                            m = mm(ps[:, half * 512:(half + 1) * 512], w[:, kc, c * P:(c + 1) * P],
                                   actT[:, kc, half * 512:(half + 1) * 512], start=kc == 0, stop=kc == NC - 1)
                    m.then_inc(filled, 1)

            def mlp(n, k, w1, w2):
                for half in range(2):
                    for fp in range(NF // 2):
                        ps, filled = take_wide(("up", n, half, fp), 2)
                        pe.wait_ge(*wide.empty((("ln", k), half)))
                        for j in range(2):
                            f = 2 * fp + j
                            for kc in range(NC):
                                m = mm(ps[:, j * 512:(j + 1) * 512], w1[:, kc, f * P:(f + 1) * P],
                                       actT[:, kc, half * 512:(half + 1) * 512], start=kc == 0, stop=kc == NC - 1)
                        m.then_inc(filled, 1)
                for q in range(NQ):
                    ps, filled = take_narrow(("down", n, q))
                    for fp in range(NF // 2):
                        pe.wait_ge(*wide.empty(("up", n, q // 4, fp)))
                    for f in range(NF):
                        m = mm(ps[:, 0:D], hid[:, f, qoff(q)], w2[:, f, :], start=f == 0, stop=f == NF - 1)
                    m.then_inc(filled, 1)

            def project(layer, q, w, aokeys):
                ps, filled = take_narrow(("proj", layer, q))
                for key in aokeys:
                    pe.wait_ge(*narrow.empty(key))
                for c in range(NC):
                    m = mm(ps[:, 0:D], qT[:, c, qoff(q)], w[:, c, :], start=c == 0, stop=c == NC - 1)
                m.then_inc(filled, 1)

            def turn_probs(u):
                ps, filled = take_wide(("T", u), among=TURNS)
                pe.wait_ge(prob_ready, probcount[u + 1])
                n = 5 if u < len(units0) else 8
                for j in range(n):
                    m = nc.tensor.transpose(ps[:, j * P:(j + 1) * P], probs[:, u % 2, j * P:(j + 1) * P], ident[:])
                m.then_inc(filled, 1)

            pe.wait_ge(consts, 1)
            pe.wait_ge(load["cols"], 16 * LOADS["cols"])
            ps, filled = take_wide("cols")
            for i in range(2):
                m = nc.tensor.transpose(ps[:, i * P:(i + 1) * P], colraw[:, i, :], ident[:])
            m.then_inc(filled, 1)
            pe.wait_ge(load["x"], 16)
            turn("x0T", xA)
            pe.wait_ge(load["ctx"], 16)
            ps, filled = take_wide("ctxT")
            for c in range(NC):
                for j in range(2):
                    m = nc.tensor.transpose(ps[:, c * 256 + j * P:c * 256 + (j + 1) * P],
                                            xn[:, j, c * P:(c + 1) * P], ident[:])
            m.then_inc(filled, 1)

            pe.wait_ge(load["w0"], 16 * 3)
            queries(0, q_w0, "x0T")
            pe.wait_ge(*wide.empty("ctxT"))
            pe.wait_ge(ctxd_ready, 1)

            def keys0(b):
                ps, filled = take_wide(("k0", b), 2)
                for c in range(NC):
                    for off, n, src in ((0, S, actT[:, :, b * S:(b + 1) * S]), (S, T, ctxT[:, :, b * T:(b + 1) * T])):
                        for kc in range(NC):
                            m = mm(ps[:, c * 512 + off:c * 512 + off + n], kv_w0[:, kc, 0, c * P:(c + 1) * P],
                                   src[:, kc, :], start=kc == 0, stop=kc == NC - 1)
                m.then_inc(filled, 1)
                ps, filled = take_wide(("v0", b), 4)
                for j in range(3):
                    for kc in range(NC):
                        src = (actT[:, kc, b * S + j * P:b * S + (j + 1) * P] if j < 2 else
                               ctxD[:, kc, b, :, :].rearrange("p a k -> p (a k)"))
                        m = mm(ps[:, j * 256:(j + 1) * 256], src, kv_w0[:, kc, 1, :], start=kc == 0, stop=kc == NC - 1)
                m.then_inc(filled, 1)

            def scores0(u):
                b, q, r = units0[u]
                ps, filled = take_wide(("S", u), 2, SCORES)
                if q == 0 and r == 0:
                    pe.wait_ge(kbd_ready, 2 * (b + 1))
                if u == 0:
                    pe.wait_ge(*wide.empty(("q", 0, 0)))
                    pe.wait_ge(*wide.empty(("q", 0, 1)))
                c = r // 4
                for i in range(2):
                    m = mm(ps[:, i * 512:i * 512 + KEYS0], qT[:, c, qoff(2 * b + q)],
                           kbd0[b % 2][:, c, 2 * (r % 4) + i, :], start=True, stop=True)
                m.then_inc(filled, 1)

            def values0(u):
                b, q, r = units0[u]
                c = r // 4
                if r % 4 == 0:
                    ps, filled = take_narrow(("ao", 0, 2 * b + q, c))
                    ao[0] = (ps, filled)
                ps, filled = ao[0]
                pe.wait_ge(*wide.empty(("T", u)))
                if q == 0 and r == 0:
                    pe.wait_ge(*wide.empty(("v0", b)))
                vp = vpad0[b % 2]
                for j in range(5):
                    i, kb = j // 2, j % 2
                    lhs = (vp[:, (kb * 16 + 2 * r + i) * 64:(kb * 16 + 2 * r + i + 1) * 64] if j < 4 else
                           vp[:, 2048 + r * 64:2048 + (r + 1) * 64])
                    po = 64 * (r % 4 // 2)
                    m = mm(ps[po:po + 64, 0:P], lhs, probsT[:, u % 2, j * P:(j + 1) * P],
                           start=r % 2 == 0 and j == 0, stop=r % 2 == 1 and j == 4)
                if r % 4 == 3:
                    m.then_inc(filled, 1)

            ao = [None]
            keys0(0)
            n0 = len(units0)
            for step in range(-3, n0 + 2):
                if 0 <= step < n0:
                    turn_probs(step)
                if step + 3 < n0:
                    scores0(step + 3)
                if 0 <= step < n0 and step % 16 == 4 and step // 16 + 1 < B:
                    keys0(step // 16 + 1)
                if 0 <= step - 1 < n0:
                    values0(step - 1)
                if step - 2 >= 0 and units0[step - 2][2] == 7:
                    q = (step - 2) // 8
                    project(0, q, out_w0, [("ao", 0, q, 0), ("ao", 0, q, 1)])
            norm_turn(0)
            pe.wait_ge(load["mlp0"], 32)
            mlp(0, 0, mlp_w1_0, mlp_w2_0)

            turn("x1T", xA, lambda q: pe.wait_ge(*narrow.empty(("down", 0, q))))
            pe.wait_ge(load["w1"], 16 * 4)
            queries(1, q_w1, "x1T")

            def keys_small(layer, wk, wv, nv):
                ps, filled = take_wide(("k", layer), 2)
                for c in range(NC):
                    for kc in range(NC):
                        m = mm(ps[:, c * 256:(c + 1) * 256], wk(kc, c), ctxT[:, kc, :], start=kc == 0, stop=kc == NC - 1)
                m.then_inc(filled, 1)
                ps, filled = take_wide(("v", layer), 16 if layer == 1 else 8)
                for b in range(B):
                    for kc in range(NC):
                        m = mm(ps[:, b * nv:(b + 1) * nv], ctxD[:, kc, b, :, :].rearrange("p a k -> p (a k)"),
                               wv[:, kc, :], start=kc == 0, stop=kc == NC - 1)
                m.then_inc(filled, 1)

            pe.wait_ge(wk_ready, 2)
            keys_small(1, lambda kc, c: wkrep[:, kc, c, :], v_w1, 64)

            def scores1(i):
                q, c = units1[i]
                ps, filled = take_wide(("S", base["1"] + i), among=SCORES)
                if i == 0:
                    pe.wait_ge(*wide.empty(("q", 1, 0)))
                    pe.wait_ge(*wide.empty(("q", 1, 1)))
                    pe.wait_ge(kbd_ready, 2 * B + 2)
                for g in range(2):
                    m = mm(ps[:, g * 512:(g + 1) * 512], qT[:, c, qoff(q)], kbd1[:, c, q // 2, 8 * g:8 * g + 8, :],
                           start=True, stop=True)
                m.then_inc(filled, 1)

            def values1(i):
                q, c = units1[i]
                u = base["1"] + i
                ps, filled = take_narrow(("ao", 1, q, c))
                pe.wait_ge(*wide.empty(("T", u)))
                if i == 0:
                    pe.wait_ge(*wide.empty(("v", 1)))
                for j in range(8):
                    m = mm(ps[:, 0:P], vpad1[:, q // 2, 8 * c + j, :], probsT[:, u % 2, j * P:(j + 1) * P],
                           start=j == 0, stop=j == 7)
                m.then_inc(filled, 1)

            n1 = len(units1)
            for step in range(-3, n1 + 2):
                if 0 <= step < n1:
                    turn_probs(base["1"] + step)
                if step + 3 < n1:
                    scores1(step + 3)
                if 0 <= step - 1 < n1:
                    values1(step - 1)
                if step - 2 >= 0 and units1[step - 2][1] == 1:
                    q = units1[step - 2][0]
                    project(1, q, out_w1, [("ao", 1, q, 0), ("ao", 1, q, 1)])

            def weights2(a, h):
                g = 4 * a + h // GROUP
                wbuf = wring[g % 2]
                return [wbuf[:, m, :].rearrange("p (c n) -> p c n", c=NC) for m in range(3)] + [
                    wbuf[:, 3, :].rearrange("p (h n) -> p h n", h=GROUP)]

            def head_products2(a, h):
                g = 4 * a + h // GROUP
                wq, wk, wv, wo = weights2(a, h)
                o = (h % GROUP) * P
                if h % GROUP == 0:
                    pe.wait_ge(ring_loaded[g % 2], 64 * (g // 2 + 1))
                if h == 0:
                    pe.wait_ge(hot_ready, a + 1)
                ps, filled = take_wide(("kvq", a, h), 4)
                for kc in range(NC):
                    mm(ps[:, 0:256], wk[:, kc, o:o + P], ctxT[:, kc, :], start=kc == 0, stop=kc == NC - 1)
                for kc in range(NC):
                    mm(ps[:, 256:512], wv[:, kc, o:o + P], ctxT[:, kc, :], start=kc == 0, stop=kc == NC - 1)
                mm(ps[0:16, 768:1024], bvhot[:, h, :], wo[:, h % GROUP, :], start=True, stop=True)
                for kc in range(NC):
                    m = nc.tensor.transpose(ps[:, 512 + kc * P:512 + (kc + 1) * P], wq[:, kc, o:o + P], ident[:])
                m.then_inc(filled, 1)

            def precompute2(a):
                head_products2(a, 0)
                for h in range(H2):
                    if h + 1 < H2:
                        head_products2(a, h + 1)
                    wo = weights2(a, h)[3]
                    hb = heads[:, h % 2, :]
                    ps, filled = take_wide(("G", a, h))
                    pe.wait_ge(*wide.empty(("kvq", a, h)))
                    pe.wait_ge(bias_key, a * H2 + h + 1)
                    for c in range(NC):
                        m = mm(ps[:, c * 512:c * 512 + NK2], hb[:, 513 + c * P:513 + (c + 1) * P], hb[:, 0:NK2],
                               start=True, stop=True)
                    m.then_inc(filled, 1)
                    bq = column(f"L2_bq{a + 1}", h)
                    ps, filled = take_narrow(("cB", a, h))
                    mm(ps[:, 0:NK2], bq.broadcast_to([P, P]), hb[:, 0:NK2], start=True, stop=True).then_inc(filled, 1)
                    if h % 2 == 0:
                        vw = take_wide(("VW", a, h // 2))
                    ps, filled = vw
                    po = T * (h % 2)
                    for b in range(B):
                        m = mm(ps[po:po + T, b * D:(b + 1) * D], hb[:, 257 + b * T:257 + (b + 1) * T],
                               wo[:, h % GROUP, :], start=True, stop=True)
                    if h % 2 == 1:
                        m.then_inc(filled, 1)

            def scores2(a, q):
                u = base["2a" if a == 0 else "2b"] + q
                b = q // 2
                ps, filled = take_wide(("S", u), among=SCORES)
                if q == 0:
                    for half in range(2):
                        pe.wait_ge(*wide.empty((("ln", 2 + a), half)))
                for g in range(2):
                    for c in range(NC):
                        m = mm(ps[:, g * 512:(g + 1) * 512], actT[:, c, qoff(q)],
                               G[:, c, 8 * g:8 * g + 8, b * T:(b + 1) * T], start=c == 0, stop=c == NC - 1)
                m.then_inc(filled, 1)

            def scores2_bias(ps, q):
                for c in range(NC):
                    m = mm(ps[:, 0:H2], actT[:, c, qoff(q)], G[:, c, :, NK2 - 1], start=c == 0, stop=c == NC - 1)
                return m

            def attend2(a):
                u0 = base["2a" if a == 0 else "2b"]
                for h in range(H2):
                    pe.wait_ge(*wide.empty(("G", a, h)))
                for step in range(-3, NQ + 1):
                    if 0 <= step < NQ:
                        turn_probs(u0 + step)
                    if step + 3 < NQ:
                        scores2(a, step + 3)
                    if step < NQ:
                        both = step >= 0 and step + 3 < NQ
                        ps, filled = take_narrow(("X", a, step), 2 if both else 1)
                        if step + 3 < NQ:
                            m = scores2_bias(ps, step + 3)
                        if step >= 0:
                            m = nc.tensor.transpose(ps[0:16, P:2 * P], probsb[:, (u0 + step) % 2, :], ident[:])
                        m.then_inc(filled, 1)
                    if step >= 1:
                        q = step - 1
                        u = u0 + q
                        ps, filled = take_narrow(("proj", 2 + a, q))
                        pe.wait_ge(*wide.empty(("T", u)))
                        pe.wait_ge(*narrow.empty(("X", a, q)))
                        if q == 0:
                            for r in range(8):
                                pe.wait_ge(*wide.empty(("VW", a, r)))
                        for r in range(8):
                            mm(ps[:, 0:D], probsT[:, u % 2, r * P:(r + 1) * P], VW[:, q // 2, r, :],
                               start=r == 0, stop=False)
                        mm(ps[:, 0:D], probsbT[:, u % 2, :], vwb[:, :], start=False, stop=True).then_inc(filled, 1)

            precompute2(0)
            norm_turn(2)
            attend2(0)
            precompute2(1)
            norm_turn(3)
            attend2(1)
            norm_turn(4)
            pe.wait_ge(load["mlp2"], 32)
            mlp(1, 4, fc1_w2, fc2_w2)

            pe.wait_ge(load["w3"], 64)
            keys_small(3, lambda kc, c: w3[1][:, kc, c * P:(c + 1) * P], w3[2], 256)
            norm_turn(5)
            queries(3, w3[0], ("ln", 5))

            def scores3(q):
                ps, filled = take_wide(("S", base["3"] + q), among=SCORES)
                if q == 0:
                    pe.wait_ge(*wide.empty(("q", 3, 0)))
                    pe.wait_ge(*wide.empty(("q", 3, 1)))
                    pe.wait_ge(kbd_ready, 2 * B + 4)
                for c in range(NC):
                    m = mm(ps[:, c * 512:(c + 1) * 512], qT[:, c, qoff(q)], kbd3[:, c, q // 2, :, :],
                           start=True, stop=True)
                m.then_inc(filled, 1)

            def values3(q):
                u = base["3"] + q
                ps, filled = take_narrow(("ao", 3, q), 2)
                pe.wait_ge(*wide.empty(("T", u)))
                if q == 0:
                    pe.wait_ge(*wide.empty(("v", 3)))
                for c in range(NC):
                    for j in range(4):
                        m = mm(ps[:, c * P:(c + 1) * P], vpad3[:, q // 2, 4 * c + j, :],
                               probsT[:, u % 2, (4 * c + j) * P:(4 * c + j + 1) * P], start=j == 0, stop=j == 3)
                m.then_inc(filled, 1)

            for step in range(-3, NQ + 2):
                if 0 <= step < NQ:
                    turn_probs(base["3"] + step)
                if step + 3 < NQ:
                    scores3(step + 3)
                if 0 <= step - 1 < NQ:
                    values3(step - 1)
                if step >= 2:
                    project(4, step - 2, w3[3], [("ao", 3, step - 2)])
            norm_turn(6)
            pe.wait_ge(load["mlp3"], 32)
            mlp(2, 6, fc_w3, proj_w3)

        @block.sync
        def _(sp):
            def halves(dst, src):
                return dst, src.rearrange("(c p) n -> p c n", p=P)

            sp.dma_start(xA, t["x"].rearrange("b (h p) d -> p (b h) d", p=P)).then_inc(load["x"], 16)
            sp.dma_start(xn[:, 0:2, :], t["ctx_2048"].rearrange("(g b) k d -> (b k) g d", g=2)).then_inc(load["ctx"], 16)
            sp.dma_start(*halves(q_w0, t["L0_xattn_q_w"])).then_inc(load["w0"], 16)
            sp.dma_start(w0[:, 512:1536].rearrange("p (c n) -> p c n", c=NC),
                         t["L0_xattn_kv_w"].rearrange("(c p) n -> p c n", p=P)).then_inc(load["w0"], 16)
            sp.dma_start(*halves(out_w0, t["L0_xattn_out_w"])).then_inc(load["w0"], 16)
            sp.dma_start(mask0i, t["mask_BxS2_ik0"].rearrange("(a b) k -> a (b k)", a=1).broadcast_to([P, B * T])).then_inc(load["masks"], 16)
            sp.dma_start(mask3i, t["mask_BxS2_bf1"].rearrange("(a b) k -> a (b k)", a=1).broadcast_to([P, B * T])).then_inc(load["masks"], 16)
            sp.dma_start(mask1[:], t["mask_Bx1xSxS2_ff0"].rearrange("b o (h p) k -> p (b o h) k", p=P)).then_inc(load["masks"], 16)
            for i, name in enumerate(ROWS):
                key = name[:3] + "xattn_" + name[3:]
                sp.dma_start(rows[:, i, :], t[key].rearrange("(a d) -> a d", a=1).broadcast_to([P, D])).then_inc(load["rows"], 16)
            sp.dma_start(*halves(mlp_w1_0, t["L0_xattn_mlp_w1"])).then_inc(load["mlp0"], 16)
            sp.dma_start(*halves(mlp_w2_0, t["L0_xattn_mlp_w2"])).then_inc(load["mlp0"], 16)
            sp.dma_start(*halves(q_w1, t["L1_xattn_Wq"])).then_inc(load["w1"], 16)
            sp.dma_start(*halves(k_w1, t["L1_xattn_Wk"])).then_inc(load["w1"], 16)
            sp.dma_start(*halves(v_w1, t["L1_xattn_Wv"])).then_inc(load["w1"], 16)
            sp.dma_start(*halves(out_w1, t["L1_xattn_Wo"])).then_inc(load["w1"], 16)

            for g in range(8):
                a, h0 = g // 4, (g % 4) * GROUP
                if g < 2:
                    sp.wait_ge(*narrow.full(("down", 0, NQ - 1)))
                else:
                    sp.wait_ge(*wide.full(("VW", (g - 2) // 4, 2 * ((g - 2) % 4) + 1)))
                wbuf = wring[g % 2]
                for m, w in enumerate(("wq", "wk", "wv")):
                    sp.dma_start(wbuf[:, m, :].rearrange("p (c n) -> p c n", c=NC),
                                 t[f"L2_xattn_{w}{a + 1}"].rearrange("(c p) n -> p c n", p=P)[:, :, h0 * P:(h0 + GROUP) * P]
                                 ).then_inc(ring_loaded[g % 2], 16)
                sp.dma_start(wbuf[:, 3, :].rearrange("p (h n) -> p h n", h=GROUP),
                             t[f"L2_xattn_wo{a + 1}"].rearrange("(h p) n -> p h n", p=P)[:, h0:h0 + GROUP, :]
                             ).then_inc(ring_loaded[g % 2], 16)
                if g == 3:
                    sp.wait_ge(*narrow.full(("proj", 1, NQ - 1)))
                    for w, key in zip(w3, ("q_w", "k_w", "v_w", "cproj_w")):
                        sp.dma_start(*halves(w, t["L3_xattn_" + key])).then_inc(load["w3"], 16)
            sp.wait_ge(*wide.full(("VW", 1, 5)))
            sp.dma_start(*halves(fc1_w2, t["L2_xattn_w_fc1"])).then_inc(load["mlp2"], 16)
            sp.dma_start(*halves(fc2_w2, t["L2_xattn_w_fc2"])).then_inc(load["mlp2"], 16)
            sp.wait_ge(*wide.full(("VW", 1, 7)))
            sp.dma_start(*halves(fc_w3, t["L3_xattn_fc_w"])).then_inc(load["mlp3"], 16)
            sp.dma_start(*halves(proj_w3, t["L3_xattn_proj_w"])).then_inc(load["mlp3"], 16)
            for q in range(NQ):
                sp.wait_ge(*narrow.empty(("down", 2, q)))
                sp.dma_start(out.rearrange("b (h p) d -> p (b h) d", p=P)[:, q, :], xB[:, q, :]).then_inc(stored, 16)
            sp.wait_ge(stored, 16 * NQ)

        @block.scalar
        def _(act):
            def load_rows(name, src, apart=False):
                r, k = colrow[name]
                act.dma_start(colraw[r % P:r % P + k, r // P, :], src, allow_slow_non_contiguous=apart).then_inc(load["cols"], 16)

            act.wait_ge(cols_zeroed, 1)
            for name, k in COLUMNS:
                key = name[:3] + "xattn_" + name[3:]
                if name in ("L0_k_b", "L0_v_b"):
                    src = t["L0_xattn_kv_b"].rearrange("(r p two) -> two r p", r=2, two=2)[int(name == "L0_v_b")]
                    load_rows(name, src, apart=True)
                elif name in ("L1_bk", "L1_bv"):
                    r, _ = colrow[name]
                    for c in range(NC):
                        src = t[key].rearrange("(k d) -> k d", d=8)[4 * c:4 * c + 4].unsqueeze(1).broadcast_to([4, 4, 8]).unsqueeze(0)
                        act.dma_start(colraw[r % P + c:r % P + c + 1, r // P, :].rearrange("p (a b c) -> p a b c", a=4, b=4),
                                      src).then_inc(load["cols"], 16)
                elif "bias_" in name:
                    load_rows(name, t[key].rearrange("a b h d -> (a b h) d"))
                else:
                    load_rows(name, t[key].rearrange("(r p) -> r p", p=P))

            def evac(dst, src, ring, key, **kw):
                nc.scalar.activation(dst, src, ACT.Identity, **kw).then_inc(ring.drained[ring.slot(key)], 1)

            def turned(key, dst):
                for half in range(2):
                    act.wait_ge(*wide.full((key, half)))
                    evac(dst[:, :, half * 512:(half + 1) * 512],
                         wide_ps[:, wide.slot((key, half)), :].rearrange("p (c n) -> p c n", c=NC), wide, (key, half))

            def norm_turned(k, w, b):
                for half in range(2):
                    key = (("ln", k), half)
                    act.wait_ge(*wide.full(key))
                    for c in range(NC):
                        kw = {"scale": column(w, c)}
                        if b:
                            kw["bias"] = column(b, c)
                        evac(actT[:, c, half * 512:(half + 1) * 512],
                             wide_ps[:, wide.slot(key), c * 512:(c + 1) * 512], wide, key, **kw)

            def queries(layer, b):
                for c in range(NC):
                    key = ("q", layer, c)
                    act.wait_ge(*wide.full(key))
                    evac(qT[:, c, :], wide_ps[:, wide.slot(key), :], wide, key, bias=column(b, c))

            def mlp(n, func, b1):
                for half in range(2):
                    for fp in range(NF // 2):
                        key = ("up", n, half, fp)
                        act.wait_ge(*wide.full(key))
                        for j in range(2):
                            f = 2 * fp + j
                            nc.scalar.activation(hid[:, f, half * 512:(half + 1) * 512],
                                                 wide_ps[:, wide.slot(key), j * 512:(j + 1) * 512], func,
                                                 bias=column(b1, f)).then_inc(wide.drained[wide.slot(key)], 1)

            def probs_turned(u):
                key = ("T", u)
                act.wait_ge(*wide.full(key))
                n = 5 if u < len(units0) else 8
                evac(probsT[:, u % 2, 0:n * P], wide_ps[:, wide.slot(key), 0:n * P], wide, key)

            def keys0(b):
                key = ("k0", b)
                act.wait_ge(*wide.full(key))
                if b >= 1:
                    act.wait_ge(kbd_ready, 2 * b)
                for c in range(NC):
                    evac(kT2[:, c, :], wide_ps[:, wide.slot(key), c * 512:c * 512 + KEYS0], wide, key,
                         bias=column("L0_k_b", c))

            def exp0(u):
                key = ("S", u)
                act.wait_ge(max_ready, u + 1)
                if u >= 3:
                    act.wait_ge(prob_ready, probcount[u - 2])
                for i in range(2):
                    nc.scalar.activation(scoresb[:, u % 3, i * KEYS0:(i + 1) * KEYS0],
                                         wide_ps[:, wide.slot(key), i * 512:i * 512 + KEYS0], ACT.Exp,
                                         scale=1.0 / 16, bias=mx[:, u % 3, i:i + 1],
                                         accum_out=sums[:, u % 3, i:i + 1]).then_inc(wide.drained[wide.slot(key)], 1)

            def exp(u, n):
                act.wait_ge(shifted, shiftcount[u + 1])
                nc.scalar.activation(scoresb[:, u % 3, 0:n], scoresb[:, u % 3, 0:n], ACT.Exp).then_inc(exp_done, 1)

            def attended(layer, q, c, vb):
                key = ("ao", layer, q, c)
                act.wait_ge(*narrow.full(key))
                evac(qT[:, c, qoff(q)], narrow_ps[:, narrow.slot(key), 0:P], narrow, key, bias=column(vb, c))

            act.wait_ge(*wide.full("cols"))
            evac(col[:], wide_ps[:, wide.slot("cols"), 0:256].rearrange("p (a b) -> p a b", a=2), wide, "cols")
            turned("x0T", actT)
            act.wait_ge(*wide.full("ctxT"))
            evac(ctxT[:], wide_ps[:, wide.slot("ctxT"), 0:512].rearrange("p (c n) -> p c n", c=NC), wide, "ctxT")
            act.wait_ge(*wide.empty("cols"))
            queries(0, "L0_q_b")
            keys0(0)
            n0 = len(units0)
            for step in range(-2, n0 + 2):
                if step - 2 >= 0 and units0[step - 2][2] % 4 == 3:
                    b, q, r = units0[step - 2]
                    attended(0, 2 * b + q, r // 4, "L0_v_b")
                if 0 <= step < n0:
                    probs_turned(step)
                if step + 2 < n0:
                    exp0(step + 2)
                if 0 <= step < n0 and step % 16 == 4 and step // 16 + 1 < B:
                    keys0(step // 16 + 1)
            norm_turned(0, "L0_postnorm_w", None)
            mlp(0, ACT.Gelu_apprx_tanh, "L0_mlp_b1")

            turned("x1T", actT)
            queries(1, "L1_bq")

            def keys_small(layer, kb):
                key = ("k", layer)
                act.wait_ge(*wide.full(key))
                for c in range(NC):
                    evac(kT2[:, c, 0:256], wide_ps[:, wide.slot(key), c * 256:(c + 1) * 256], wide, key, bias=column(kb, c))

            keys_small(1, "L1_bk")
            n1 = len(units1)
            for step in range(-2, n1 + 2):
                if step - 2 >= 0:
                    attended(1, *units1[step - 2], "L1_bv")
                if 0 <= step < n1:
                    probs_turned(base["1"] + step)
                if step + 2 < n1:
                    exp(base["1"] + step + 2, 1024)

            def head2(a, h):
                key = ("kvq", a, h)
                act.wait_ge(*wide.full(key))
                ps = wide_ps[:, wide.slot(key), :]
                hb = heads[:, h % 2, :]
                evac(hb[:, 0:256], ps[:, 0:256], wide, key, bias=column(f"L2_bk{a + 1}", h))
                evac(hb[:, 257:513], ps[:, 256:512], wide, key, bias=column(f"L2_bv{a + 1}", h))
                nc.scalar.copy(hb[:, 256:257], column(f"L2_bias_k{a + 1}", h)).then_inc(bias_key, 1)

            def precompute2(a):
                head2(a, 0)
                for h in range(H2):
                    if h + 1 < H2:
                        head2(a, h + 1)
                    key = ("cB", a, h)
                    act.wait_ge(*narrow.full(key))
                    if a == 0 and h == 0:
                        act.wait_ge(xn_ready, 2 * NQ)
                    nc.scalar.mul(cB[:, h, :], narrow_ps[:, narrow.slot(key), 0:NK2], DH2 ** -0.5
                                  ).then_inc(narrow.drained[narrow.slot(key)], 1)
                    if h % 2 == 1:
                        key = ("VW", a, h // 2)
                        act.wait_ge(*wide.full(key))
                        evac(VW[:, :, h // 2, :], wide_ps[:, wide.slot(key), :].rearrange("p (b n) -> p b n", b=B), wide, key)

            def attend2(a):
                u0 = base["2a" if a == 0 else "2b"]
                for step in range(-2, NQ):
                    if step >= 0:
                        probs_turned(u0 + step)
                    if step + 2 < NQ:
                        exp(u0 + step + 2, 16 * 65)

            precompute2(0)
            norm_turned(2, "L2_ln1_scale", "L2_ln1_offset")
            attend2(0)
            precompute2(1)
            norm_turned(3, "L2_ln2_scale", "L2_ln2_offset")
            attend2(1)
            norm_turned(4, "L2_ln_mlp_scale", "L2_ln_mlp_offset")
            mlp(1, ACT.Gelu, "L2_b_fc1")
            keys_small(3, "L3_k_b")
            norm_turned(5, "L3_ln1_w", "L3_ln1_b")
            queries(3, "L3_q_b")
            for step in range(-2, NQ + 2):
                if step >= 2:
                    key = ("ao", 3, step - 2)
                    act.wait_ge(*narrow.full(key))
                    for c in range(NC):
                        evac(qT[:, c, qoff(step - 2)], narrow_ps[:, narrow.slot(key), c * P:(c + 1) * P], narrow, key,
                             bias=column("L3_v_b", c))
                if 0 <= step < NQ:
                    probs_turned(base["3"] + step)
                if step + 2 < NQ:
                    exp(base["3"] + step + 2, 1024)
            norm_turned(6, "L3_ln2_w", "L3_ln2_b")
            mlp(2, ACT.Gelu_apprx_tanh, "L3_fc_b")

        @block.vector
        def _(dve):
            v = nc.vector
            chain = [0]

            def link(ins):
                chain[0] += 1
                ins.then_inc(link_dve, 1)
                dve.wait_ge(link_dve, chain[0])

            def stat(k, q, src, ready, eps, rms):
                ready(q)
                link(v.bn_stats(stats[:, q, :], src[:, q, :]))
                link(v.bn_aggr(mv[:, q, :], stats[:, q, :]))
                if rms:
                    link(v.scalar_tensor_tensor(out=mv[:, q, 1:2], in0=mv[:, q, 0:1], scalar=mv[:, q, 0:1],
                                                in1=mv[:, q, 1:2], op0=ALU.mult, op1=ALU.add))
                v.tensor_scalar_add(veps[:, q:q + 1], mv[:, q, 1:2], eps).then_inc(stat_ready, 1)

            def norm(k, src, ready, eps, rms=False):
                stat(k, 0, src, ready, eps, rms)
                for q in range(NQ):
                    if q + 1 < NQ:
                        stat(k, q + 1, src, ready, eps, rms)
                    dve.wait_ge(rstd_ready, k * NQ + q + 1)
                    if rms:
                        ins = v.tensor_scalar(xn[:, q, :], src[:, q, :], rstd[:, q:q + 1], None, ALU.mult)
                    else:
                        ins = v.tensor_scalar(xn[:, q, :], src[:, q, :], mv[:, q, 0:1], rstd[:, q:q + 1],
                                              ALU.subtract, ALU.mult)
                    ins.then_inc(xn_ready, 1)

            def add_residual(key, dst, q, n):
                dve.wait_ge(*narrow.full(key))
                dve.wait_ge(row_added, n)
                v.tensor_tensor(dst[:, q, :], narrow_ps[:, narrow.slot(key), 0:D], dst[:, q, :], ALU.add
                                ).then_inc(narrow.drained[narrow.slot(key)], 1)

            def front(u, n, scale, addend, n_scores, bias=None):
                key = ("S", u)
                dve.wait_ge(*wide.full(key))
                dve.wait_ge(prob_ready, probcount[u - 2])
                s3 = scoresb[:, u % 3, 0:16 * n_scores].rearrange("p (h k) -> p h k", h=16)
                v.scalar_tensor_tensor(out=s3[:, :, 0:T], in0=wide_ps[:, wide.slot(key), :].rearrange("p (h k) -> p h k", h=16),
                                       scalar=scale, in1=addend, op0=ALU.mult, op1=ALU.add
                                       ).then_inc(wide.drained[wide.slot(key)], 1)
                dve.wait_ge(*wide.empty(key))
                if bias:
                    bias(s3[:, :, T])
                v.tensor_reduce(mx[:, u % 3, :], s3, AX, ALU.max).then_inc(max_ready, 1)

            def middle(u, n_scores):
                dve.wait_ge(exp_done, shiftcount[u + 1])
                s3 = scoresb[:, u % 3, 0:16 * n_scores].rearrange("p (h k) -> p h k", h=16)
                link(v.tensor_reduce(sums[:, u % 3, :], s3, AX, ALU.add))
                v.reciprocal(rcp[:, u % 3, :], sums[:, u % 3, :]).then_inc(rcp_ready, 1)

            v.memset(colraw[:].rearrange("p a b -> p (a b)"), 0.0).then_inc(cols_zeroed, 1)
            link(v.memset(bvhot[:].rearrange("p a b -> p (a b)"), 0.0))
            dve.wait_ge(load["masks"], 48)
            link(v.tensor_scalar(mask0[:].rearrange("p b k -> p (b k)"), mask0i, 0, NEG0, ALU.is_equal, ALU.mult))
            link(v.tensor_scalar(mask3[:].rearrange("p b k -> p (b k)"), mask3i, 0, NEG3, ALU.is_equal, ALU.mult))

            def values0(b):
                key = ("v0", b)
                dve.wait_ge(*wide.full(key))
                if b < 2:
                    dve.wait_ge(vzero, b + 1)
                vp = vpad0[b % 2]
                ps = wide_ps[:, wide.slot(key), :]
                done = wide.drained[wide.slot(key)]
                for kb in range(2):
                    v.tensor_copy(diagonal(vp, kb * 1024, [(256, 4), (64 + 16, 4), (1, 16)]), ps[:, kb * 256:(kb + 1) * 256].rearrange("p (a h d) -> p a h d", a=4, h=4)
                                  ).then_inc(done, 1)
                for i in range(2):
                    dst = diagonal(vp, 2048 + 16 * i, [(128, 4), (64 + 32, 2), (1, 16)])
                    src = ps[:, 512:768].rearrange("p (a j two d) -> p a j two d", a=4, two=2, d=16)[:, :, :, i, :]
                    v.tensor_copy(dst[64 * i:64 * i + 64], src[64 * i:64 * i + 64]).then_inc(done, 1)

            def front0(u):
                b, q, r = units0[u]
                key = ("S", u)
                dve.wait_ge(*wide.full(key))
                ps = wide_ps[:, wide.slot(key), :].rearrange("p (i n) -> p i n", i=2)
                link(v.tensor_tensor(ps[:, :, S:KEYS0], ps[:, :, S:KEYS0],
                                     mask0[:, b, :].unsqueeze(1).broadcast_to([P, 2, T]), ALU.add))
                if u >= 3:
                    dve.wait_ge(*wide.empty(("S", u - 3)))
                link(v.tensor_reduce(mx[:, u % 3, 4:6], ps[:, :, 0:KEYS0], AX, ALU.max))
                v.tensor_scalar(mx[:, u % 3, 0:2], mx[:, u % 3, 4:6], -1.0 / 16, None, ALU.mult).then_inc(max_ready, 1)

            def middle0(u):
                dve.wait_ge(*wide.empty(("S", u)))
                v.reciprocal(rcp[:, u % 3, 0:2], sums[:, u % 3, 0:2]).then_inc(rcp_ready, 1)

            dve.wait_ge(*wide.empty("cols"))
            values0(0)
            n0 = len(units0)
            for step in range(-2, n0 + 3):
                if step - 3 >= 0 and units0[step - 3][2] == 7:
                    add_residual(("proj", 0, (step - 3) // 8), xB, (step - 3) // 8, 1)
                if 0 <= step < n0:
                    middle0(step)
                if step + 2 < n0:
                    front0(step + 2)
                if 0 <= step < n0 and step % 16 == 4 and step // 16 + 1 < B:
                    values0(step // 16 + 1)
            norm(0, xB, lambda q: dve.wait_ge(*narrow.empty(("proj", 0, q))), 1e-6, rms=True)
            for q in range(NQ):
                add_residual(("down", 0, q), xA, q, 2)

            dve.wait_ge(*wide.full(("v", 1)))
            dve.wait_ge(vzero, 3)
            ps = wide_ps[:, wide.slot(("v", 1)), :]
            for b in range(B):
                for c in range(NC):
                    for i in range(2):
                        dst = diagonal(region, b * 2048 + c * 1024 + 8 * i, [(288, 4), (144, 2), (1, 8)])
                        src = ps[:, b * 64 + c * 32:b * 64 + (c + 1) * 32].rearrange("p (k d) -> p k d", d=8).unsqueeze(2).broadcast_to([P, 4, 2, 8])
                        v.tensor_copy(dst[64 * i:64 * i + 64], src[64 * i:64 * i + 64]
                                      ).then_inc(wide.drained[wide.slot(("v", 1))], 1)
            n1 = len(units1)
            for step in range(-2, n1 + 3):
                if step - 3 >= 0 and units1[step - 3][1] == 1:
                    q = units1[step - 3][0]
                    add_residual(("proj", 1, q), xA, q, 3)
                if 0 <= step < n1:
                    middle(base["1"] + step, T)
                if step + 2 < n1:
                    q, c = units1[step + 2]
                    front(base["1"] + step + 2, 1024, 8 ** -0.5,
                          mask1[:, q, :].unsqueeze(1).broadcast_to([P, 16, T]), T)
            norm(1, xA, lambda q: dve.wait_ge(*narrow.empty(("proj", 1, q))), 1e-6)

            def head2(a, h):
                key = ("kvq", a, h)
                dve.wait_ge(*wide.full(key))
                ps = wide_ps[:, wide.slot(key), :]
                v.tensor_copy(heads[:, h % 2, 513:769], ps[:, 512:768]).then_inc(wide.drained[wide.slot(key)], 1)
                v.tensor_tensor(vwb[:, :], ps[0:16, 768:1024], vwb[:, :], ALU.add
                                ).then_inc(wide.drained[wide.slot(key)], 1)

            def precompute2(a):
                v.tensor_copy(diagonal(bvhot, 0, [(17, 16)], 256),
                              colrange(f"L2_bias_v{a + 1}")).then_inc(hot_ready, 1)
                link(v.memset(vwb[:], 0.0))
                head2(a, 0)
                for h in range(H2):
                    if h + 1 < H2:
                        dve.wait_ge(*wide.empty(("kvq", a, h)))
                        head2(a, h + 1)
                    key = ("G", a, h)
                    dve.wait_ge(*wide.full(key))
                    v.tensor_copy(G[:, :, h, :], wide_ps[:, wide.slot(key), :].rearrange("p (c n) -> p c n", c=NC)[:, :, 0:NK2]
                                  ).then_inc(wide.drained[wide.slot(key)], 1)

            def attend2(a, rows_before):
                u0 = base["2a" if a == 0 else "2b"]
                for step in range(-2, NQ + 2):
                    if 0 <= step - 1 < NQ:
                        key = ("X", a, step - 1)
                        dve.wait_ge(*narrow.full(key))
                        v.tensor_copy(probsbT[:, (u0 + step - 1) % 2, :], narrow_ps[0:16, narrow.slot(key), P:2 * P]
                                      ).then_inc(narrow.drained[narrow.slot(key)], 1)
                    if step >= 2:
                        add_residual(("proj", 2 + a, step - 2), xB, step - 2, rows_before)
                    if 0 <= step < NQ:
                        middle(u0 + step, 65)
                    if step + 2 < NQ:
                        q = step + 2
                        b = q // 2
                        if q == 0:
                            for h in range(H2 - 2, H2):
                                dve.wait_ge(*narrow.empty(("cB", a, h)))

                        def bias(dst):
                            key = ("X", a, step - 1)
                            dve.wait_ge(*narrow.full(key))
                            v.scalar_tensor_tensor(out=dst, in0=narrow_ps[:, narrow.slot(key), 0:16], scalar=DH2 ** -0.5,
                                                   in1=cB[:, :, NK2 - 1], op0=ALU.mult, op1=ALU.add
                                                   ).then_inc(narrow.drained[narrow.slot(key)], 1)
                            dve.wait_ge(*narrow.empty(key))
                        front(u0 + q, 1024, DH2 ** -0.5, cB[:, :, b * T:(b + 1) * T], 65, bias)

            precompute2(0)
            norm(2, xB, lambda q: dve.wait_ge(x2_ready, q + 1), 1e-5)
            attend2(0, 4)
            precompute2(1)
            norm(3, xB, lambda q: dve.wait_ge(*narrow.empty(("proj", 2, q))), 1e-5)
            attend2(1, 5)
            norm(4, xB, lambda q: dve.wait_ge(*narrow.empty(("proj", 3, q))), 1e-5)
            for q in range(NQ):
                add_residual(("down", 1, q), xB, q, 6)

            dve.wait_ge(*wide.full(("v", 3)))
            dve.wait_ge(vzero, 4)
            ps = wide_ps[:, wide.slot(("v", 3)), :]
            for b in range(B):
                for i in range(2):
                    dst = diagonal(region, 12288 + b * 1024 + 16 * i, [(512, NC), (P + 32, 4), (1, 16)])
                    src = ps[:, b * 256:(b + 1) * 256].rearrange("p (c j two d) -> p c j two d", c=NC, two=2, d=16)[:, :, :, i, :]
                    v.tensor_copy(dst[64 * i:64 * i + 64], src[64 * i:64 * i + 64]
                                  ).then_inc(wide.drained[wide.slot(("v", 3))], 1)
            norm(5, xB, lambda q: dve.wait_ge(*narrow.empty(("down", 1, q))), 1e-5)
            for step in range(-2, NQ + 3):
                if step >= 3:
                    add_residual(("proj", 4, step - 3), xB, step - 3, 7)
                if 0 <= step < NQ:
                    middle(base["3"] + step, T)
                if step + 2 < NQ:
                    q = step + 2
                    front(base["3"] + q, 1024, 0.25, mask3[:, q // 2, :].unsqueeze(1).broadcast_to([P, 16, T]), T)
            norm(6, xB, lambda q: dve.wait_ge(*narrow.empty(("proj", 4, q))), 1e-5)
            for q in range(NQ):
                add_residual(("down", 2, q), xB, q, 8)

        @block.gpsimd
        def _(pool):
            g = nc.gpsimd
            chain = [0]

            def link(ins):
                chain[0] += 1
                ins.then_inc(link_pool, 1)
                pool.wait_ge(link_pool, chain[0])

            def head_mask(tile, width, heads_):
                link(g.memset(tile[:], 1.0))
                link(g.affine_select(out=tile[:], in_=tile[:], compare_op=ALU.is_ge, fill=0.0, base=0,
                                     pattern=[[-width, heads_]], channel_multiplier=1))
                link(g.affine_select(out=tile[:], in_=tile[:], compare_op=ALU.is_ge, fill=0.0, base=width - 1,
                                     pattern=[[width, heads_]], channel_multiplier=-1))

            def add_row(dst, src, name):
                g.tensor_tensor(dst, src, row(name).unsqueeze(1).broadcast_to([P, NQ, D]), ALU.add
                                ).then_inc(row_added, 1)

            def rstds(k):
                for q in range(NQ):
                    pool.wait_ge(stat_ready, k * NQ + q + 1)
                    g.tensor_tensor(rstd[:, q:q + 1], veps[:, q:q + 1], mhalf[:], ALU.pow).then_inc(rstd_ready, 1)

            def shift(u, n_scores):
                pool.wait_ge(max_ready, u + 1)
                s3 = scoresb[:, u % 3, 0:16 * n_scores].rearrange("p (h k) -> p h k", h=16)
                g.tensor_tensor(s3, s3, mx[:, u % 3, :].unsqueeze(2).broadcast_to([P, 16, n_scores]), ALU.subtract
                                ).then_inc(shifted, 1)

            def normalize(u, n_scores):
                pool.wait_ge(rcp_ready, u + 1)
                pool.wait_ge(*wide.full(("T", u - 2)))
                s3 = scoresb[:, u % 3, 0:16 * n_scores].rearrange("p (h k) -> p h k", h=16)
                g.tensor_tensor(probs[:, u % 2, :].rearrange("p (h k) -> p h k", h=16), s3[:, :, 0:T],
                                rcp[:, u % 3, :].unsqueeze(2).broadcast_to([P, 16, T]), ALU.mult).then_inc(prob_ready, 1)
                if n_scores > T:
                    g.tensor_tensor(probsb[:, u % 2, :], s3[:, :, T], rcp[:, u % 3, :], ALU.mult).then_inc(prob_ready, 1)

            def normalize0(u):
                pool.wait_ge(rcp_ready, u + 1)
                if u >= 2:
                    pool.wait_ge(*wide.full(("T", u - 2)))
                s3 = scoresb[:, u % 3, 0:2 * KEYS0].rearrange("p (i k) -> p i k", i=2)
                for lo, hi, o in ((0, S, 0), (S, KEYS0, 2 * S)):
                    n = hi - lo
                    g.tensor_tensor(probs[:, u % 2, o:o + 2 * n].rearrange("p (i k) -> p i k", i=2), s3[:, :, lo:hi],
                                    rcp[:, u % 3, 0:2].unsqueeze(2).broadcast_to([P, 2, n]), ALU.mult).then_inc(prob_ready, 1)

            def spread_keys0(b):
                pool.wait_ge(*wide.empty(("k0", b)))
                for c in range(NC):
                    g.tensor_tensor(kbd0[b % 2][:, c], kT2[:, c, :].unsqueeze(1).broadcast_to([P, 8, KEYS0]),
                                    head16[:].unsqueeze(2).broadcast_to([P, 8, KEYS0]), ALU.mult).then_inc(kbd_ready, 1)

            def spread_keys(layer, kbd, mask, heads_):
                pool.wait_ge(*wide.empty(("k", layer)))
                for c in range(NC):
                    g.tensor_tensor(kbd[:, c],
                                    kT2[:, c, 0:256].rearrange("p (b k) -> p b k", b=B).unsqueeze(2).broadcast_to([P, B, heads_, T]),
                                    mask[:].unsqueeze(1).unsqueeze(3).broadcast_to([P, B, heads_, T]), ALU.mult
                                    ).then_inc(kbd_ready, 1)

            link(g.memset(ident[:], 0.0))
            g.affine_select(out=ident[:], in_=ident[:], compare_op=ALU.not_equal, fill=1.0, base=0,
                            pattern=[[-1, P]], channel_multiplier=1).then_inc(consts, 1)
            link(g.memset(mhalf[:], -0.5))
            head_mask(head16, 16, 8)
            head_mask(head8, 8, 16)
            pool.wait_ge(*wide.empty("ctxT"))
            g.tensor_copy(ctxD[:].rearrange("p c b a k -> p (c b) a k"),
                          ctxT[:].rearrange("p c (b k) -> p (c b) k", b=B).unsqueeze(2).broadcast_to([P, NC * B, 2, T])
                          ).then_inc(ctxd_ready, 1)
            for i in range(2):
                g.memset(vpad0[i], 0.0).then_inc(vzero, 1)
            spread_keys0(0)
            pool.wait_ge(load["rows"], 16 * len(ROWS))
            pool.wait_ge(load["x"], 16)
            add_row(xB[:], xA, "L0_out_b")
            pool.wait_ge(row_added, 1)
            pool.wait_ge(*wide.full(("x0T", 1)))
            add_row(xA, xA, "L0_mlp_b2")
            for step in range(len(units0)):
                normalize0(step)
                if step % 16 == 4 and step // 16 + 1 < B:
                    spread_keys0(step // 16 + 1)
            rstds(0)
            pool.wait_ge(load["w1"], 64)
            for kc in range(NC):
                g.tensor_copy(wkrep[:, kc].rearrange("p c (k r d) -> p (c k) r d", r=4, d=8),
                              k_w1[:, kc].rearrange("p (k d) -> p k d", d=8).unsqueeze(2).broadcast_to([P, 8, 4, 8])
                              ).then_inc(wk_ready, 1)
            pool.wait_ge(*narrow.full(("down", 0, NQ - 1)))
            g.memset(region[:, 0:8192], 0.0).then_inc(vzero, 1)
            pool.wait_ge(*wide.full(("x1T", 1)))
            add_row(xA, xA, "L1_bo")
            spread_keys(1, kbd1, head8, 16)

            def attend(first, n, n_scores):
                for step in range(-2, n):
                    if step >= 0:
                        normalize(first + step, n_scores)
                    if step + 2 < n:
                        shift(first + step + 2, n_scores)

            attend(base["1"], len(units1), T)
            rstds(1)
            for q in range(NQ):
                pool.wait_ge(xn_ready, NQ + q + 1)
                link(g.tensor_tensor(xn[:, q, :], xn[:, q, :], row("L1_gamma"), ALU.mult))
                g.tensor_tensor(xB[:, q, :], xn[:, q, :], row("L1_beta"), ALU.add).then_inc(x2_ready, 1)
            rstds(2)
            pool.wait_ge(xn_ready, 3 * NQ)
            add_row(xB[:], xB[:], "L2_bo1")
            attend(base["2a"], NQ, 65)
            rstds(3)
            pool.wait_ge(xn_ready, 4 * NQ)
            add_row(xB[:], xB[:], "L2_bo2")
            attend(base["2b"], NQ, 65)
            pool.wait_ge(*narrow.full(("proj", 3, NQ - 1)))
            g.memset(region[:, 12288:16384], 0.0).then_inc(vzero, 1)
            rstds(4)
            pool.wait_ge(xn_ready, 5 * NQ)
            add_row(xB[:], xB[:], "L2_b_fc2")
            spread_keys(3, kbd3, head16, 8)
            rstds(5)
            pool.wait_ge(xn_ready, 6 * NQ)
            add_row(xB[:], xB[:], "L3_cproj_b")
            attend(base["3"], NQ, T)
            rstds(6)
            pool.wait_ge(xn_ready, 7 * NQ)
            add_row(xB[:], xB[:], "L3_proj_b")


def kernel(**inputs):
    import numpy as np
    import concourse.bacc as bacc
    from concourse.bass_utils import run_bass_kernel_spmd

    nc = bacc.Bacc("TRN2", target_bir_lowering=False, num_devices=1)
    arrays, args = {}, {}
    for name, value in inputs.items():
        a = np.ascontiguousarray(value)
        if a.dtype == np.bool_:
            a = a.view(np.uint8)
        arrays["in_" + name] = a
        args[name] = nc.dram_tensor("in_" + name, a.shape, mybir.dt.from_np(a.dtype), kind="ExternalInput").ap()
    out = nc.dram_tensor("out", (B, S, D), F32, kind="ExternalOutput").ap()
    build(nc, args, out)
    r = run_bass_kernel_spmd(nc, [arrays], core_ids=[0])
    return r.results[0]["out"]
```

```python
from contextlib import ExitStack

import concourse.bass as bass
from concourse import mybir

P = 128
B, S, D, T = 4, 256, 256, 64
NQ = B * S // P
NC = D // P
F = 4 * D
NF = F // P
H2, DH2 = 16, 128
NK2 = B * T + 1
KEYS0 = S + T
GROUP = 4
TURN_AT = 4
NEG0 = -1.0e30
NEG3 = -3.4028234663852886e38
SCORES, TURNS = (0, 1), (2,)
ALU = mybir.AluOpType
ACT = mybir.ActivationFunctionType
AX = mybir.AxisListType.X
F32 = mybir.dt.float32
I32 = mybir.dt.int32
U8 = mybir.dt.uint8

COLUMNS = [
    ("L0_q_b", 2), ("L0_k_b", 2), ("L0_v_b", 2), ("L0_postnorm_w", 2), ("L0_mlp_b1", 8),
    ("L1_bq", 2), ("L1_bk", 2), ("L1_bv", 2),
    ("L2_ln1_scale", 2), ("L2_ln1_offset", 2), ("L2_bq1", 16), ("L2_bk1", 16), ("L2_bv1", 16),
    ("L2_bias_k1", 16), ("L2_bias_v1", 16),
    ("L2_ln2_scale", 2), ("L2_ln2_offset", 2), ("L2_bq2", 16), ("L2_bk2", 16), ("L2_bv2", 16),
    ("L2_bias_k2", 16), ("L2_bias_v2", 16), ("L2_ln_mlp_scale", 2), ("L2_ln_mlp_offset", 2),
    ("L2_b_fc1", 8),
    ("L3_ln1_w", 2), ("L3_ln1_b", 2), ("L3_q_b", 2), ("L3_k_b", 2), ("L3_v_b", 2),
    ("L3_ln2_w", 2), ("L3_ln2_b", 2), ("L3_fc_b", 8),
]
ROWS = ["L0_out_b", "L0_mlp_b2", "L1_bo", "L1_gamma", "L1_beta", "L2_bo1", "L2_bo2", "L2_b_fc2",
        "L3_cproj_b", "L3_proj_b"]


class Ring:

    def __init__(self, filled, drained):
        self.filled, self.drained = filled, drained
        self.uses = [0] * len(filled)
        self.owed = [0] * len(filled)
        self.order = list(range(len(filled)))
        self.tiles = {}

    def take(self, key, drains=1, among=(0, 1, 2)):
        s = next(x for x in self.order if x in among)
        before = self.owed[s]
        self.order.remove(s)
        self.order.append(s)
        self.uses[s] += 1
        self.owed[s] += drains
        self.tiles[key] = (s, self.uses[s], self.owed[s])
        return s, before

    def slot(self, key):
        return self.tiles[key][0]

    def full(self, key):
        s, n, _ = self.tiles[key]
        return self.filled[s], n

    def empty(self, key):
        s, _, n = self.tiles[key]
        return self.drained[s], n


def build(nc, t, out):
    ctx = ExitStack()
    with ctx:
        def sb(name, shape, dt=F32):
            return ctx.enter_context(nc.sbuf_tensor(name, shape, dt))

        def sem(name):
            return ctx.enter_context(nc.semaphore(name))

        wide_ps = ctx.enter_context(nc.psum_tensor("wide_ps", [P, 3, 1024], F32))
        narrow_ps = ctx.enter_context(nc.psum_tensor("narrow_ps", [P, 2, 512], F32))
        wide = Ring([sem(f"wide{i}_filled") for i in range(3)], [sem(f"wide{i}_drained") for i in range(3)])
        narrow = Ring([sem(f"narrow{i}_filled") for i in range(2)], [sem(f"narrow{i}_drained") for i in range(2)])

        ident = sb("ident", [P, P])
        head16 = sb("head16", [P, 8])
        head8 = sb("head8", [P, 16])
        mhalf = sb("mhalf", [P, 1])
        col = sb("col", [P, 3, P])
        rows = sb("rows", [P, len(ROWS), D])
        mask0 = sb("mask0", [P, B, T])
        mask1 = sb("mask1", [P, NQ, T])
        mask3 = sb("mask3", [P, B, T])
        xq = sb("xq", [P, 4112])
        xA = xq[:, 2064:4112].rearrange("p (q d) -> p q d", q=NQ)
        xB = sb("xB", [P, NQ, D])
        xn = sb("xn", [P, NQ, D])
        actT = sb("actT", [P, NC, B * S])
        qT = xq[:, 0:2048].rearrange("p (c n) -> p c n", c=NC)
        ctxT = sb("ctxT", [P, NC, B * T])
        ctxD = sb("ctxD", [P, NC, B, 2, T])
        stats = sb("stats", [P, NQ, 6])
        mv = sb("mv", [P, NQ, 2])
        veps = sb("veps", [P, NQ])
        rstd = sb("rstd", [P, NQ])
        scoresb = sb("scoresb", [P, 3, 16 * 65])
        probs = sb("probs", [P, 2, 1024])
        mask0i = probs[:, 0, 0:B * T].bitcast(I32)
        mask3i = probs[:, 0, B * T:B * T + B * T // 4].bitcast(U8)
        probsb = sb("probsb", [P, 2, 16])
        probsT = sb("probsT", [P, 2, 1024])
        probsbT = sb("probsbT", [16, 2, P])
        mx = sb("mx", [P, 3, 16])
        sums = sb("sums", [P, 3, 16])
        rcp = sb("rcp", [P, 3, 16])
        wstream = sb("wstream", [P, 8192])
        wsmall = sb("wsmall", [P, 2048])
        colraw = wsmall[:, 1280:1664].rearrange("p (a n) -> p a n", a=3)
        wkrep = sb("wkrep", [P, NC, NC, P])
        bvhot = sb("bvhot", [P, H2, H2])
        vwb = sb("vwb", [16, D])
        headbuf = sb("headbuf", [P, 1568])
        heads = headbuf[:].rearrange("p (a n) -> p a n", a=2)
        kT2 = headbuf[:, 0:NC * KEYS0].rearrange("p (c n) -> p c n", c=NC)
        region = sb("region", [P, 16416])

        kbd0 = [region[:, i * 5120:(i + 1) * 5120].rearrange("p (c h k) -> p c h k", c=NC, h=8) for i in range(2)]
        vpad0 = [region[:, 10240 + i * 2560:10240 + (i + 1) * 2560] for i in range(2)]
        w0 = wstream
        q_w0 = w0[:, 0:512].rearrange("p (c n) -> p c n", c=NC)
        kv_w0 = w0[:, 512:1536].rearrange("p (c n two) -> p c two n", c=NC, two=2)
        out_w0 = w0[:, 1536:2048].rearrange("p (c n) -> p c n", c=NC)
        mlp_w1_0 = w0[:, 2048:4096].rearrange("p (c n) -> p c n", c=NC)
        mlp_w2_0 = w0[:, 4096:6144].rearrange("p (c n) -> p c n", c=NF)
        hid = region[:, 0:NF * 1024].rearrange("p (f n) -> p f n", f=NF)
        q_w1 = wsmall[:, 0:512].rearrange("p (c n) -> p c n", c=NC)
        k_w1 = wsmall[:, 512:640].rearrange("p (c n) -> p c n", c=NC)
        v_w1 = wsmall[:, 640:768].rearrange("p (c n) -> p c n", c=NC)
        out_w1 = wsmall[:, 768:1280].rearrange("p (c n) -> p c n", c=NC)
        vpad1 = region[:, 0:8192].rearrange("p (b r n) -> p b r n", b=B, r=16)
        kbd1 = region[:, 8192:16384].rearrange("p (c b h k) -> p c b h k", c=NC, b=B, h=16)
        G = region[:, 0:NC * H2 * NK2].rearrange("p (c h k) -> p c h k", c=NC, h=H2)
        VW = region[:, 8224:8224 + 8192].rearrange("p (b r n) -> p b r n", b=B, r=8)
        cB = xq[:, 0:H2 * NK2].rearrange("p (h k) -> p h k", h=H2)
        wring = [wstream[:, i * 4096:(i + 1) * 4096].rearrange("p (m n) -> p m n", m=4) for i in range(2)]
        fc1_w2 = wstream[:, 0:2048].rearrange("p (c n) -> p c n", c=NC)
        fc2_w2 = wstream[:, 2048:4096].rearrange("p (c n) -> p c n", c=NF)
        fc_w3 = wstream[:, 4096:6144].rearrange("p (c n) -> p c n", c=NC)
        proj_w3 = wstream[:, 6144:8192].rearrange("p (c n) -> p c n", c=NF)
        w3 = [wsmall[:, i * 512:(i + 1) * 512].rearrange("p (c n) -> p c n", c=NC) for i in range(4)]
        kbd3 = region[:, 8192:12288].rearrange("p (c b h k) -> p c b h k", c=NC, b=B, h=8)
        vpad3 = region[:, 12288:16384].rearrange("p (b r n) -> p b r n", b=B, r=8)

        load = {k: sem("loaded_" + k) for k in
                ("x", "ctx", "cols0", "cols", "rows", "masks", "w0", "mlp0", "w1", "w3", "mlp2", "mlp3")}
        ring_loaded = [sem("ring0_loaded"), sem("ring1_loaded")]
        consts = sem("consts_ready")
        link_dve = sem("dve_step")
        link_pool = sem("pool_step")
        cols_zeroed = sem("cols_zeroed")
        stat_ready = sem("stat_ready")
        rstd_ready = sem("rstd_ready")
        xn_ready = sem("xn_ready")
        x2_ready = sem("x2_ready")
        row_added = sem("row_added")
        vzero = sem("vpad_zeroed")
        kbd_ready = sem("kbd_ready")
        vpad_ready = sem("vpad_ready")
        wk_ready = sem("wk_replicated")
        ctxd_ready = sem("ctx_doubled")
        max_ready = sem("max_ready")
        shifted = sem("scores_shifted")
        exp_done = sem("exp_done")
        rcp_ready = sem("rcp_ready")
        prob_ready = sem("probs_normalized")
        bias_key = sem("bias_key_copied")
        hot_ready = sem("bias_values_spread")
        ring_used = sem("ring_chunk_used")
        stored = sem("out_stored")

        colrow = {}
        n = 0
        for name, k in COLUMNS:
            if n // P != (n + k - 1) // P or name == "L1_bq":
                n = -(-n // P) * P
            colrow[name] = (n, k)
            n += k

        def column(name, i=0):
            r = colrow[name][0] + i
            return col[:, r // P, r % P:r % P + 1]

        def row(name):
            i = ROWS.index(name)
            return rows[:, i, :]

        units0 = [(b, q, r) for b in range(B) for q in range(2) for r in range(8)]
        units1 = [(q, c) for q in range(NQ) for c in range(NC)]
        units2 = [(q,) for q in range(NQ)]
        units3 = [(q,) for q in range(NQ)]
        base = {}
        probcount = [0]
        shiftcount = [0]
        at = 0
        LOADS = {"cols0": 5, "cols": len(COLUMNS) - 5 + 2}
        for name, us in (("0", units0), ("1", units1), ("2a", units2), ("2b", units2), ("3", units3)):
            base[name] = at
            at += len(us)
            for _ in us:
                probcount.append(probcount[-1] + (1 if name in "13" else 2))
                shiftcount.append(shiftcount[-1] + (name != "0"))

        def done0(step):
            return (step - 3) // 8 if 0 <= step - 3 < len(units0) and units0[step - 3][2] == 7 else None

        def done1(step):
            return units1[step - 3][0] if 0 <= step - 3 < len(units1) and units1[step - 3][1] == 1 else None

        def done2(step):
            return step - 2 if 0 <= step - 2 < NQ else None

        def done3(step):
            return step - 3 if 0 <= step - 3 < NQ else None

        qoff = lambda q: slice(q * P, (q + 1) * P)

        def diagonal(tile, offset, dims, width=None):
            a = tile[:, offset:offset + 1] if len(tile.shape) == 2 else tile[:].rearrange("p a b -> p (a b)")[:, offset:offset + 1]
            return bass.AP(tensor=a.tensor, offset=a.offset, ap=[list(a.ap[0])] + [list(d) for d in dims])

        def colrange(name):
            r, k = colrow[name]
            return col[:, r // P, r % P:r % P + k]

        def parameter_rows(first):
            loads = []
            for name, k in COLUMNS:
                r, _ = colrow[name]
                dst = colraw[r % P:r % P + k, r // P, :]
                key = name[:3] + "xattn_" + name[3:]
                if (name[:2] == "L0") != first:
                    continue
                if name in ("L0_k_b", "L0_v_b"):
                    src = t["L0_xattn_kv_b"].rearrange("(r p two) -> two r p", r=2, two=2)[int(name == "L0_v_b")]
                    loads.append((dst, src, True))
                elif name in ("L1_bk", "L1_bv"):
                    for c in range(NC):
                        src = t[key].rearrange("(k d) -> k d", d=8)[4 * c:4 * c + 4].unsqueeze(1).broadcast_to([4, 4, 8]).unsqueeze(0)
                        loads.append((colraw[r % P + c:r % P + c + 1, r // P, :].rearrange("p (a b c) -> p a b c", a=4, b=4),
                                      src, False))
                elif "bias_" in name:
                    loads.append((dst, t[key].rearrange("a b h d -> (a b h) d"), False))
                else:
                    loads.append((dst, t[key].rearrange("(r p) -> r p", p=P), False))
            return loads

        block = ctx.enter_context(nc.Block())

        @block.tensor
        def _(pe):
            mm = nc.tensor.matmul

            def take_wide(key, drains=1, among=(0, 1, 2)):
                s, before = wide.take(key, drains, among)
                if before:
                    pe.wait_ge(wide.drained[s], before)
                return wide_ps[:, s, :], wide.filled[s]

            def take_narrow(key, drains=1):
                s, before = narrow.take(key, drains)
                if before:
                    pe.wait_ge(narrow.drained[s], before)
                return narrow_ps[:, s, :], narrow.filled[s]

            def turn(key, src, ready=None, drains=1):
                for half in range(2):
                    ps, filled = take_wide((key, half), drains)
                    for j in range(4):
                        q = 4 * half + j
                        if ready:
                            ready(q)
                        for c in range(NC):
                            m = nc.tensor.transpose(ps[:, c * 512 + j * P:c * 512 + (j + 1) * P],
                                                    src[:, q, c * P:(c + 1) * P], ident[:])
                    m.then_inc(filled, 1)

            def norm_turn(k):
                turn(("ln", k), xn, lambda q: pe.wait_ge(xn_ready, k * NQ + q + 1), 2)

            def queries(layer, w, src_key):
                for c in range(NC):
                    ps, filled = take_wide(("q", layer, c))
                    for half in range(2):
                        pe.wait_ge(*wide.empty((src_key, half)))
                        for kc in range(NC):
                            m = mm(ps[:, half * 512:(half + 1) * 512], w[:, kc, c * P:(c + 1) * P],
                                   actT[:, kc, half * 512:(half + 1) * 512], start=kc == 0, stop=kc == NC - 1)
                    m.then_inc(filled, 1)

            def mlp(n, k, w1, w2):
                for half in range(2):
                    for fp in range(NF // 2):
                        ps, filled = take_wide(("up", n, half, fp), 2)
                        pe.wait_ge(*wide.empty((("ln", k), half)))
                        for j in range(2):
                            f = 2 * fp + j
                            for kc in range(NC):
                                m = mm(ps[:, j * 512:(j + 1) * 512], w1[:, kc, f * P:(f + 1) * P],
                                       actT[:, kc, half * 512:(half + 1) * 512], start=kc == 0, stop=kc == NC - 1)
                        m.then_inc(filled, 1)
                for q in range(NQ):
                    ps, filled = take_narrow(("down", n, q))
                    for fp in range(NF // 2):
                        pe.wait_ge(*wide.empty(("up", n, q // 4, fp)))
                    for f in range(NF):
                        m = mm(ps[:, 0:D], hid[:, f, qoff(q)], w2[:, f, :], start=f == 0, stop=f == NF - 1)
                    m.then_inc(filled, 1)

            def project(layer, q, w, aokeys):
                ps, filled = take_narrow(("proj", layer, q))
                for key in aokeys:
                    pe.wait_ge(*narrow.empty(key))
                for c in range(NC):
                    m = mm(ps[:, 0:D], qT[:, c, qoff(q)], w[:, c, :], start=c == 0, stop=c == NC - 1)
                m.then_inc(filled, 1)

            def turn_probs(u):
                ps, filled = take_wide(("T", u), among=TURNS)
                pe.wait_ge(prob_ready, probcount[u + 1])
                n = 5 if u < len(units0) else 8
                for j in range(n):
                    m = nc.tensor.transpose(ps[:, j * P:(j + 1) * P], probs[:, u % 2, j * P:(j + 1) * P], ident[:])
                m.then_inc(filled, 1)

            def values_small(layer, wv, nv):
                ps, filled = take_wide(("v", layer), 16 if layer == 1 else 8)
                for b in range(B):
                    for kc in range(NC):
                        m = mm(ps[:, b * nv:(b + 1) * nv], ctxD[:, kc, b, :, :].rearrange("p a k -> p (a k)"),
                               wv[:, kc, :], start=kc == 0, stop=kc == NC - 1)
                m.then_inc(filled, 1)

            def keys_small(layer, wk):
                ps, filled = take_wide(("k", layer), 2)
                for c in range(NC):
                    for kc in range(NC):
                        m = mm(ps[:, c * 256:(c + 1) * 256], wk(kc, c), ctxT[:, kc, :], start=kc == 0, stop=kc == NC - 1)
                m.then_inc(filled, 1)

            pe.wait_ge(consts, 1)
            pe.wait_ge(load["x"], 16)
            turn("x0T", xA)
            pe.wait_ge(load["ctx"], 16)
            ps, filled = take_wide("ctxT")
            for c in range(NC):
                for j in range(2):
                    m = nc.tensor.transpose(ps[:, c * 256 + j * P:c * 256 + (j + 1) * P],
                                            xn[:, j, c * P:(c + 1) * P], ident[:])
            m.then_inc(filled, 1)

            pe.wait_ge(load["cols0"], 16 * LOADS["cols0"])
            ps, filled = take_wide("cols0")
            nc.tensor.transpose(ps[:, 0:P], colraw[:, 0, :], ident[:]).then_inc(filled, 1)

            pe.wait_ge(load["w0"], 16 * 3)
            queries(0, q_w0, "x0T")
            pe.wait_ge(*wide.empty("ctxT"))
            pe.wait_ge(ctxd_ready, 1)

            def keys0(b):
                ps, filled = take_wide(("k0", b), 2)
                for c in range(NC):
                    for off, n, src in ((0, S, actT[:, :, b * S:(b + 1) * S]), (S, T, ctxT[:, :, b * T:(b + 1) * T])):
                        for kc in range(NC):
                            m = mm(ps[:, c * 512 + off:c * 512 + off + n], kv_w0[:, kc, 0, c * P:(c + 1) * P],
                                   src[:, kc, :], start=kc == 0, stop=kc == NC - 1)
                m.then_inc(filled, 1)
                ps, filled = take_wide(("v0", b), 4)
                for j in range(3):
                    for kc in range(NC):
                        src = (actT[:, kc, b * S + j * P:b * S + (j + 1) * P] if j < 2 else
                               ctxD[:, kc, b, :, :].rearrange("p a k -> p (a k)"))
                        m = mm(ps[:, j * 256:(j + 1) * 256], src, kv_w0[:, kc, 1, :], start=kc == 0, stop=kc == NC - 1)
                m.then_inc(filled, 1)

            def scores0(u):
                b, q, r = units0[u]
                ps, filled = take_wide(("S", u), 2, SCORES)
                if q == 0 and r == 0:
                    pe.wait_ge(kbd_ready, 8 * (b + 1))
                if u == 0:
                    pe.wait_ge(*wide.empty(("q", 0, 0)))
                    pe.wait_ge(*wide.empty(("q", 0, 1)))
                c = r // 4
                for i in range(2):
                    m = mm(ps[:, i * 512:i * 512 + KEYS0], qT[:, c, qoff(2 * b + q)],
                           kbd0[b % 2][:, c, 2 * (r % 4) + i, :], start=True, stop=True)
                m.then_inc(filled, 1)

            def values0(u):
                b, q, r = units0[u]
                c = r // 4
                if r % 4 == 0:
                    ps, filled = take_narrow(("ao", 0, 2 * b + q, c))
                    ao[0] = (ps, filled)
                ps, filled = ao[0]
                pe.wait_ge(*wide.empty(("T", u)))
                if q == 0 and r == 0:
                    pe.wait_ge(*wide.empty(("v0", b)))
                vp = vpad0[b % 2]
                for j in range(5):
                    i, kb = j // 2, j % 2
                    lhs = (vp[:, (kb * 16 + 2 * r + i) * 64:(kb * 16 + 2 * r + i + 1) * 64] if j < 4 else
                           vp[:, 2048 + r * 64:2048 + (r + 1) * 64])
                    po = 64 * (r % 4 // 2)
                    m = mm(ps[po:po + 64, 0:P], lhs, probsT[:, u % 2, j * P:(j + 1) * P],
                           start=r % 2 == 0 and j == 0, stop=r % 2 == 1 and j == 4)
                if r % 4 == 3:
                    m.then_inc(filled, 1)

            ao = [None]
            keys0(0)
            n0 = len(units0)
            for step in range(-3, n0 + 2):
                if 0 <= step < n0:
                    turn_probs(step)
                if step + 3 < n0:
                    scores0(step + 3)
                if 0 <= step < n0 and step % 16 == 4 and step // 16 + 1 < B:
                    keys0(step // 16 + 1)
                if 0 <= step - 1 < n0:
                    values0(step - 1)
                if step - 2 >= 0 and units0[step - 2][2] == 7:
                    q = (step - 2) // 8
                    project(0, q, out_w0, [("ao", 0, q, 0), ("ao", 0, q, 1)])
            pe.wait_ge(load["cols"], 16 * LOADS["cols"])
            ps, filled = take_wide("cols")
            for i in range(2):
                m = nc.tensor.transpose(ps[:, i * P:(i + 1) * P], colraw[:, 1 + i, :], ident[:])
            m.then_inc(filled, 1)
            pe.wait_ge(wk_ready, 2)
            keys_small(1, lambda kc, c: wkrep[:, kc, c, :])
            norm_turn(0)
            pe.wait_ge(load["mlp0"], 32)
            mlp(0, 0, mlp_w1_0, mlp_w2_0)

            turn("x1T", xA, lambda q: pe.wait_ge(*narrow.empty(("down", 0, q))))
            pe.wait_ge(load["w1"], 16 * 4)
            queries(1, q_w1, "x1T")

            values_small(1, v_w1, 64)

            def scores1(i):
                q, c = units1[i]
                ps, filled = take_wide(("S", base["1"] + i), among=SCORES)
                if i == 0:
                    pe.wait_ge(*wide.empty(("q", 1, 0)))
                    pe.wait_ge(*wide.empty(("q", 1, 1)))
                    pe.wait_ge(kbd_ready, 8 * B + 2)
                for g in range(2):
                    m = mm(ps[:, g * 512:(g + 1) * 512], qT[:, c, qoff(q)], kbd1[:, c, q // 2, 8 * g:8 * g + 8, :],
                           start=True, stop=True)
                m.then_inc(filled, 1)

            def values1(i):
                q, c = units1[i]
                u = base["1"] + i
                ps, filled = take_narrow(("ao", 1, q, c))
                pe.wait_ge(*wide.empty(("T", u)))
                if i == 0:
                    pe.wait_ge(*wide.empty(("v", 1)))
                for j in range(8):
                    m = mm(ps[:, 0:P], vpad1[:, q // 2, 8 * c + j, :], probsT[:, u % 2, j * P:(j + 1) * P],
                           start=j == 0, stop=j == 7)
                m.then_inc(filled, 1)

            n1 = len(units1)
            for step in range(-3, n1 + 2):
                if 0 <= step < n1:
                    turn_probs(base["1"] + step)
                if step + 3 < n1:
                    scores1(step + 3)
                if 0 <= step - 1 < n1:
                    values1(step - 1)
                if step - 2 >= 0 and units1[step - 2][1] == 1:
                    q = units1[step - 2][0]
                    project(1, q, out_w1, [("ao", 1, q, 0), ("ao", 1, q, 1)])

            def weights2(a, h):
                g = 4 * a + h // GROUP
                wbuf = wring[g % 2]
                return [wbuf[:, m, :].rearrange("p (c n) -> p c n", c=NC) for m in range(3)] + [
                    wbuf[:, 3, :].rearrange("p (h n) -> p h n", h=GROUP)]

            def head_products2(a, h):
                g = 4 * a + h // GROUP
                wq, wk, wv, wo = weights2(a, h)
                o = (h % GROUP) * P
                if h % GROUP == 0:
                    pe.wait_ge(ring_loaded[g % 2], 64 * (g // 2 + 1))
                if h == 0:
                    pe.wait_ge(hot_ready, a + 1)
                ps, filled = take_wide(("kvq", a, h), 4)
                for kc in range(NC):
                    mm(ps[:, 0:256], wk[:, kc, o:o + P], ctxT[:, kc, :], start=kc == 0, stop=kc == NC - 1)
                for kc in range(NC):
                    mm(ps[:, 256:512], wv[:, kc, o:o + P], ctxT[:, kc, :], start=kc == 0, stop=kc == NC - 1)
                mm(ps[0:16, 768:1024], bvhot[:, h, :], wo[:, h % GROUP, :], start=True, stop=True)
                for kc in range(NC):
                    m = nc.tensor.transpose(ps[:, 512 + kc * P:512 + (kc + 1) * P], wq[:, kc, o:o + P], ident[:])
                m.then_inc(filled, 1)

            def precompute2(a):
                head_products2(a, 0)
                for h in range(H2):
                    if a == 1 and h == TURN_AT:
                        norm_turn(3)
                    if h + 1 < H2:
                        head_products2(a, h + 1)
                    wo = weights2(a, h)[3]
                    hb = heads[:, h % 2, :]
                    ps, filled = take_wide(("G", a, h))
                    pe.wait_ge(*wide.empty(("kvq", a, h)))
                    pe.wait_ge(bias_key, a * H2 + h + 1)
                    for c in range(NC):
                        m = mm(ps[:, c * 512:c * 512 + NK2], hb[:, 513 + c * P:513 + (c + 1) * P], hb[:, 0:NK2],
                               start=True, stop=True)
                    m.then_inc(filled, 1)
                    bq = column(f"L2_bq{a + 1}", h)
                    ps, filled = take_narrow(("cB", a, h))
                    mm(ps[:, 0:NK2], bq.broadcast_to([P, P]), hb[:, 0:NK2], start=True, stop=True).then_inc(filled, 1)
                    if h % 2 == 0:
                        vw = take_wide(("VW", a, h // 2))
                    ps, filled = vw
                    po = T * (h % 2)
                    for b in range(B):
                        m = mm(ps[po:po + T, b * D:(b + 1) * D], hb[:, 257 + b * T:257 + (b + 1) * T],
                               wo[:, h % GROUP, :], start=True, stop=True)
                    if h % 2 == 1:
                        m.then_inc(filled, 1)

            def scores2(a, q):
                u = base["2a" if a == 0 else "2b"] + q
                b = q // 2
                ps, filled = take_wide(("S", u), among=SCORES)
                if q == 0:
                    for half in range(2):
                        pe.wait_ge(*wide.empty((("ln", 2 + a), half)))
                for g in range(2):
                    for c in range(NC):
                        m = mm(ps[:, g * 512:(g + 1) * 512], actT[:, c, qoff(q)],
                               G[:, c, 8 * g:8 * g + 8, b * T:(b + 1) * T], start=c == 0, stop=c == NC - 1)
                m.then_inc(filled, 1)

            def scores2_bias(ps, q):
                for c in range(NC):
                    m = mm(ps[:, 0:H2], actT[:, c, qoff(q)], G[:, c, :, NK2 - 1], start=c == 0, stop=c == NC - 1)
                return m

            def attend2(a):
                u0 = base["2a" if a == 0 else "2b"]
                for h in range(H2):
                    pe.wait_ge(*wide.empty(("G", a, h)))
                for step in range(-3, NQ + 1):
                    if 0 <= step < NQ:
                        turn_probs(u0 + step)
                    if step + 3 < NQ:
                        scores2(a, step + 3)
                    if step < NQ:
                        ps, filled = take_narrow(("X", a, step), int(step + 3 < NQ) + int(step >= 0))
                        if step + 3 < NQ:
                            m = scores2_bias(ps, step + 3)
                        if step >= 0:
                            m = nc.tensor.transpose(ps[0:16, P:2 * P], probsb[:, (u0 + step) % 2, :], ident[:])
                        m.then_inc(filled, 1)
                    if step >= 1:
                        q = step - 1
                        u = u0 + q
                        ps, filled = take_narrow(("proj", 2 + a, q))
                        pe.wait_ge(*wide.empty(("T", u)))
                        pe.wait_ge(*narrow.empty(("X", a, q)))
                        if q == 0:
                            for r in range(8):
                                pe.wait_ge(*wide.empty(("VW", a, r)))
                        for r in range(8):
                            mm(ps[:, 0:D], probsT[:, u % 2, r * P:(r + 1) * P], VW[:, q // 2, r, :],
                               start=r == 0, stop=False)
                        mm(ps[:, 0:D], probsbT[:, u % 2, :], vwb[:, :], start=False, stop=True).then_inc(filled, 1)

            precompute2(0)
            norm_turn(2)
            attend2(0)
            precompute2(1)
            attend2(1)
            pe.wait_ge(load["w3"], 64)
            keys_small(3, lambda kc, c: w3[1][:, kc, c * P:(c + 1) * P])
            values_small(3, w3[2], 256)
            norm_turn(4)
            pe.wait_ge(load["mlp2"], 32)
            mlp(1, 4, fc1_w2, fc2_w2)

            norm_turn(5)
            queries(3, w3[0], ("ln", 5))

            def scores3(q):
                ps, filled = take_wide(("S", base["3"] + q), among=SCORES)
                if q == 0:
                    pe.wait_ge(*wide.empty(("q", 3, 0)))
                    pe.wait_ge(*wide.empty(("q", 3, 1)))
                    pe.wait_ge(kbd_ready, 8 * B + 4)
                for c in range(NC):
                    m = mm(ps[:, c * 512:(c + 1) * 512], qT[:, c, qoff(q)], kbd3[:, c, q // 2, :, :],
                           start=True, stop=True)
                m.then_inc(filled, 1)

            def values3(q):
                u = base["3"] + q
                ps, filled = take_narrow(("ao", 3, q), 2)
                pe.wait_ge(*wide.empty(("T", u)))
                if q == 0:
                    pe.wait_ge(*wide.empty(("v", 3)))
                for c in range(NC):
                    for j in range(4):
                        m = mm(ps[:, c * P:(c + 1) * P], vpad3[:, q // 2, 4 * c + j, :],
                               probsT[:, u % 2, (4 * c + j) * P:(4 * c + j + 1) * P], start=j == 0, stop=j == 3)
                m.then_inc(filled, 1)

            for step in range(-3, NQ + 2):
                if 0 <= step < NQ:
                    turn_probs(base["3"] + step)
                if step + 3 < NQ:
                    scores3(step + 3)
                if 0 <= step - 1 < NQ:
                    values3(step - 1)
                if step >= 2:
                    project(4, step - 2, w3[3], [("ao", 3, step - 2)])
            norm_turn(6)
            pe.wait_ge(load["mlp3"], 32)
            mlp(2, 6, fc_w3, proj_w3)

        @block.sync
        def _(sp):
            def halves(dst, src):
                return dst, src.rearrange("(c p) n -> p c n", p=P)

            sp.dma_start(xA, t["x"].rearrange("b (h p) d -> p (b h) d", p=P)).then_inc(load["x"], 16)
            sp.dma_start(xn[:, 0:2, :], t["ctx_2048"].rearrange("(g b) k d -> (b k) g d", g=2)).then_inc(load["ctx"], 16)
            sp.dma_start(*halves(q_w0, t["L0_xattn_q_w"])).then_inc(load["w0"], 16)
            sp.dma_start(w0[:, 512:1536].rearrange("p (c n) -> p c n", c=NC),
                         t["L0_xattn_kv_w"].rearrange("(c p) n -> p c n", p=P)).then_inc(load["w0"], 16)
            sp.dma_start(*halves(out_w0, t["L0_xattn_out_w"])).then_inc(load["w0"], 16)
            sp.dma_start(mask0i, t["mask_BxS2_ik0"].rearrange("(a b) k -> a (b k)", a=1).broadcast_to([P, B * T])).then_inc(load["masks"], 16)
            sp.dma_start(mask3i, t["mask_BxS2_bf1"].rearrange("(a b) k -> a (b k)", a=1).broadcast_to([P, B * T])).then_inc(load["masks"], 16)
            sp.dma_start(mask1[:], t["mask_Bx1xSxS2_ff0"].rearrange("b o (h p) k -> p (b o h) k", p=P)).then_inc(load["masks"], 16)
            for i, name in enumerate(ROWS):
                key = name[:3] + "xattn_" + name[3:]
                sp.dma_start(rows[:, i, :], t[key].rearrange("(a d) -> a d", a=1).broadcast_to([P, D])).then_inc(load["rows"], 16)
            sp.wait_ge(cols_zeroed, 1)
            for dst, src, apart in parameter_rows(False):
                sp.dma_start(dst, src, allow_slow_non_contiguous=apart).then_inc(load["cols"], 16)
            sp.dma_start(*halves(mlp_w1_0, t["L0_xattn_mlp_w1"])).then_inc(load["mlp0"], 16)
            sp.dma_start(*halves(mlp_w2_0, t["L0_xattn_mlp_w2"])).then_inc(load["mlp0"], 16)
            sp.dma_start(*halves(q_w1, t["L1_xattn_Wq"])).then_inc(load["w1"], 16)
            sp.dma_start(*halves(k_w1, t["L1_xattn_Wk"])).then_inc(load["w1"], 16)
            sp.dma_start(*halves(v_w1, t["L1_xattn_Wv"])).then_inc(load["w1"], 16)
            sp.dma_start(*halves(out_w1, t["L1_xattn_Wo"])).then_inc(load["w1"], 16)

            for g in range(8):
                a, h0 = g // 4, (g % 4) * GROUP
                if g < 2:
                    sp.wait_ge(*narrow.full(("down", 0, NQ - 1)))
                else:
                    sp.wait_ge(*wide.full(("VW", (g - 2) // 4, 2 * ((g - 2) % 4) + 1)))
                wbuf = wring[g % 2]
                for m, w in enumerate(("wq", "wk", "wv")):
                    sp.dma_start(wbuf[:, m, :].rearrange("p (c n) -> p c n", c=NC),
                                 t[f"L2_xattn_{w}{a + 1}"].rearrange("(c p) n -> p c n", p=P)[:, :, h0 * P:(h0 + GROUP) * P]
                                 ).then_inc(ring_loaded[g % 2], 16)
                sp.dma_start(wbuf[:, 3, :].rearrange("p (h n) -> p h n", h=GROUP),
                             t[f"L2_xattn_wo{a + 1}"].rearrange("(h p) n -> p h n", p=P)[:, h0:h0 + GROUP, :]
                             ).then_inc(ring_loaded[g % 2], 16)
                if g == 3:
                    sp.wait_ge(*narrow.full(("proj", 1, NQ - 1)))
                    for w, key in zip(w3, ("q_w", "k_w", "v_w", "cproj_w")):
                        sp.dma_start(*halves(w, t["L3_xattn_" + key])).then_inc(load["w3"], 16)
            sp.wait_ge(*wide.full(("VW", 1, 5)))
            sp.dma_start(*halves(fc1_w2, t["L2_xattn_w_fc1"])).then_inc(load["mlp2"], 16)
            sp.dma_start(*halves(fc2_w2, t["L2_xattn_w_fc2"])).then_inc(load["mlp2"], 16)
            sp.wait_ge(*wide.full(("VW", 1, 7)))
            sp.dma_start(*halves(fc_w3, t["L3_xattn_fc_w"])).then_inc(load["mlp3"], 16)
            sp.dma_start(*halves(proj_w3, t["L3_xattn_proj_w"])).then_inc(load["mlp3"], 16)
            for q in range(NQ):
                sp.wait_ge(*narrow.empty(("down", 2, q)))
                sp.dma_start(out.rearrange("b (h p) d -> p (b h) d", p=P)[:, q, :], xB[:, q, :]).then_inc(stored, 16)
            sp.wait_ge(stored, 16 * NQ)

        @block.scalar
        def _(act):
            act.wait_ge(cols_zeroed, 1)
            for dst, src, apart in parameter_rows(True):
                act.dma_start(dst, src, allow_slow_non_contiguous=apart).then_inc(load["cols0"], 16)

            def evac(dst, src, ring, key, **kw):
                nc.scalar.activation(dst, src, ACT.Identity, **kw).then_inc(ring.drained[ring.slot(key)], 1)

            def turned(key, dst):
                for half in range(2):
                    act.wait_ge(*wide.full((key, half)))
                    evac(dst[:, :, half * 512:(half + 1) * 512],
                         wide_ps[:, wide.slot((key, half)), :].rearrange("p (c n) -> p c n", c=NC), wide, (key, half))

            def norm_turned(k, w, b):
                for half in range(2):
                    key = (("ln", k), half)
                    act.wait_ge(*wide.full(key))
                    for c in range(NC):
                        kw = {"scale": column(w, c)}
                        if b:
                            kw["bias"] = column(b, c)
                        evac(actT[:, c, half * 512:(half + 1) * 512],
                             wide_ps[:, wide.slot(key), c * 512:(c + 1) * 512], wide, key, **kw)

            def queries(layer, b):
                for c in range(NC):
                    key = ("q", layer, c)
                    act.wait_ge(*wide.full(key))
                    evac(qT[:, c, :], wide_ps[:, wide.slot(key), :], wide, key, bias=column(b, c))

            def mlp(n, func, b1):
                for half in range(2):
                    for fp in range(NF // 2):
                        key = ("up", n, half, fp)
                        act.wait_ge(*wide.full(key))
                        for j in range(2):
                            f = 2 * fp + j
                            nc.scalar.activation(hid[:, f, half * 512:(half + 1) * 512],
                                                 wide_ps[:, wide.slot(key), j * 512:(j + 1) * 512], func,
                                                 bias=column(b1, f)).then_inc(wide.drained[wide.slot(key)], 1)

            def probs_turned(u):
                key = ("T", u)
                act.wait_ge(*wide.full(key))
                n = 5 if u < len(units0) else 8
                evac(probsT[:, u % 2, 0:n * P], wide_ps[:, wide.slot(key), 0:n * P], wide, key)

            def keys0(b):
                key = ("k0", b)
                act.wait_ge(*wide.full(key))
                if b >= 1:
                    act.wait_ge(kbd_ready, 8 * b)
                for c in range(NC):
                    evac(kT2[:, c, :], wide_ps[:, wide.slot(key), c * 512:c * 512 + KEYS0], wide, key,
                         bias=column("L0_k_b", c))

            def exp0(u):
                key = ("S", u)
                act.wait_ge(max_ready, u + 1)
                if u >= 3:
                    act.wait_ge(prob_ready, probcount[u - 2])
                for i in range(2):
                    nc.scalar.activation(scoresb[:, u % 3, i * KEYS0:(i + 1) * KEYS0],
                                         wide_ps[:, wide.slot(key), i * 512:i * 512 + KEYS0], ACT.Exp,
                                         scale=1.0 / 16, bias=mx[:, u % 3, i:i + 1],
                                         accum_out=sums[:, u % 3, i:i + 1]).then_inc(wide.drained[wide.slot(key)], 1)

            def exp(u, n):
                act.wait_ge(shifted, shiftcount[u + 1])
                nc.scalar.activation(scoresb[:, u % 3, 0:n], scoresb[:, u % 3, 0:n], ACT.Exp).then_inc(exp_done, 1)

            def attended(layer, q, c, vb):
                key = ("ao", layer, q, c)
                act.wait_ge(*narrow.full(key))
                evac(qT[:, c, qoff(q)], narrow_ps[:, narrow.slot(key), 0:P], narrow, key, bias=column(vb, c))

            def keys_small(layer, kb):
                key = ("k", layer)
                act.wait_ge(*wide.full(key))
                for c in range(NC):
                    evac(kT2[:, c, 0:256], wide_ps[:, wide.slot(key), c * 256:(c + 1) * 256], wide, key, bias=column(kb, c))

            turned("x0T", actT)
            act.wait_ge(*wide.full("ctxT"))
            evac(ctxT[:], wide_ps[:, wide.slot("ctxT"), 0:512].rearrange("p (c n) -> p c n", c=NC), wide, "ctxT")
            act.wait_ge(*wide.full("cols0"))
            evac(col[:, 0, :], wide_ps[:, wide.slot("cols0"), 0:P], wide, "cols0")
            act.wait_ge(*wide.empty("cols0"))
            queries(0, "L0_q_b")
            keys0(0)
            n0 = len(units0)
            for step in range(-2, n0 + 2):
                if step - 2 >= 0 and units0[step - 2][2] % 4 == 3:
                    b, q, r = units0[step - 2]
                    attended(0, 2 * b + q, r // 4, "L0_v_b")
                if 0 <= step < n0:
                    probs_turned(step)
                if step + 2 < n0:
                    exp0(step + 2)
                if 0 <= step < n0 and step % 16 == 4 and step // 16 + 1 < B:
                    keys0(step // 16 + 1)
            act.wait_ge(*wide.full("cols"))
            evac(col[:, 1:3, :], wide_ps[:, wide.slot("cols"), 0:256].rearrange("p (a b) -> p a b", a=2), wide, "cols")
            act.wait_ge(*wide.empty("cols"))
            keys_small(1, "L1_bk")
            norm_turned(0, "L0_postnorm_w", None)
            mlp(0, ACT.Gelu_apprx_tanh, "L0_mlp_b1")

            turned("x1T", actT)
            queries(1, "L1_bq")

            n1 = len(units1)
            for step in range(-2, n1 + 2):
                if step - 2 >= 0:
                    attended(1, *units1[step - 2], "L1_bv")
                if 0 <= step < n1:
                    probs_turned(base["1"] + step)
                if step + 2 < n1:
                    exp(base["1"] + step + 2, 1024)

            def head2(a, h):
                key = ("kvq", a, h)
                act.wait_ge(*wide.full(key))
                ps = wide_ps[:, wide.slot(key), :]
                hb = heads[:, h % 2, :]
                evac(hb[:, 0:256], ps[:, 0:256], wide, key, bias=column(f"L2_bk{a + 1}", h))
                evac(hb[:, 257:513], ps[:, 256:512], wide, key, bias=column(f"L2_bv{a + 1}", h))
                nc.scalar.copy(hb[:, 256:257], column(f"L2_bias_k{a + 1}", h)).then_inc(bias_key, 1)

            def precompute2(a):
                head2(a, 0)
                for h in range(H2):
                    if a == 1 and h == TURN_AT:
                        norm_turned(3, "L2_ln2_scale", "L2_ln2_offset")
                    if h + 1 < H2:
                        head2(a, h + 1)
                    key = ("cB", a, h)
                    act.wait_ge(*narrow.full(key))
                    if a == 0 and h == 8:
                        act.wait_ge(xn_ready, 2 * NQ)
                    nc.scalar.mul(cB[:, h, :], narrow_ps[:, narrow.slot(key), 0:NK2], DH2 ** -0.5
                                  ).then_inc(narrow.drained[narrow.slot(key)], 1)
                    if h % 2 == 1:
                        key = ("VW", a, h // 2)
                        act.wait_ge(*wide.full(key))
                        evac(VW[:, :, h // 2, :], wide_ps[:, wide.slot(key), :].rearrange("p (b n) -> p b n", b=B), wide, key)

            def attend2(a):
                u0 = base["2a" if a == 0 else "2b"]
                for step in range(-2, NQ):
                    if step >= 0:
                        probs_turned(u0 + step)
                    if step + 2 < NQ:
                        exp(u0 + step + 2, 16 * 65)

            precompute2(0)
            norm_turned(2, "L2_ln1_scale", "L2_ln1_offset")
            attend2(0)
            precompute2(1)
            attend2(1)
            keys_small(3, "L3_k_b")
            norm_turned(4, "L2_ln_mlp_scale", "L2_ln_mlp_offset")
            mlp(1, ACT.Gelu, "L2_b_fc1")
            norm_turned(5, "L3_ln1_w", "L3_ln1_b")
            queries(3, "L3_q_b")
            for step in range(-2, NQ + 2):
                if step >= 2:
                    key = ("ao", 3, step - 2)
                    act.wait_ge(*narrow.full(key))
                    for c in range(NC):
                        evac(qT[:, c, qoff(step - 2)], narrow_ps[:, narrow.slot(key), c * P:(c + 1) * P], narrow, key,
                             bias=column("L3_v_b", c))
                if 0 <= step < NQ:
                    probs_turned(base["3"] + step)
                if step + 2 < NQ:
                    exp(base["3"] + step + 2, 1024)
            norm_turned(6, "L3_ln2_w", "L3_ln2_b")
            mlp(2, ACT.Gelu_apprx_tanh, "L3_fc_b")

        @block.vector
        def _(dve):
            v = nc.vector
            chain = [0]

            def link(ins):
                chain[0] += 1
                ins.then_inc(link_dve, 1)
                dve.wait_ge(link_dve, chain[0])

            def stat(k, q):
                src, eps = NORMS[k]
                link(v.bn_stats(stats[:, q, :], src[:, q, :]))
                link(v.bn_aggr(mv[:, q, :], stats[:, q, :]))
                if k == 0:
                    link(v.scalar_tensor_tensor(out=mv[:, q, 1:2], in0=mv[:, q, 0:1], scalar=mv[:, q, 0:1],
                                                in1=mv[:, q, 1:2], op0=ALU.mult, op1=ALU.add))
                v.tensor_scalar_add(veps[:, q:q + 1], mv[:, q, 1:2], eps).then_inc(stat_ready, 1)

            def norm(k, q):
                src, _ = NORMS[k]
                dve.wait_ge(rstd_ready, k * NQ + q + 1)
                if k == 0:
                    ins = v.tensor_scalar(xn[:, q, :], src[:, q, :], rstd[:, q:q + 1], None, ALU.mult)
                else:
                    ins = v.tensor_scalar(xn[:, q, :], src[:, q, :], mv[:, q, 0:1], rstd[:, q:q + 1],
                                          ALU.subtract, ALU.mult)
                ins.then_inc(xn_ready, 1)

            NORMS = [(xB, 1e-6), (xA, 1e-6), (xB, 1e-5), (xB, 1e-5), (xB, 1e-5), (xB, 1e-5), (xB, 1e-5)]

            def stream_norm(k, q, before, key, dst, n):
                if before is not None and k is not None:
                    norm(k, before)
                if q is not None:
                    add_residual(key, dst, q, n)
                    if k is not None:
                        dve.wait_ge(*narrow.empty(key))
                        stat(k, q)

            def add_residual(key, dst, q, n):
                dve.wait_ge(*narrow.full(key))
                dve.wait_ge(row_added, n * NQ + q + 1)
                v.tensor_tensor(dst[:, q, :], narrow_ps[:, narrow.slot(key), 0:D], dst[:, q, :], ALU.add
                                ).then_inc(narrow.drained[narrow.slot(key)], 1)

            def front(u, n, scale, addend, n_scores, bias=None):
                key = ("S", u)
                dve.wait_ge(*wide.full(key))
                dve.wait_ge(prob_ready, probcount[u - 2])
                s3 = scoresb[:, u % 3, 0:16 * n_scores].rearrange("p (h k) -> p h k", h=16)
                v.scalar_tensor_tensor(out=s3[:, :, 0:T], in0=wide_ps[:, wide.slot(key), :].rearrange("p (h k) -> p h k", h=16),
                                       scalar=scale, in1=addend, op0=ALU.mult, op1=ALU.add
                                       ).then_inc(wide.drained[wide.slot(key)], 1)
                dve.wait_ge(*wide.empty(key))
                if bias:
                    dve.wait_ge(*narrow.empty(bias))
                v.tensor_reduce(mx[:, u % 3, :], s3, AX, ALU.max).then_inc(max_ready, 1)

            def middle(u, n_scores):
                dve.wait_ge(exp_done, shiftcount[u + 1])
                s3 = scoresb[:, u % 3, 0:16 * n_scores].rearrange("p (h k) -> p h k", h=16)
                link(v.tensor_reduce(sums[:, u % 3, :], s3, AX, ALU.add))
                v.reciprocal(rcp[:, u % 3, :], sums[:, u % 3, :]).then_inc(rcp_ready, 1)

            v.memset(colraw[:].rearrange("p a b -> p (a b)"), 0.0).then_inc(cols_zeroed, 1)
            link(v.memset(bvhot[:].rearrange("p a b -> p (a b)"), 0.0))
            dve.wait_ge(load["masks"], 48)
            link(v.tensor_scalar(mask0[:].rearrange("p b k -> p (b k)"), mask0i, 0, NEG0, ALU.is_equal, ALU.mult))
            link(v.tensor_scalar(mask3[:].rearrange("p b k -> p (b k)"), mask3i, 0, NEG3, ALU.is_equal, ALU.mult))

            def values0(b):
                key = ("v0", b)
                dve.wait_ge(*wide.full(key))
                if b < 2:
                    dve.wait_ge(vzero, b + 1)
                vp = vpad0[b % 2]
                ps = wide_ps[:, wide.slot(key), :]
                done = wide.drained[wide.slot(key)]
                for kb in range(2):
                    v.tensor_copy(diagonal(vp, kb * 1024, [(256, 4), (64 + 16, 4), (1, 16)]), ps[:, kb * 256:(kb + 1) * 256].rearrange("p (a h d) -> p a h d", a=4, h=4)
                                  ).then_inc(done, 1)
                for i in range(2):
                    dst = diagonal(vp, 2048 + 16 * i, [(128, 4), (64 + 32, 2), (1, 16)])
                    src = ps[:, 512:768].rearrange("p (a j two d) -> p a j two d", a=4, two=2, d=16)[:, :, :, i, :]
                    v.tensor_copy(dst[64 * i:64 * i + 64], src[64 * i:64 * i + 64]).then_inc(done, 1)

            def front0(u):
                b, q, r = units0[u]
                key = ("S", u)
                dve.wait_ge(*wide.full(key))
                ps = wide_ps[:, wide.slot(key), :].rearrange("p (i n) -> p i n", i=2)
                link(v.tensor_tensor(ps[:, :, S:KEYS0], ps[:, :, S:KEYS0],
                                     mask0[:, b, :].unsqueeze(1).broadcast_to([P, 2, T]), ALU.add))
                if u >= 3:
                    dve.wait_ge(*wide.empty(("S", u - 3)))
                link(v.tensor_reduce(mx[:, u % 3, 4:6], ps[:, :, 0:KEYS0], AX, ALU.max))
                v.tensor_scalar(mx[:, u % 3, 0:2], mx[:, u % 3, 4:6], -1.0 / 16, None, ALU.mult).then_inc(max_ready, 1)

            def middle0(u):
                dve.wait_ge(*wide.empty(("S", u)))
                v.reciprocal(rcp[:, u % 3, 0:2], sums[:, u % 3, 0:2]).then_inc(rcp_ready, 1)

            def spread_keys0(b, c, pair):
                if c == 0 and pair == 0:
                    dve.wait_ge(*wide.empty(("k0", b)))
                v.tensor_tensor(kbd0[b % 2][:, c, 2 * pair:2 * pair + 2],
                                kT2[:, c, :].unsqueeze(1).broadcast_to([P, 2, KEYS0]),
                                head16[:, 2 * pair:2 * pair + 2].unsqueeze(2).broadcast_to([P, 2, KEYS0]), ALU.mult
                                ).then_inc(kbd_ready, 1)

            dve.wait_ge(ctxd_ready, 1)
            for i in range(8):
                spread_keys0(0, i // 4, i % 4)
            values0(0)
            n0 = len(units0)
            for step in range(-2, n0 + 4):
                if 0 <= step < n0:
                    middle0(step)
                if step + 2 < n0:
                    front0(step + 2)
                if 0 <= step < n0 and step % 16 == 4 and step // 16 + 1 < B:
                    values0(step // 16 + 1)
                if 0 <= step < n0 and 5 <= step % 16 < 13 and step // 16 + 1 < B:
                    i = step % 16 - 5
                    spread_keys0(step // 16 + 1, i // 4, i % 4)
                q = done0(step)
                stream_norm(0, q, done0(step - 1), ("proj", 0, q), xB, 0)
            dve.wait_ge(*wide.empty("cols"))
            for q in range(NQ):
                add_residual(("down", 0, q), xA, q, 1)

            dve.wait_ge(*wide.full(("v", 1)))
            dve.wait_ge(vzero, 3)
            ps = wide_ps[:, wide.slot(("v", 1)), :]
            for b in range(B):
                for c in range(NC):
                    for i in range(2):
                        dst = diagonal(region, b * 2048 + c * 1024 + 8 * i, [(288, 4), (144, 2), (1, 8)])
                        src = ps[:, b * 64 + c * 32:b * 64 + (c + 1) * 32].rearrange("p (k d) -> p k d", d=8).unsqueeze(2).broadcast_to([P, 4, 2, 8])
                        v.tensor_copy(dst[64 * i:64 * i + 64], src[64 * i:64 * i + 64]
                                      ).then_inc(wide.drained[wide.slot(("v", 1))], 1)
            n1 = len(units1)
            for step in range(-2, n1 + 4):
                if 0 <= step < n1:
                    middle(base["1"] + step, T)
                if step + 2 < n1:
                    q, c = units1[step + 2]
                    front(base["1"] + step + 2, 1024, 8 ** -0.5,
                          mask1[:, q, :].unsqueeze(1).broadcast_to([P, 16, T]), T)
                q = done1(step)
                stream_norm(1, q, done1(step - 1), ("proj", 1, q), xA, 2)

            def head2(a, h):
                key = ("kvq", a, h)
                dve.wait_ge(*wide.full(key))
                ps = wide_ps[:, wide.slot(key), :]
                v.tensor_copy(heads[:, h % 2, 513:769], ps[:, 512:768]).then_inc(wide.drained[wide.slot(key)], 1)
                v.tensor_tensor(vwb[:, :], ps[0:16, 768:1024], vwb[:, :], ALU.add
                                ).then_inc(wide.drained[wide.slot(key)], 1)

            def precompute2(a):
                v.tensor_copy(diagonal(bvhot, 0, [(17, 16)], 256),
                              colrange(f"L2_bias_v{a + 1}")).then_inc(hot_ready, 1)
                link(v.memset(vwb[:], 0.0))
                head2(a, 0)
                for h in range(H2):
                    if h + 1 < H2:
                        dve.wait_ge(*wide.empty(("kvq", a, h)))
                        head2(a, h + 1)
                    key = ("G", a, h)
                    dve.wait_ge(*wide.full(key))
                    v.tensor_copy(G[:, :, h, :], wide_ps[:, wide.slot(key), :].rearrange("p (c n) -> p c n", c=NC)[:, :, 0:NK2]
                                  ).then_inc(wide.drained[wide.slot(key)], 1)
                    if a == 0 and h >= 8:
                        dve.wait_ge(x2_ready, h - 7)
                        stat(2, h - 8)
                        if h >= 9:
                            norm(2, h - 9)
                if a == 0:
                    norm(2, NQ - 1)

            def attend2(a, rows_before):
                u0 = base["2a" if a == 0 else "2b"]
                for step in range(-2, NQ + 3):
                    if step == -2:
                        for h in range(H2 - 2, H2):
                            dve.wait_ge(*narrow.empty(("cB", a, h)))
                    if step - 1 < NQ:
                        key = ("X", a, step - 1)
                        dve.wait_ge(*narrow.full(key))
                        ps = narrow_ps[:, narrow.slot(key), :]
                        if step + 2 < NQ:
                            u = u0 + step + 2
                            dve.wait_ge(prob_ready, probcount[u - 2])
                            v.scalar_tensor_tensor(out=scoresb[:, u % 3, 0:16 * 65].rearrange("p (h k) -> p h k", h=16)[:, :, T],
                                                   in0=ps[:, 0:16], scalar=DH2 ** -0.5, in1=cB[:, :, NK2 - 1],
                                                   op0=ALU.mult, op1=ALU.add).then_inc(narrow.drained[narrow.slot(key)], 1)
                        if step - 1 >= 0:
                            v.tensor_copy(probsbT[:, (u0 + step - 1) % 2, :], ps[0:16, P:2 * P]
                                          ).then_inc(narrow.drained[narrow.slot(key)], 1)
                    if 0 <= step < NQ:
                        middle(u0 + step, 65)
                    if step + 2 < NQ:
                        q = step + 2
                        b = q // 2
                        front(u0 + q, 1024, DH2 ** -0.5, cB[:, :, b * T:(b + 1) * T], 65, ("X", a, step - 1))
                    q = done2(step)
                    stream_norm(3 + a, q, done2(step - 1), ("proj", 2 + a, q), xB, rows_before)

            precompute2(0)
            attend2(0, 3)
            precompute2(1)
            attend2(1, 4)

            dve.wait_ge(*wide.full(("v", 3)))
            dve.wait_ge(vzero, 4)
            ps = wide_ps[:, wide.slot(("v", 3)), :]
            for b in range(B):
                for i in range(2):
                    dst = diagonal(region, 12288 + b * 1024 + 16 * i, [(512, NC), (P + 32, 4), (1, 16)])
                    src = ps[:, b * 256:(b + 1) * 256].rearrange("p (c j two d) -> p c j two d", c=NC, two=2, d=16)[:, :, :, i, :]
                    v.tensor_copy(dst[64 * i:64 * i + 64], src[64 * i:64 * i + 64]
                                  ).then_inc(wide.drained[wide.slot(("v", 3))], 1)
            for q in range(NQ):
                stream_norm(5, q, q - 1 if q else None, ("down", 1, q), xB, 5)
            norm(5, NQ - 1)
            for step in range(-2, NQ + 4):
                if 0 <= step < NQ:
                    middle(base["3"] + step, T)
                if step + 2 < NQ:
                    q = step + 2
                    front(base["3"] + q, 1024, 0.25, mask3[:, q // 2, :].unsqueeze(1).broadcast_to([P, 16, T]), T)
                q = done3(step)
                stream_norm(6, q, done3(step - 1), ("proj", 4, q), xB, 6)
            for q in range(NQ):
                add_residual(("down", 2, q), xB, q, 7)

        @block.gpsimd
        def _(pool):
            g = nc.gpsimd
            chain = [0]

            def link(ins):
                chain[0] += 1
                ins.then_inc(link_pool, 1)
                pool.wait_ge(link_pool, chain[0])

            def head_mask(tile, width, heads_):
                link(g.memset(tile[:], 1.0))
                link(g.affine_select(out=tile[:], in_=tile[:], compare_op=ALU.is_ge, fill=0.0, base=0,
                                     pattern=[[-width, heads_]], channel_multiplier=1))
                link(g.affine_select(out=tile[:], in_=tile[:], compare_op=ALU.is_ge, fill=0.0, base=width - 1,
                                     pattern=[[width, heads_]], channel_multiplier=-1))

            def add_row(q, dst, src, name):
                g.tensor_tensor(dst[:, q, :], src[:, q, :], row(name), ALU.add).then_inc(row_added, 1)

            def rstd_of(k, q):
                pool.wait_ge(stat_ready, k * NQ + q + 1)
                g.tensor_tensor(rstd[:, q:q + 1], veps[:, q:q + 1], mhalf[:], ALU.pow).then_inc(rstd_ready, 1)

            def stream_norm(k, q, before, name):
                if q is not None:
                    rstd_of(k, q)
                if before is not None and name:
                    pool.wait_ge(xn_ready, k * NQ + before + 1)
                    add_row(before, xB, xB, name)

            def shift(u, n_scores):
                pool.wait_ge(max_ready, u + 1)
                s3 = scoresb[:, u % 3, 0:16 * n_scores].rearrange("p (h k) -> p h k", h=16)
                g.tensor_tensor(s3, s3, mx[:, u % 3, :].unsqueeze(2).broadcast_to([P, 16, n_scores]), ALU.subtract
                                ).then_inc(shifted, 1)

            def normalize(u, n_scores):
                pool.wait_ge(rcp_ready, u + 1)
                pool.wait_ge(*wide.full(("T", u - 2)))
                s3 = scoresb[:, u % 3, 0:16 * n_scores].rearrange("p (h k) -> p h k", h=16)
                g.tensor_tensor(probs[:, u % 2, :].rearrange("p (h k) -> p h k", h=16), s3[:, :, 0:T],
                                rcp[:, u % 3, :].unsqueeze(2).broadcast_to([P, 16, T]), ALU.mult).then_inc(prob_ready, 1)
                if n_scores > T:
                    g.tensor_tensor(probsb[:, u % 2, :], s3[:, :, T], rcp[:, u % 3, :], ALU.mult).then_inc(prob_ready, 1)

            def normalize0(u):
                pool.wait_ge(rcp_ready, u + 1)
                if u >= 2:
                    pool.wait_ge(*wide.full(("T", u - 2)))
                s3 = scoresb[:, u % 3, 0:2 * KEYS0].rearrange("p (i k) -> p i k", i=2)
                for lo, hi, o in ((0, S, 0), (S, KEYS0, 2 * S)):
                    n = hi - lo
                    g.tensor_tensor(probs[:, u % 2, o:o + 2 * n].rearrange("p (i k) -> p i k", i=2), s3[:, :, lo:hi],
                                    rcp[:, u % 3, 0:2].unsqueeze(2).broadcast_to([P, 2, n]), ALU.mult).then_inc(prob_ready, 1)

            def spread_keys(layer, kbd, mask, heads_):
                pool.wait_ge(*wide.empty(("k", layer)))
                for c in range(NC):
                    g.tensor_tensor(kbd[:, c],
                                    kT2[:, c, 0:256].rearrange("p (b k) -> p b k", b=B).unsqueeze(2).broadcast_to([P, B, heads_, T]),
                                    mask[:].unsqueeze(1).unsqueeze(3).broadcast_to([P, B, heads_, T]), ALU.mult
                                    ).then_inc(kbd_ready, 1)

            link(g.memset(ident[:], 0.0))
            g.affine_select(out=ident[:], in_=ident[:], compare_op=ALU.not_equal, fill=1.0, base=0,
                            pattern=[[-1, P]], channel_multiplier=1).then_inc(consts, 1)
            link(g.memset(mhalf[:], -0.5))
            head_mask(head16, 16, 8)
            head_mask(head8, 8, 16)
            pool.wait_ge(*wide.empty("ctxT"))
            g.tensor_copy(ctxD[:].rearrange("p c b a k -> p (c b) a k"),
                          ctxT[:].rearrange("p c (b k) -> p (c b) k", b=B).unsqueeze(2).broadcast_to([P, NC * B, 2, T])
                          ).then_inc(ctxd_ready, 1)
            for i in range(2):
                g.memset(vpad0[i], 0.0).then_inc(vzero, 1)
            pool.wait_ge(load["rows"], 16 * len(ROWS))
            pool.wait_ge(load["x"], 16)
            for q in range(NQ):
                add_row(q, xB, xA, "L0_out_b")
            pool.wait_ge(load["w1"], 64)
            for kc in range(NC):
                g.tensor_copy(wkrep[:, kc].rearrange("p c (k r d) -> p (c k) r d", r=4, d=8),
                              k_w1[:, kc].rearrange("p (k d) -> p k d", d=8).unsqueeze(2).broadcast_to([P, 8, 4, 8])
                              ).then_inc(wk_ready, 1)
            for step in range(len(units0) + 4):
                if step < len(units0):
                    normalize0(step)
                if step == 0:
                    pool.wait_ge(*wide.full(("x0T", 1)))
                    pool.wait_ge(row_added, NQ)
                    for q in range(NQ):
                        add_row(q, xA, xA, "L0_mlp_b2")
                stream_norm(0, done0(step), None, None)
            spread_keys(1, kbd1, head8, 16)
            pool.wait_ge(*narrow.full(("down", 0, NQ - 1)))
            g.memset(region[:, 0:8192], 0.0).then_inc(vzero, 1)
            pool.wait_ge(*wide.full(("x1T", 1)))
            for q in range(NQ):
                add_row(q, xA, xA, "L1_bo")

            def attend(first, n, n_scores, k, done, name):
                for step in range(-2, n + 4):
                    if 0 <= step < n:
                        normalize(first + step, n_scores)
                    if step + 2 < n:
                        shift(first + step + 2, n_scores)
                    stream_norm(k, done(step), done(step - 1), name)

            attend(base["1"], len(units1), T, 1, done1, None)
            for q in range(NQ):
                pool.wait_ge(xn_ready, NQ + q + 1)
                link(g.tensor_tensor(xn[:, q, :], xn[:, q, :], row("L1_gamma"), ALU.mult))
                g.tensor_tensor(xB[:, q, :], xn[:, q, :], row("L1_beta"), ALU.add).then_inc(x2_ready, 1)
            for q in range(NQ + 1):
                stream_norm(2, q if q < NQ else None, q - 1 if q else None, "L2_bo1")
            attend(base["2a"], NQ, 65, 3, done2, "L2_bo2")
            attend(base["2b"], NQ, 65, 4, done2, "L2_b_fc2")
            pool.wait_ge(*narrow.full(("proj", 3, NQ - 1)))
            g.memset(region[:, 12288:16384], 0.0).then_inc(vzero, 1)
            spread_keys(3, kbd3, head16, 8)
            for q in range(NQ + 1):
                stream_norm(5, q if q < NQ else None, q - 1 if q else None, "L3_cproj_b")
            attend(base["3"], NQ, T, 6, done3, "L3_proj_b")


def kernel(**inputs):
    import numpy as np
    import concourse.bacc as bacc
    from concourse.bass_utils import run_bass_kernel_spmd

    nc = bacc.Bacc("TRN2", target_bir_lowering=False, num_devices=1)
    arrays, args = {}, {}
    for name, value in inputs.items():
        a = np.ascontiguousarray(value)
        if a.dtype == np.bool_:
            a = a.view(np.uint8)
        arrays["in_" + name] = a
        args[name] = nc.dram_tensor("in_" + name, a.shape, mybir.dt.from_np(a.dtype), kind="ExternalInput").ap()
    out = nc.dram_tensor("out", (B, S, D), F32, kind="ExternalOutput").ap()
    build(nc, args, out)
    r = run_bass_kernel_spmd(nc, [arrays], core_ids=[0])
    return r.results[0]["out"]
```

```python
from contextlib import ExitStack

import concourse.bass as bass
from concourse import mybir

P = 128
B, S, D, T = 4, 256, 256, 64
NQ = B * S // P
NC = D // P
F = 4 * D
NF = F // P
H0 = 16
H2, DH2 = 16, 128
NK2 = B * T + 1
KEYS0 = S + T
GROUP = 4
DIRECT = 4
TURN_AT = ((10, 14), (4, 6))
NEG0 = -1.0e30
NEG3 = -3.4028234663852886e38
SCORES, TURNS = (0, 1), (2,)
ATTENDED, SIDE = (0,), (1,)
ALU = mybir.AluOpType
ACT = mybir.ActivationFunctionType
AX = mybir.AxisListType.X
F32 = mybir.dt.float32
F32R = mybir.dt.float32r
I32 = mybir.dt.int32
U8 = mybir.dt.uint8

COLUMNS = [
    ("L0_q_b", 2), ("L0_k_b", 2), ("L0_v_b", 2), ("L0_postnorm_w", 2), ("L0_mlp_b1", 8),
    ("L1_bq", 2), ("L1_bk", 2), ("L1_bv", 2),
    ("L2_ln1_scale", 2), ("L2_ln1_offset", 2), ("L2_bq1", 16), ("L2_bk1", 16), ("L2_bv1", 16),
    ("L2_bias_k1", 16), ("L2_bias_v1", 16),
    ("L2_ln2_scale", 2), ("L2_ln2_offset", 2), ("L2_bq2", 16), ("L2_bk2", 16), ("L2_bv2", 16),
    ("L2_bias_k2", 16), ("L2_bias_v2", 16), ("L2_ln_mlp_scale", 2), ("L2_ln_mlp_offset", 2),
    ("L2_b_fc1", 8),
    ("L3_ln1_w", 2), ("L3_ln1_b", 2), ("L3_q_b", 2), ("L3_k_b", 2), ("L3_v_b", 2),
    ("L3_ln2_w", 2), ("L3_ln2_b", 2), ("L3_fc_b", 8),
]
ROWS = ["L0_out_b", "L0_mlp_b2", "L1_bo", "L1_gamma", "L1_beta", "L2_bo1", "L2_bo2", "L2_b_fc2",
        "L3_cproj_b", "L3_proj_b"]


class Ring:

    def __init__(self, filled, drained):
        self.filled, self.drained = filled, drained
        self.uses = [0] * len(filled)
        self.owed = [0] * len(filled)
        self.order = list(range(len(filled)))
        self.tiles = {}

    def take(self, key, drains=1, among=(0, 1, 2)):
        s = next(x for x in self.order if x in among)
        before = self.owed[s]
        self.order.remove(s)
        self.order.append(s)
        self.uses[s] += 1
        self.owed[s] += drains
        self.tiles[key] = (s, self.uses[s], self.owed[s])
        return s, before

    def slot(self, key):
        return self.tiles[key][0]

    def full(self, key):
        s, n, _ = self.tiles[key]
        return self.filled[s], n

    def empty(self, key):
        s, _, n = self.tiles[key]
        return self.drained[s], n


def build(nc, t, out):
    ctx = ExitStack()
    with ctx:
        def sb(name, shape, dt=F32):
            return ctx.enter_context(nc.sbuf_tensor(name, shape, dt))

        def sem(name):
            return ctx.enter_context(nc.semaphore(name))

        wide_ps = ctx.enter_context(nc.psum_tensor("wide_ps", [P, 3, 1024], F32))
        narrow_ps = ctx.enter_context(nc.psum_tensor("narrow_ps", [P, 2, 512], F32))
        wide = Ring([sem(f"wide{i}_filled") for i in range(3)], [sem(f"wide{i}_drained") for i in range(3)])
        narrow = Ring([sem(f"narrow{i}_filled") for i in range(2)], [sem(f"narrow{i}_drained") for i in range(2)])

        ident = sb("ident", [P, P])
        head16 = sb("head16", [P, 8])
        head8 = sb("head8", [P, 16])
        mhalf = sb("mhalf", [P, 1])
        col = sb("col", [P, 3, P])
        rows = sb("rows", [P, len(ROWS), D])
        mask0 = sb("mask0", [P, B, T])
        mask1 = sb("mask1", [P, NQ, T])
        mask3 = sb("mask3", [P, B, T])
        xB = sb("xB", [P, NQ, D])
        xn = sb("xn", [P, NQ, D])
        ctxT = sb("ctxT", [P, NC, B * T])
        ctxD = sb("ctxD", [P, NC, B, 2, T])
        stats = sb("stats", [P, NQ, 6])
        mv = sb("mv", [P, NQ, 2])
        veps = sb("veps", [P, NQ])
        rstd = sb("rstd", [P, NQ])
        probsb = sb("probsb", [P, 2, 16])
        probsT = sb("probsT", [P, 2, 1024])
        probsbT = sb("probsbT", [16, 2, P])
        mx = sb("mx", [P, 3, 16])
        negmx = sb("negmx", [P, 3, DIRECT])
        sums = sb("sums", [P, 3, 16])
        rcp = sb("rcp", [P, 3, 16])
        wsmall = sb("wsmall", [P, 2048])
        colraw = wsmall[:, 1280:1664].rearrange("p (a n) -> p a n", a=3)
        wkrep = sb("wkrep", [P, NC, NC, P])
        bvhot = sb("bvhot", [P, H2, H2])
        vwb = sb("vwb", [16, D])
        headbuf = sb("headbuf", [P, 1568])
        heads = headbuf[:].rearrange("p (a n) -> p a n", a=2)
        kT2 = headbuf[:, 0:NC * B * T].rearrange("p (c n) -> p c n", c=NC)
        with ExitStack() as twins:
            def twin(name, shape):
                return twins.enter_context(nc.sbuf_tensor(name, shape, F32R))

            xq_r = twin("xq_r", [P, 4112])
            actT_r = twin("actT_r", [P, NC, B * S])
            wstream_r = twin("wstream_r", [P, 8192])
            scoresb_r = twin("scoresb_r", [P, 3, 16 * 65])
            probs_r = twin("probs_r", [P, 2, 1024])
            hidden = twin("hidden", [P, 2, NF, 512])
        xq = sb("xq", [P, 4112])
        xA = xq[:, 2064:4112].rearrange("p (q d) -> p q d", q=NQ)
        qT = xq[:, 0:2048].rearrange("p (c n) -> p c n", c=NC)
        actT = sb("actT", [P, NC, B * S])
        wstream = sb("wstream", [P, 8192])
        scoresb = sb("scoresb", [P, 3, 16 * 65])
        probs = sb("probs", [P, 2, 1024])
        mask0i = probs[:, 0, 0:B * T].bitcast(I32)
        mask3i = probs[:, 0, B * T:B * T + B * T // 4].bitcast(U8)
        xparts = [xq_r[:, 0:2048].rearrange("p (c n) -> p c n", c=NC), actT_r]
        with ExitStack() as first:
            def sb0(name, shape, dt=F32R):
                return first.enter_context(nc.sbuf_tensor(name, shape, dt))

            place = sb0("place", [P, 4, 4 * P])
            qparts = sb0("qparts", [P, 2, NC, S])
            kparts = sb0("kparts", [P, 2, NC, KEYS0])
            qhot = sb0("qhot", [P, H0 // 2, 2, S])
            kpair = sb0("kpair", [P, H0 // 2, KEYS0])
            vpad_mem = sb0("vpad0", [P, 2, 2560], F32)
            vpad0 = [vpad_mem[:, i, :] for i in range(2)]
        region = sb("region", [P, 16416])

        w0 = wstream
        q_w0 = w0[:, 0:512].rearrange("p (c n) -> p c n", c=NC)
        kv_w0 = w0[:, 512:1536].rearrange("p (c n two) -> p c two n", c=NC, two=2)
        out_w0 = w0[:, 1536:2048].rearrange("p (c n) -> p c n", c=NC)
        MLP_LOW = [(2048, 4096), (0, 2048), (0, 2048)]
        MLP_HIGH = [(6144, 0), (4096, 6144), (4096, 6144)]

        def mlp_load(n, which):
            return wstream[:, MLP_LOW[n][which]:MLP_LOW[n][which] + 2048].rearrange("p (c n) -> p c n", c=(NC, NF)[which])

        def mlp_parts(n, which):
            return [wstream_r[:, at[n][which]:at[n][which] + 2048].rearrange("p (c n) -> p c n", c=(NC, NF)[which])
                    for at in (MLP_HIGH, MLP_LOW)]

        def mlp_high(copy, n, chunk):
            which, o = chunk // 2, chunk % 2 * 1024
            high, low = MLP_HIGH[n][which] + o, MLP_LOW[n][which] + o
            return copy(wstream_r[:, high:high + 1024], wstream[:, low:low + 1024])

        def mlp_low(engine, n, chunk):
            which, o = chunk // 2, chunk % 2 * 1024
            high, low = MLP_HIGH[n][which] + o, MLP_LOW[n][which] + o
            return engine.tensor_tensor(wstream_r[:, low:low + 1024], wstream[:, low:low + 1024],
                                        wstream_r[:, high:high + 1024].bitcast(F32), ALU.subtract)

        q_w1 = wsmall[:, 0:512].rearrange("p (c n) -> p c n", c=NC)
        k_w1 = wsmall[:, 512:640].rearrange("p (c n) -> p c n", c=NC)
        v_w1 = wsmall[:, 640:768].rearrange("p (c n) -> p c n", c=NC)
        out_w1 = wsmall[:, 768:1280].rearrange("p (c n) -> p c n", c=NC)
        vpad1 = region[:, 0:2048].rearrange("p (b r n) -> p b r n", b=B, r=16)
        kbd1 = region[:, 8192:16384].rearrange("p (c b h k) -> p c b h k", c=NC, b=B, h=16)
        G = region[:, 0:NC * H2 * NK2].rearrange("p (c h k) -> p c h k", c=NC, h=H2)
        VW = region[:, 8224:8224 + 8192].rearrange("p (b r n) -> p b r n", b=B, r=8)
        cB = xq[:, 0:H2 * NK2].rearrange("p (h k) -> p h k", h=H2)
        wring = [wstream[:, i * 4096:(i + 1) * 4096].rearrange("p (m n) -> p m n", m=4) for i in range(2)]
        cparts = scoresb_r[:].rearrange("p a n -> p (a n)")[:, 0:1024].rearrange("p (part c n) -> p part c n", part=2, c=NC)

        def kv_weights(a, h):
            g, o = 4 * a + h // GROUP, h % GROUP * P
            at = [w[:, g % 2 * 4096 + 1024:g % 2 * 4096 + 3072].rearrange("p (m c n) -> p m c n", m=2, c=NC)[:, :, :, o:o + P]
                  for w in (wstream, wstream_r)]
            high = probs_r[:, h % 2, 0:512].rearrange("p (m c n) -> p m c n", m=2, c=NC)
            return at[0], high, at[1]

        w3 = [wsmall[:, i * 512:(i + 1) * 512].rearrange("p (c n) -> p c n", c=NC) for i in range(4)]
        kbd3 = region[:, 8192:12288].rearrange("p (c b h k) -> p c b h k", c=NC, b=B, h=8)
        vpad3 = region[:, 12288:13312].rearrange("p (b r n) -> p b r n", b=B, r=8)

        load = {k: sem("loaded_" + k) for k in
                ("x", "ctx", "cols0", "cols", "rows", "masks", "w0", "mlp0", "w1", "w3", "mlp2", "mlp3")}
        ring_loaded = [sem("ring0_loaded"), sem("ring1_loaded")]
        consts = sem("consts_ready")
        link_dve = sem("dve_step")
        link_pool = sem("pool_step")
        cols_zeroed = sem("cols_zeroed")
        stat_ready = sem("stat_ready")
        rstd_ready = sem("rstd_ready")
        xn_ready = sem("xn_ready")
        x2_ready = sem("x2_ready")
        placed = sem("placement_ready")
        x_split = sem("mlp_input_split")
        w_high = sem("mlp_weights_high")
        w_split = sem("mlp_weights_split")
        hidden_split = sem("hidden_split")
        row_added = sem("row_added")
        vzero = sem("vpad_zeroed")
        kbd_ready = sem("kbd_ready")
        wk_ready = sem("wk_replicated")
        ctxd_ready = sem("ctx_doubled")
        max_ready = sem("max_ready")
        shifted = sem("scores_shifted")
        exp_done = sem("exp_done")
        rcp_ready = sem("rcp_ready")
        prob_ready = sem("probs_normalized")
        bias_key = sem("bias_key_copied")
        hot_ready = sem("bias_values_spread")
        ctx_split = sem("context_split")
        kv_high = sem("kv_weights_high")
        kv_split = sem("kv_weights_split")
        stored = sem("out_stored")

        colrow = {}
        n = 0
        for name, k in COLUMNS:
            if n // P != (n + k - 1) // P or name == "L1_bq":
                n = -(-n // P) * P
            colrow[name] = (n, k)
            n += k

        def column(name, i=0):
            r = colrow[name][0] + i
            return col[:, r // P, r % P:r % P + 1]

        def row(name):
            i = ROWS.index(name)
            return rows[:, i, :]

        units0 = [(b, r, q) for b in range(B) for r in range(H0 // 2) for q in range(2)]
        units1 = [(q, c) for q in range(NQ) for c in range(NC)]
        units2 = [(q,) for q in range(NQ)]
        units3 = [(q,) for q in range(NQ)]
        base = {}
        probcount = [0]
        shiftcount = [0]
        at = 0
        LOADS = {"cols0": 5, "cols": len(COLUMNS) - 5 + 2}
        for name, us in (("0", units0), ("1", units1), ("2a", units2), ("2b", units2), ("3", units3)):
            base[name] = at
            at += len(us)
            for _ in us:
                probcount.append(probcount[-1] + (1 if name in "13" else 2))
                shiftcount.append(shiftcount[-1] + (name != "0"))

        def done0(step):
            b, s = divmod(step - 16, 16)
            return 2 * b + s - 2 if b >= 0 and 2 <= s <= 3 else None

        SIDE0 = [("q",), ("proj", 0), ("proj", 1), ("k", 0), ("k", 1), ("qhot", 0), ("qhot", 1), ("kpair", 0),
                 ("kpair", 1), ("qhot", 2), ("kpair", 2), ("kpair", 3), ("qhot", 3), ("kpair", 4), ("v", 0), ("v", 1)]
        START0 = [[("q",), ("k", 0), ("qhot", 0), ("kpair", 0), ("kpair", 1)],
                  [("v", 0), ("v", 1), ("k", 1), ("qhot", 1), ("kpair", 2), ("kpair", 3), ("qhot", 2), ("qhot", 3),
                   ("kpair", 4)]]

        def side0(step):
            if step < 0:
                return None, None
            b, s = divmod(step, 16)
            job = SIDE0[s]
            if job[0] == "proj":
                return (job, b - 1) if b else (None, None)
            return (job, b + 1) if b + 1 < B else (None, None)

        def done1(step):
            return units1[step - 3][0] if 0 <= step - 3 < len(units1) and units1[step - 3][1] == 1 else None

        def done2(step):
            return step - 2 if 0 <= step - 2 < NQ else None

        def done3(step):
            return step - 3 if 0 <= step - 3 < NQ else None

        qoff = lambda q: slice(q * P, (q + 1) * P)

        def diagonal(tile, offset, dims, width=None):
            a = tile[:, offset:offset + 1] if len(tile.shape) == 2 else tile[:].rearrange("p a b -> p (a b)")[:, offset:offset + 1]
            return bass.AP(tensor=a.tensor, offset=a.offset, ap=[list(a.ap[0])] + [list(d) for d in dims])

        def colrange(name):
            r, k = colrow[name]
            return col[:, r // P, r % P:r % P + k]

        def parameter_rows(first):
            loads = []
            for name, k in COLUMNS:
                r, _ = colrow[name]
                dst = colraw[r % P:r % P + k, r // P, :]
                key = name[:3] + "xattn_" + name[3:]
                if (name[:2] == "L0") != first:
                    continue
                if name in ("L0_k_b", "L0_v_b"):
                    src = t["L0_xattn_kv_b"].rearrange("(r p two) -> two r p", r=2, two=2)[int(name == "L0_v_b")]
                    loads.append((dst, src, True))
                elif name in ("L1_bk", "L1_bv"):
                    for c in range(NC):
                        src = t[key].rearrange("(k d) -> k d", d=8)[4 * c:4 * c + 4].unsqueeze(1).broadcast_to([4, 4, 8]).unsqueeze(0)
                        loads.append((colraw[r % P + c:r % P + c + 1, r // P, :].rearrange("p (a b c) -> p a b c", a=4, b=4),
                                      src, False))
                elif "bias_" in name:
                    loads.append((dst, t[key].rearrange("a b h d -> (a b h) d"), False))
                else:
                    loads.append((dst, t[key].rearrange("(r p) -> r p", p=P), False))
            return loads

        block = ctx.enter_context(nc.Block())

        @block.tensor
        def _(pe):
            mm = nc.tensor.matmul

            def take_wide(key, drains=1, among=(0, 1, 2)):
                s, before = wide.take(key, drains, among)
                if before:
                    pe.wait_ge(wide.drained[s], before)
                return wide_ps[:, s, :], wide.filled[s]

            def take_narrow(key, drains=1, among=(0, 1)):
                s, before = narrow.take(key, drains, among)
                if before:
                    pe.wait_ge(narrow.drained[s], before)
                return narrow_ps[:, s, :], narrow.filled[s]

            def turn(key, src, ready=None, drains=1, halves=(0, 1), among=(0, 1, 2)):
                for half in halves:
                    ps, filled = take_wide((key, half), drains, among)
                    for j in range(4):
                        q = 4 * half + j
                        if ready:
                            ready(q)
                        for c in range(NC):
                            m = nc.tensor.transpose(ps[:, c * 512 + j * P:c * 512 + (j + 1) * P],
                                                    src[:, q, c * P:(c + 1) * P], ident[:])
                    m.then_inc(filled, 1)

            def norm_turn(k, halves=(0, 1), among=(0, 1, 2)):
                turn(("ln", k), xn, lambda q: pe.wait_ge(xn_ready, k * NQ + q + 1), 2, halves, among)

            def queries(layer, w, src_key):
                for c in range(NC):
                    ps, filled = take_wide(("q", layer, c))
                    for half in range(2):
                        pe.wait_ge(*wide.empty((src_key, half)))
                        for kc in range(NC):
                            m = mm(ps[:, half * 512:(half + 1) * 512], w[:, kc, c * P:(c + 1) * P],
                                   actT[:, kc, half * 512:(half + 1) * 512], start=kc == 0, stop=kc == NC - 1)
                    m.then_inc(filled, 1)

            PARTS = ((0, 0), (1, 0), (0, 1))

            def mlp(n):
                w1, w2 = mlp_parts(n, 0), mlp_parts(n, 1)

                def up(half, fp):
                    ps, filled = take_wide(("up", n, half, fp), 2)
                    pe.wait_ge(x_split, 2 * (2 * n + half) + 1)
                    if half == 0 and fp == 0:
                        pe.wait_ge(w_split, 4 * n + 2)
                    for j in range(2):
                        f = 2 * fp + j
                        for kc in range(NC):
                            for i, (pw, px) in enumerate(PARTS):
                                if fp == 0 and j == 0 and kc == 0 and px == 1:
                                    pe.wait_ge(x_split, 2 * (2 * n + half) + 2)
                                m = mm(ps[:, j * 512:(j + 1) * 512], w1[pw][:, kc, f * P:(f + 1) * P],
                                       xparts[px][:, kc, half * 512:(half + 1) * 512],
                                       start=kc == 0 and i == 0, stop=kc == NC - 1 and i == 2)
                    m.then_inc(filled, 1)

                def down(q):
                    tiles = []
                    if q == 0:
                        pe.wait_ge(w_split, 4 * n + 4)
                    for fs in (range(NF - 2), range(NF - 2, NF)):
                        for i in range(2):
                            if 0 in fs:
                                tiles.append(take_narrow(("down", n, q + i)))
                            ps, filled = tiles[i]
                            for f in fs:
                                if q % 4 == 0 and f % 2 == 0 and i == 0:
                                    pe.wait_ge(hidden_split, 8 * n + 4 * (q // 4) + f // 2 + 1)
                                for part, (pw, ph) in enumerate(PARTS):
                                    m = mm(ps[:, 0:D], hidden[:, ph, f, qoff((q + i) % 4)], w2[pw][:, f, :],
                                           start=f == 0 and part == 0, stop=f == NF - 1 and part == 2)
                            if NF - 1 in fs:
                                m.then_inc(filled, 1)

                for fp in range(NF // 2):
                    up(0, fp)
                up(1, 0)
                for q in range(0, NQ // 2, 2):
                    down(q)
                for fp in range(1, NF // 2):
                    up(1, fp)
                for q in range(NQ // 2, NQ, 2):
                    down(q)

            def project(layer, q, w, aokeys):
                ps, filled = take_narrow(("proj", layer, q))
                for key in aokeys:
                    pe.wait_ge(*narrow.empty(key))
                for c in range(NC):
                    m = mm(ps[:, 0:D], qT[:, c, qoff(q)], w[:, c, :], start=c == 0, stop=c == NC - 1)
                m.then_inc(filled, 1)

            def turn_probs(u):
                ps, filled = take_wide(("T", u), among=TURNS)
                pe.wait_ge(prob_ready, probcount[u + 1])
                n = 5 if u < len(units0) else 8
                for j in range(n):
                    m = nc.tensor.transpose(ps[:, j * P:(j + 1) * P], probs[:, u % 2, j * P:(j + 1) * P], ident[:])
                m.then_inc(filled, 1)

            def values_small(layer, wv, nv):
                ps, filled = take_wide(("v", layer), 16 if layer == 1 else 8)
                for b in range(B):
                    for kc in range(NC):
                        m = mm(ps[:, b * nv:(b + 1) * nv], ctxD[:, kc, b, :, :].rearrange("p a k -> p (a k)"),
                               wv[:, kc, :], start=kc == 0, stop=kc == NC - 1)
                m.then_inc(filled, 1)

            def keys_small(layer, wk):
                ps, filled = take_wide(("k", layer), 2)
                for c in range(NC):
                    for kc in range(NC):
                        m = mm(ps[:, c * 256:(c + 1) * 256], wk(kc, c), ctxT[:, kc, :], start=kc == 0, stop=kc == NC - 1)
                m.then_inc(filled, 1)

            pe.wait_ge(consts, 1)
            pe.wait_ge(load["x"], 16)
            turn("x0T", xA)
            pe.wait_ge(load["ctx"], 16)
            ps, filled = take_wide("ctxT")
            for c in range(NC):
                for j in range(2):
                    m = nc.tensor.transpose(ps[:, c * 256 + j * P:c * 256 + (j + 1) * P],
                                            xn[:, j, c * P:(c + 1) * P], ident[:])
            m.then_inc(filled, 1)

            pe.wait_ge(load["cols0"], 16 * LOADS["cols0"])
            ps, filled = take_wide("cols0")
            nc.tensor.transpose(ps[:, 0:P], colraw[:, 0, :], ident[:]).then_inc(filled, 1)

            pe.wait_ge(load["w0"], 16 * 3)
            pe.wait_ge(*wide.empty("ctxT"))

            def side_product0(job, b, among):
                kind = job[0]
                if kind == "proj":
                    q = 2 * b + job[1]
                    ps, filled = take_narrow(("proj", 0, q), among=among)
                    for c in range(NC):
                        pe.wait_ge(*narrow.empty(("ao", 0, b, c)))
                    for c in range(NC):
                        m = mm(ps[:, 0:D], qT[:, c, qoff(q)], out_w0[:, c, :], start=c == 0, stop=c == NC - 1)
                elif kind == "q":
                    ps, filled = take_narrow((job, b), 4, among)
                    pe.wait_ge(*wide.empty(("x0T", b // 2)))
                    for c in range(NC):
                        for kc in range(NC):
                            m = mm(ps[:, c * S:(c + 1) * S], q_w0[:, kc, c * P:(c + 1) * P],
                                   actT[:, kc, b * S:(b + 1) * S], start=kc == 0, stop=kc == NC - 1)
                elif kind == "k":
                    c = job[1]
                    ps, filled = take_narrow((job, b), 2, among)
                    for off, n, src in ((0, S, actT[:, :, b * S:(b + 1) * S]), (S, T, ctxT[:, :, b * T:(b + 1) * T])):
                        for kc in range(NC):
                            m = mm(ps[:, off:off + n], kv_w0[:, kc, 0, c * P:(c + 1) * P],
                                   src[:, kc, :], start=kc == 0, stop=kc == NC - 1)
                elif kind == "v":
                    ps, filled = take_narrow((job, b), 2, among)
                    for i in range(2 if job[1] == 0 else 1):
                        for kc in range(NC):
                            if job[1] == 0:
                                src = actT[:, kc, b * S + i * P:b * S + (i + 1) * P]
                            else:
                                if kc == 0:
                                    pe.wait_ge(ctxd_ready, 1)
                                src = ctxD[:, kc, b, :, :].rearrange("p a k -> p (a k)")
                            m = mm(ps[:, i * D:(i + 1) * D], src, kv_w0[:, kc, 1, :], start=kc == 0, stop=kc == NC - 1)
                elif kind == "qhot":
                    ps, filled = take_narrow((job, b), 2, among)
                    pe.wait_ge(*narrow.empty((("q",), b)))
                    for i in range(2):
                        r = 2 * job[1] + i
                        for part in range(2):
                            m = mm(ps[:, i * S:(i + 1) * S], place[:, part, (r % 4) * P:(r % 4 + 1) * P],
                                   qparts[:, part, r // 4, :], start=part == 0, stop=part == 1)
                else:
                    ps, filled = take_narrow((job, b), 1, among)
                    lo, hi = 512 * job[1], 512 * (job[1] + 1)
                    for r in range(lo // KEYS0, -(-hi // KEYS0)):
                        if r % 4 == 0 or r == lo // KEYS0:
                            pe.wait_ge(*narrow.empty((("k", r // 4), b)))
                        a, z = max(lo, r * KEYS0), min(hi, (r + 1) * KEYS0)
                        for part in range(2):
                            m = mm(ps[:, a - lo:z - lo], place[:, 2 + part, (r % 4) * P:(r % 4 + 1) * P],
                                   kparts[:, part, r // 4, a - r * KEYS0:z - r * KEYS0], start=part == 0, stop=part == 1)
                m.then_inc(filled, 1)

            def scores0(u):
                b, r, q = units0[u]
                ps, filled = take_wide(("S", u), 2, SCORES)
                if q == 0:
                    pe.wait_ge(*narrow.empty((("qhot", r // 2), b)))
                    for piece in range(r * KEYS0 // 512, -(-(r + 1) * KEYS0 // 512)):
                        pe.wait_ge(*narrow.empty((("kpair", piece), b)))
                for i in range(2):
                    m = mm(ps[:, i * 512:i * 512 + KEYS0], qhot[:, r, i, q * P:(q + 1) * P], kpair[:, r, :],
                           start=True, stop=True)
                m.then_inc(filled, 1)

            def values0(u):
                b, r, q = units0[u]
                c = r // 4
                if r % 4 == 0 and q == 0:
                    ao[0] = take_narrow(("ao", 0, b, c), among=ATTENDED)
                ps, filled = ao[0]
                pe.wait_ge(*wide.empty(("T", u)))
                if q == 0 and r == 0:
                    for i in range(2):
                        pe.wait_ge(*narrow.empty((("v", i), b)))
                vp = vpad0[b % 2]
                for j in range(5):
                    i, kb = j // 2, j % 2
                    lhs = (vp[:, (kb * 16 + 2 * r + i) * 64:(kb * 16 + 2 * r + i + 1) * 64] if j < 4 else
                           vp[:, 2048 + r * 64:2048 + (r + 1) * 64])
                    po = 64 * (r % 4 // 2)
                    m = mm(ps[po:po + 64, qoff(q)], lhs, probsT[:, u % 2, j * P:(j + 1) * P],
                           start=(r % 2, q, j) == (0, 0, 0), stop=(r % 2, q, j) == (1, 1, 4))
                if r % 4 == 3 and q == 1:
                    m.then_inc(filled, 1)

            ao = [None]
            pe.wait_ge(placed, 5)
            for job in START0[0]:
                side_product0(job, 0, (0, 1))
            n0 = len(units0)
            for step in range(-3, n0 + 3):
                if step == -1:
                    for job in START0[1]:
                        side_product0(job, 0, (0, 1))
                if 0 <= step < n0:
                    turn_probs(step)
                if step + 3 < n0:
                    scores0(step + 3)
                if 0 <= step - 1 < n0:
                    values0(step - 1)
                job, b = side0(step)
                if job:
                    side_product0(job, b, SIDE)
            pe.wait_ge(load["cols"], 16 * LOADS["cols"])
            ps, filled = take_wide("cols")
            for i in range(2):
                m = nc.tensor.transpose(ps[:, i * P:(i + 1) * P], colraw[:, 1 + i, :], ident[:])
            m.then_inc(filled, 1)
            pe.wait_ge(wk_ready, 2)
            keys_small(1, lambda kc, c: wkrep[:, kc, c, :])
            norm_turn(0)
            mlp(0)

            turn("x1T", xA, lambda q: pe.wait_ge(*narrow.empty(("down", 0, q))))
            pe.wait_ge(load["w1"], 16 * 4)
            queries(1, q_w1, "x1T")

            values_small(1, v_w1, 64)

            def scores1(i):
                q, c = units1[i]
                ps, filled = take_wide(("S", base["1"] + i), among=SCORES)
                if i == 0:
                    pe.wait_ge(*wide.empty(("q", 1, 0)))
                    pe.wait_ge(*wide.empty(("q", 1, 1)))
                    pe.wait_ge(kbd_ready, 2)
                for g in range(2):
                    m = mm(ps[:, g * 512:(g + 1) * 512], qT[:, c, qoff(q)], kbd1[:, c, q // 2, 8 * g:8 * g + 8, :],
                           start=True, stop=True)
                m.then_inc(filled, 1)

            def values1(i):
                q, c = units1[i]
                u = base["1"] + i
                ps, filled = take_narrow(("ao", 1, q, c))
                pe.wait_ge(*wide.empty(("T", u)))
                if i == 0:
                    pe.wait_ge(*wide.empty(("v", 1)))
                for j in (0, 2, 4, 6, 1, 3, 5, 7):
                    po = 32 * (j // 2)
                    m = mm(ps[po:po + 32, 0:P], vpad1[:, q // 2, 8 * c + j, :], probsT[:, u % 2, j * P:(j + 1) * P],
                           start=j % 2 == 0, stop=j % 2 == 1)
                m.then_inc(filled, 1)

            n1 = len(units1)
            for step in range(-3, n1 + 2):
                if step + 3 < n1:
                    scores1(step + 3)
                if 0 <= step < n1:
                    turn_probs(base["1"] + step)
                if 0 <= step - 1 < n1:
                    values1(step - 1)
                if step - 2 >= 0 and units1[step - 2][1] == 1:
                    q = units1[step - 2][0]
                    project(1, q, out_w1, [("ao", 1, q, 0), ("ao", 1, q, 1)])

            def weights2(a, h):
                g = 4 * a + h // GROUP
                wbuf = wring[g % 2]
                return [wbuf[:, m, :].rearrange("p (c n) -> p c n", c=NC) for m in range(3)] + [
                    wbuf[:, 3, :].rearrange("p (h n) -> p h n", h=GROUP)]

            def head_products2(a, h):
                g = 4 * a + h // GROUP
                wq, _, _, wo = weights2(a, h)
                o = (h % GROUP) * P
                if h % GROUP == 0:
                    pe.wait_ge(ring_loaded[g % 2], 64 * (g // 2 + 1))
                if h == 0:
                    pe.wait_ge(hot_ready, a + 1)
                ps, filled = take_wide(("kvq", a, h), 4, among=(0,))
                _, high, low = kv_weights(a, h)
                pe.wait_ge(ctx_split, a + 1)
                pe.wait_ge(kv_split, a * H2 + h + 1)
                for m in range(2):
                    for kc in range(NC):
                        for i, (w, part) in enumerate(((high, 0), (low, 0), (high, 1))):
                            mm(ps[:, m * 256:(m + 1) * 256], w[:, m, kc, :], cparts[:, part, kc, :],
                               start=kc == 0 and i == 0, stop=kc == NC - 1 and i == 2)
                mm(ps[0:16, 768:1024], bvhot[:, h, :], wo[:, h % GROUP, :], start=True, stop=True)
                for kc in range(NC):
                    m = nc.tensor.transpose(ps[:, 512 + kc * P:512 + (kc + 1) * P], wq[:, kc, o:o + P], ident[:])
                m.then_inc(filled, 1)

            def precompute2(a):
                head_products2(a, 0)
                for h in range(H2):
                    if h + 1 < H2:
                        head_products2(a, h + 1)
                    if h in TURN_AT[a]:
                        norm_turn(2 + a, (TURN_AT[a].index(h),), (2,))
                    wo = weights2(a, h)[3]
                    hb = heads[:, h % 2, :]
                    ps, filled = take_wide(("G", a, h), among=(1,))
                    pe.wait_ge(*wide.empty(("kvq", a, h)))
                    pe.wait_ge(bias_key, a * H2 + h + 1)
                    for c in range(NC):
                        m = mm(ps[:, c * 512:c * 512 + NK2], hb[:, 513 + c * P:513 + (c + 1) * P], hb[:, 0:NK2],
                               start=True, stop=True)
                    m.then_inc(filled, 1)
                    bq = column(f"L2_bq{a + 1}", h)
                    ps, filled = take_narrow(("cB", a, h))
                    mm(ps[:, 0:NK2], bq.broadcast_to([P, P]), hb[:, 0:NK2], start=True, stop=True).then_inc(filled, 1)
                    if h % 2 == 0:
                        vw = take_wide(("VW", a, h // 2), among=(2,))
                    ps, filled = vw
                    po = T * (h % 2)
                    for b in range(B):
                        m = mm(ps[po:po + T, b * D:(b + 1) * D], hb[:, 257 + b * T:257 + (b + 1) * T],
                               wo[:, h % GROUP, :], start=True, stop=True)
                    if h % 2 == 1:
                        m.then_inc(filled, 1)

            def scores2(a, q):
                u = base["2a" if a == 0 else "2b"] + q
                b = q // 2
                ps, filled = take_wide(("S", u), among=SCORES)
                if q == 0:
                    for half in range(2):
                        pe.wait_ge(*wide.empty((("ln", 2 + a), half)))
                for g in range(2):
                    for c in range(NC):
                        m = mm(ps[:, g * 512:(g + 1) * 512], actT[:, c, qoff(q)],
                               G[:, c, 8 * g:8 * g + 8, b * T:(b + 1) * T], start=c == 0, stop=c == NC - 1)
                m.then_inc(filled, 1)

            def scores2_bias(ps, q):
                for c in range(NC):
                    m = mm(ps[:, 0:H2], actT[:, c, qoff(q)], G[:, c, :, NK2 - 1], start=c == 0, stop=c == NC - 1)
                return m

            def attend2(a):
                u0 = base["2a" if a == 0 else "2b"]
                for h in range(H2):
                    pe.wait_ge(*wide.empty(("G", a, h)))
                for step in range(-3, NQ + 1):
                    if step + 3 < NQ:
                        scores2(a, step + 3)
                    if 0 <= step < NQ:
                        turn_probs(u0 + step)
                    if step < NQ:
                        ps, filled = take_narrow(("X", a, step), int(step + 3 < NQ) + int(step >= 0))
                        if step + 3 < NQ:
                            m = scores2_bias(ps, step + 3)
                        if step >= 0:
                            m = nc.tensor.transpose(ps[0:16, P:2 * P], probsb[:, (u0 + step) % 2, :], ident[:])
                        m.then_inc(filled, 1)
                    if step >= 1:
                        q = step - 1
                        u = u0 + q
                        ps, filled = take_narrow(("proj", 2 + a, q))
                        pe.wait_ge(*wide.empty(("T", u)))
                        pe.wait_ge(*narrow.empty(("X", a, q)))
                        if q == 0:
                            for r in range(8):
                                pe.wait_ge(*wide.empty(("VW", a, r)))
                        for r in range(8):
                            mm(ps[:, 0:D], probsT[:, u % 2, r * P:(r + 1) * P], VW[:, q // 2, r, :],
                               start=r == 0, stop=False)
                        mm(ps[:, 0:D], probsbT[:, u % 2, :], vwb[:, :], start=False, stop=True).then_inc(filled, 1)

            precompute2(0)
            attend2(0)
            precompute2(1)
            attend2(1)
            pe.wait_ge(load["w3"], 64)
            keys_small(3, lambda kc, c: w3[1][:, kc, c * P:(c + 1) * P])
            values_small(3, w3[2], 256)
            norm_turn(4)
            mlp(1)

            norm_turn(5)
            queries(3, w3[0], ("ln", 5))

            def scores3(q):
                ps, filled = take_wide(("S", base["3"] + q), among=SCORES)
                if q == 0:
                    pe.wait_ge(*wide.empty(("q", 3, 0)))
                    pe.wait_ge(*wide.empty(("q", 3, 1)))
                    pe.wait_ge(kbd_ready, 4)
                for c in range(NC):
                    m = mm(ps[:, c * 512:(c + 1) * 512], qT[:, c, qoff(q)], kbd3[:, c, q // 2, :, :],
                           start=True, stop=True)
                m.then_inc(filled, 1)

            def values3(q):
                u = base["3"] + q
                ps, filled = take_narrow(("ao", 3, q), 2)
                pe.wait_ge(*wide.empty(("T", u)))
                if q == 0:
                    pe.wait_ge(*wide.empty(("v", 3)))
                for c in range(NC):
                    for j in range(4):
                        m = mm(ps[32 * j:32 * j + 32, c * P:(c + 1) * P], vpad3[:, q // 2, 4 * c + j, :],
                               probsT[:, u % 2, (4 * c + j) * P:(4 * c + j + 1) * P], start=True, stop=True)
                m.then_inc(filled, 1)

            for step in range(-3, NQ + 2):
                if step + 3 < NQ:
                    scores3(step + 3)
                if 0 <= step < NQ:
                    turn_probs(base["3"] + step)
                if 0 <= step - 1 < NQ:
                    values3(step - 1)
                if step >= 2:
                    project(4, step - 2, w3[3], [("ao", 3, step - 2)])
            norm_turn(6)
            mlp(2)

        @block.sync
        def _(sp):
            def halves(dst, src):
                return dst, src.rearrange("(c p) n -> p c n", p=P)

            sp.dma_start(xA, t["x"].rearrange("b (h p) d -> p (b h) d", p=P)).then_inc(load["x"], 16)
            sp.dma_start(xn[:, 0:2, :], t["ctx_2048"].rearrange("(g b) k d -> (b k) g d", g=2)).then_inc(load["ctx"], 16)
            sp.dma_start(*halves(q_w0, t["L0_xattn_q_w"])).then_inc(load["w0"], 16)
            sp.dma_start(w0[:, 512:1536].rearrange("p (c n) -> p c n", c=NC),
                         t["L0_xattn_kv_w"].rearrange("(c p) n -> p c n", p=P)).then_inc(load["w0"], 16)
            sp.dma_start(*halves(out_w0, t["L0_xattn_out_w"])).then_inc(load["w0"], 16)
            sp.dma_start(mask0i, t["mask_BxS2_ik0"].rearrange("(a b) k -> a (b k)", a=1).broadcast_to([P, B * T])).then_inc(load["masks"], 16)
            sp.dma_start(mask3i, t["mask_BxS2_bf1"].rearrange("(a b) k -> a (b k)", a=1).broadcast_to([P, B * T])).then_inc(load["masks"], 16)
            sp.dma_start(mask1[:], t["mask_Bx1xSxS2_ff0"].rearrange("b o (h p) k -> p (b o h) k", p=P)).then_inc(load["masks"], 16)
            for i, name in enumerate(ROWS):
                key = name[:3] + "xattn_" + name[3:]
                sp.dma_start(rows[:, i, :], t[key].rearrange("(a d) -> a d", a=1).broadcast_to([P, D])).then_inc(load["rows"], 16)
            sp.wait_ge(cols_zeroed, 1)
            for dst, src, apart in parameter_rows(False):
                sp.dma_start(dst, src, allow_slow_non_contiguous=apart).then_inc(load["cols"], 16)
            sp.dma_start(*halves(mlp_load(0, 0), t["L0_xattn_mlp_w1"])).then_inc(load["mlp0"], 16)
            sp.dma_start(*halves(mlp_load(0, 1), t["L0_xattn_mlp_w2"])).then_inc(load["mlp0"], 16)
            sp.dma_start(*halves(q_w1, t["L1_xattn_Wq"])).then_inc(load["w1"], 16)
            sp.dma_start(*halves(k_w1, t["L1_xattn_Wk"])).then_inc(load["w1"], 16)
            sp.dma_start(*halves(v_w1, t["L1_xattn_Wv"])).then_inc(load["w1"], 16)
            sp.dma_start(*halves(out_w1, t["L1_xattn_Wo"])).then_inc(load["w1"], 16)

            for g in range(8):
                a, h0 = g // 4, (g % 4) * GROUP
                if g < 2:
                    sp.wait_ge(*narrow.full(("down", 0, NQ - 1)))
                else:
                    sp.wait_ge(*wide.full(("VW", (g - 2) // 4, 2 * ((g - 2) % 4) + 1)))
                wbuf = wring[g % 2]
                for m, w in enumerate(("wq", "wk", "wv")):
                    sp.dma_start(wbuf[:, m, :].rearrange("p (c n) -> p c n", c=NC),
                                 t[f"L2_xattn_{w}{a + 1}"].rearrange("(c p) n -> p c n", p=P)[:, :, h0 * P:(h0 + GROUP) * P]
                                 ).then_inc(ring_loaded[g % 2], 16)
                sp.dma_start(wbuf[:, 3, :].rearrange("p (h n) -> p h n", h=GROUP),
                             t[f"L2_xattn_wo{a + 1}"].rearrange("(h p) n -> p h n", p=P)[:, h0:h0 + GROUP, :]
                             ).then_inc(ring_loaded[g % 2], 16)
                if g == 3:
                    sp.wait_ge(*narrow.full(("proj", 1, NQ - 1)))
                    for w, key in zip(w3, ("q_w", "k_w", "v_w", "cproj_w")):
                        sp.dma_start(*halves(w, t["L3_xattn_" + key])).then_inc(load["w3"], 16)
            sp.wait_ge(*wide.full(("VW", 1, 5)))
            sp.dma_start(*halves(mlp_load(1, 0), t["L2_xattn_w_fc1"])).then_inc(load["mlp2"], 16)
            sp.dma_start(*halves(mlp_load(1, 1), t["L2_xattn_w_fc2"])).then_inc(load["mlp2"], 16)
            sp.wait_ge(*narrow.full(("down", 1, NQ - 1)))
            sp.dma_start(*halves(mlp_load(2, 0), t["L3_xattn_fc_w"])).then_inc(load["mlp3"], 16)
            sp.dma_start(*halves(mlp_load(2, 1), t["L3_xattn_proj_w"])).then_inc(load["mlp3"], 16)
            for q in range(NQ):
                sp.wait_ge(*narrow.empty(("down", 2, q)))
                sp.dma_start(out.rearrange("b (h p) d -> p (b h) d", p=P)[:, q, :], xB[:, q, :]).then_inc(stored, 16)
            sp.wait_ge(stored, 16 * NQ)

        @block.scalar
        def _(act):
            act.wait_ge(cols_zeroed, 1)
            for dst, src, apart in parameter_rows(True):
                act.dma_start(dst, src, allow_slow_non_contiguous=apart).then_inc(load["cols0"], 16)

            def evac(dst, src, ring, key, **kw):
                nc.scalar.activation(dst, src, ACT.Identity, **kw).then_inc(ring.drained[ring.slot(key)], 1)

            def turned(key, dst):
                for half in range(2):
                    act.wait_ge(*wide.full((key, half)))
                    evac(dst[:, :, half * 512:(half + 1) * 512],
                         wide_ps[:, wide.slot((key, half)), :].rearrange("p (c n) -> p c n", c=NC), wide, (key, half))

            def norm_turned(k, w, b, halves=(0, 1)):
                for half in halves:
                    key = (("ln", k), half)
                    act.wait_ge(*wide.full(key))
                    for c in range(NC):
                        kw = {"scale": column(w, c)}
                        if b:
                            kw["bias"] = column(b, c)
                        evac(actT[:, c, half * 512:(half + 1) * 512],
                             wide_ps[:, wide.slot(key), c * 512:(c + 1) * 512], wide, key, **kw)

            def queries(layer, b):
                for c in range(NC):
                    key = ("q", layer, c)
                    act.wait_ge(*wide.full(key))
                    evac(qT[:, c, :], wide_ps[:, wide.slot(key), :], wide, key, bias=column(b, c))

            def mlp(n, func, b1):
                act.wait_ge(prob_ready, probcount[base["1"] if n == 0 else base["3"] if n == 1 else len(probcount) - 1])
                for half in range(2):
                    for fp in range(NF // 2):
                        key = ("up", n, half, fp)
                        i = 4 * half + fp
                        act.wait_ge(*wide.full(key))
                        if i >= 3:
                            act.wait_ge(hidden_split, 8 * n + i - 2)
                        for j in range(2):
                            f = 2 * fp + j
                            nc.scalar.activation(scoresb[:, i % 3, j * 512:(j + 1) * 512],
                                                 wide_ps[:, wide.slot(key), j * 512:(j + 1) * 512], func,
                                                 bias=column(b1, f)).then_inc(wide.drained[wide.slot(key)], 1)

            def probs_turned(u):
                key = ("T", u)
                act.wait_ge(*wide.full(key))
                n = 5 if u < len(units0) else 8
                evac(probsT[:, u % 2, 0:n * P], wide_ps[:, wide.slot(key), 0:n * P], wide, key)

            def side0_copy(job, b):
                key = (job, b)
                if job[0] in ("proj", "v"):
                    return
                act.wait_ge(*narrow.full(key))
                if job == ("qhot", 0) and b == 0:
                    act.wait_ge(placed, 6)
                ps = narrow_ps[:, narrow.slot(key), :]
                if job[0] == "kpair":
                    evac(kpair[:].rearrange("p r k -> p (r k)")[:, 512 * job[1]:512 * (job[1] + 1)], ps, narrow, key)
                elif job[0] == "qhot":
                    evac(qhot[64:P, 2 * job[1]:2 * job[1] + 2, 1, :], ps[64:P, :].rearrange("p (r n) -> p r n", r=2),
                         narrow, key)
                elif job[0] == "q":
                    for c in range(NC):
                        evac(qparts[:, 0, c, :], ps[:, c * S:(c + 1) * S], narrow, key, bias=column("L0_q_b", c))
                else:
                    evac(kparts[:, 0, job[1], :], ps[:, 0:KEYS0], narrow, key, bias=column("L0_k_b", job[1]))

            def exp0(u):
                key = ("S", u)
                act.wait_ge(max_ready, u + 1)
                if u >= 3:
                    act.wait_ge(prob_ready, probcount[u - 2])
                for i in range(2):
                    nc.scalar.activation(scoresb[:, u % 3, i * KEYS0:(i + 1) * KEYS0],
                                         wide_ps[:, wide.slot(key), i * 512:i * 512 + KEYS0], ACT.Exp,
                                         scale=1.0 / 16, bias=mx[:, u % 3, i:i + 1],
                                         accum_out=sums[:, u % 3, i:i + 1]).then_inc(wide.drained[wide.slot(key)], 1)

            def exp(u, n):
                if n == 1024:
                    act.wait_ge(max_ready, u + 1)
                    for h in range(DIRECT):
                        nc.scalar.activation(scoresb[:, u % 3, h * T:(h + 1) * T], scoresb[:, u % 3, h * T:(h + 1) * T],
                                             ACT.Exp, bias=negmx[:, u % 3, h:h + 1], accum_out=sums[:, u % 3, h:h + 1])
                    act.wait_ge(shifted, shiftcount[u + 1])
                    nc.scalar.activation(scoresb[:, u % 3, DIRECT * T:n], scoresb[:, u % 3, DIRECT * T:n], ACT.Exp
                                         ).then_inc(exp_done, 1)
                    return
                act.wait_ge(shifted, shiftcount[u + 1])
                nc.scalar.activation(scoresb[:, u % 3, 0:n], scoresb[:, u % 3, 0:n], ACT.Exp).then_inc(exp_done, 1)

            def attended(layer, q, c, vb):
                key = ("ao", layer, q, c)
                act.wait_ge(*narrow.full(key))
                evac(qT[:, c, qoff(q)], narrow_ps[:, narrow.slot(key), 0:P], narrow, key, bias=column(vb, c))

            def keys_small(layer, kb):
                key = ("k", layer)
                act.wait_ge(*wide.full(key))
                for c in range(NC):
                    evac(kT2[:, c, :], wide_ps[:, wide.slot(key), c * 256:(c + 1) * 256], wide, key, bias=column(kb, c))

            turned("x0T", actT)
            act.wait_ge(*wide.full("ctxT"))
            evac(ctxT[:], wide_ps[:, wide.slot("ctxT"), 0:512].rearrange("p (c n) -> p c n", c=NC), wide, "ctxT")
            act.wait_ge(*wide.full("cols0"))
            evac(col[:, 0, :], wide_ps[:, wide.slot("cols0"), 0:P], wide, "cols0")
            act.wait_ge(*wide.empty("cols0"))
            for job in START0[0]:
                side0_copy(job, 0)
            n0 = len(units0)
            for step in range(-2, n0 + 2):
                if step == 0:
                    for job in START0[1]:
                        side0_copy(job, 0)
                job, b = side0(step - 1)
                if job:
                    side0_copy(job, b)
                if step - 2 >= 0 and (step - 2) % 8 == 7:
                    b, c = (step - 2) // 16, (step - 2) // 8 % 2
                    key = ("ao", 0, b, c)
                    act.wait_ge(*narrow.full(key))
                    evac(qT[:, c, b * S:(b + 1) * S], narrow_ps[:, narrow.slot(key), 0:S], narrow, key,
                         bias=column("L0_v_b", c))
                if 0 <= step < n0:
                    probs_turned(step)
                if step + 2 < n0:
                    exp0(step + 2)
                if step in (20, 36):
                    act.wait_ge(load["mlp0"], 32)
                    mlp_high(nc.scalar.copy, 0, step // 36).then_inc(w_high, 1)
            act.wait_ge(*wide.full("cols"))
            evac(col[:, 1:3, :], wide_ps[:, wide.slot("cols"), 0:256].rearrange("p (a b) -> p a b", a=2), wide, "cols")
            act.wait_ge(*wide.empty("cols"))
            keys_small(1, "L1_bk")
            norm_turned(0, "L0_postnorm_w", None)
            act.wait_ge(*narrow.full(("proj", 0, NQ - 1)))
            for chunk in (2, 3):
                mlp_high(nc.scalar.copy, 0, chunk).then_inc(w_high, 1)
            mlp(0, ACT.Gelu_apprx_tanh, "L0_mlp_b1")

            turned("x1T", actT)
            queries(1, "L1_bq")

            n1 = len(units1)
            for step in range(-2, n1 + 2):
                if step - 2 >= 0:
                    attended(1, *units1[step - 2], "L1_bv")
                if 0 <= step < n1:
                    probs_turned(base["1"] + step)
                if step + 2 < n1:
                    exp(base["1"] + step + 2, 1024)

            def head2(a, h):
                key = ("kvq", a, h)
                act.wait_ge(*wide.full(key))
                ps = wide_ps[:, wide.slot(key), :]
                hb = heads[:, h % 2, :]
                evac(hb[:, 0:256], ps[:, 0:256], wide, key, bias=column(f"L2_bk{a + 1}", h))
                evac(hb[:, 257:513], ps[:, 256:512], wide, key, bias=column(f"L2_bv{a + 1}", h))
                nc.scalar.copy(hb[:, 256:257], column(f"L2_bias_k{a + 1}", h)).then_inc(bias_key, 1)

            def weights_high(a, h):
                g = 4 * a + h // GROUP
                if h % GROUP == 0:
                    act.wait_ge(ring_loaded[g % 2], 64 * (g // 2 + 1))
                loaded, high, _ = kv_weights(a, h)
                nc.scalar.copy(high, loaded).then_inc(kv_high, 1)

            def precompute2(a):
                for h in range(2):
                    weights_high(a, h)
                head2(a, 0)
                for h in range(H2):
                    if h + 2 < H2:
                        weights_high(a, h + 2)
                    if h + 1 < H2:
                        head2(a, h + 1)
                    if h in TURN_AT[a]:
                        norm_turned(2 + a, f"L2_ln{a + 1}_scale", f"L2_ln{a + 1}_offset", (TURN_AT[a].index(h),))
                    key = ("cB", a, h)
                    act.wait_ge(*narrow.full(key))
                    if a == 0 and h == 8:
                        act.wait_ge(xn_ready, 2 * NQ)
                    nc.scalar.mul(cB[:, h, :], narrow_ps[:, narrow.slot(key), 0:NK2], DH2 ** -0.5
                                  ).then_inc(narrow.drained[narrow.slot(key)], 1)
                    if h % 2 == 1:
                        key = ("VW", a, h // 2)
                        act.wait_ge(*wide.full(key))
                        evac(VW[:, :, h // 2, :], wide_ps[:, wide.slot(key), :].rearrange("p (b n) -> p b n", b=B), wide, key)

            def attend2(a):
                u0 = base["2a" if a == 0 else "2b"]
                for step in range(-2, NQ):
                    if step >= 0:
                        probs_turned(u0 + step)
                    if step + 2 < NQ:
                        exp(u0 + step + 2, 16 * 65)
                    if a == 1 and 2 <= step < 6:
                        if step == 2:
                            act.wait_ge(load["mlp2"], 32)
                            act.wait_ge(*wide.full(("VW", 1, 7)))
                        mlp_high(nc.scalar.copy, 1, step - 2).then_inc(w_high, 1)

            precompute2(0)
            attend2(0)
            precompute2(1)
            attend2(1)
            keys_small(3, "L3_k_b")
            norm_turned(4, "L2_ln_mlp_scale", "L2_ln_mlp_offset")
            mlp(1, ACT.Gelu, "L2_b_fc1")
            norm_turned(5, "L3_ln1_w", "L3_ln1_b")
            queries(3, "L3_q_b")
            for step in range(-2, NQ + 2):
                if step >= 2:
                    key = ("ao", 3, step - 2)
                    act.wait_ge(*narrow.full(key))
                    for c in range(NC):
                        evac(qT[:, c, qoff(step - 2)], narrow_ps[:, narrow.slot(key), c * P:(c + 1) * P], narrow, key,
                             bias=column("L3_v_b", c))
                if 0 <= step < NQ:
                    probs_turned(base["3"] + step)
                if step + 2 < NQ:
                    exp(base["3"] + step + 2, 1024)
                if 4 <= step < 8:
                    act.wait_ge(load["mlp3"], 32)
                    mlp_high(nc.scalar.copy, 2, step - 4).then_inc(w_high, 1)
            norm_turned(6, "L3_ln2_w", "L3_ln2_b")
            mlp(2, ACT.Gelu_apprx_tanh, "L3_fc_b")

        @block.vector
        def _(dve):
            v = nc.vector
            chain = [0]

            def link(ins):
                chain[0] += 1
                ins.then_inc(link_dve, 1)
                dve.wait_ge(link_dve, chain[0])

            def stat(k, q):
                src, eps = NORMS[k]
                link(v.bn_stats(stats[:, q, :], src[:, q, :]))
                link(v.bn_aggr(mv[:, q, :], stats[:, q, :]))
                if k == 0:
                    link(v.scalar_tensor_tensor(out=mv[:, q, 1:2], in0=mv[:, q, 0:1], scalar=mv[:, q, 0:1],
                                                in1=mv[:, q, 1:2], op0=ALU.mult, op1=ALU.add))
                v.tensor_scalar_add(veps[:, q:q + 1], mv[:, q, 1:2], eps).then_inc(stat_ready, 1)

            def norm(k, q):
                src, _ = NORMS[k]
                dve.wait_ge(rstd_ready, k * NQ + q + 1)
                if k == 0:
                    ins = v.tensor_scalar(xn[:, q, :], src[:, q, :], rstd[:, q:q + 1], None, ALU.mult)
                else:
                    ins = v.tensor_scalar(xn[:, q, :], src[:, q, :], mv[:, q, 0:1], rstd[:, q:q + 1],
                                          ALU.subtract, ALU.mult)
                ins.then_inc(xn_ready, 1)

            NORMS = [(xB, 1e-6), (xA, 1e-6), (xB, 1e-5), (xB, 1e-5), (xB, 1e-5), (xB, 1e-5), (xB, 1e-5)]

            def stream_norm(k, q, before, key, dst, n):
                if before is not None and k is not None:
                    norm(k, before)
                if q is not None:
                    add_residual(key, dst, q, n)
                    if k is not None:
                        dve.wait_ge(*narrow.empty(key))
                        stat(k, q)

            def add_residual(key, dst, q, n):
                dve.wait_ge(*narrow.full(key))
                dve.wait_ge(row_added, n * NQ + q + 1)
                v.tensor_tensor(dst[:, q, :], narrow_ps[:, narrow.slot(key), 0:D], dst[:, q, :], ALU.add
                                ).then_inc(narrow.drained[narrow.slot(key)], 1)

            def weights_low(n, chunk):
                dve.wait_ge(w_high, 4 * n + chunk + 1)
                mlp_low(v, n, chunk).then_inc(w_split, 1)

            def mlp(n, k, residual):
                for half in range(2):
                    cols = slice(half * 512, (half + 1) * 512)
                    dve.wait_ge(*wide.empty((("ln", k), half)))
                    v.tensor_copy(xparts[0][:, :, cols], actT[:, :, cols]).then_inc(x_split, 1)
                    dve.wait_ge(x_split, 2 * (2 * n + half) + 1)
                    v.tensor_tensor(xparts[1][:, :, cols], actT[:, :, cols], xparts[0][:, :, cols].bitcast(F32), ALU.subtract
                                    ).then_inc(x_split, 1)
                if n != 1:
                    for chunk in (2, 3):
                        weights_low(n, chunk)
                for half in range(2):
                    if half:
                        dve.wait_ge(*narrow.full(("down", n, NQ // 2 - 1)))
                    for fp in range(NF // 2):
                        dve.wait_ge(*wide.empty(("up", n, half, fp)))
                        src = scoresb[:, (4 * half + fp) % 3, 0:1024].rearrange("p (f n) -> p f n", f=2)
                        high, low = (hidden[:, part, 2 * fp:2 * fp + 2, :] for part in range(2))
                        link(v.tensor_copy(high, src))
                        v.tensor_tensor(low, src, high.bitcast(F32), ALU.subtract).then_inc(hidden_split, 1)
                    for q in range(half * NQ // 2, (half + 1) * NQ // 2):
                        residual(q)

            def front(u, n, scale, addend, n_scores, bias=None):
                key = ("S", u)
                dve.wait_ge(*wide.full(key))
                dve.wait_ge(prob_ready, probcount[u - 2])
                s3 = scoresb[:, u % 3, 0:16 * n_scores].rearrange("p (h k) -> p h k", h=16)
                v.scalar_tensor_tensor(out=s3[:, :, 0:T], in0=wide_ps[:, wide.slot(key), :].rearrange("p (h k) -> p h k", h=16),
                                       scalar=scale, in1=addend, op0=ALU.mult, op1=ALU.add
                                       ).then_inc(wide.drained[wide.slot(key)], 1)
                dve.wait_ge(*wide.empty(key))
                if bias:
                    dve.wait_ge(*narrow.empty(bias))
                if bias:
                    v.tensor_reduce(mx[:, u % 3, :], s3, AX, ALU.max).then_inc(max_ready, 1)
                else:
                    link(v.tensor_reduce(mx[:, u % 3, :], s3, AX, ALU.max))
                    v.tensor_scalar(negmx[:, u % 3, :], mx[:, u % 3, 0:DIRECT], -1.0, None, ALU.mult).then_inc(max_ready, 1)

            def middle(u, n_scores):
                dve.wait_ge(exp_done, shiftcount[u + 1])
                s3 = scoresb[:, u % 3, 0:16 * n_scores].rearrange("p (h k) -> p h k", h=16)
                first = DIRECT if n_scores == T else 0
                link(v.tensor_reduce(sums[:, u % 3, first:], s3[:, first:], AX, ALU.add))
                v.reciprocal(rcp[:, u % 3, :], sums[:, u % 3, :]).then_inc(rcp_ready, 1)

            v.memset(colraw[:].rearrange("p a b -> p (a b)"), 0.0).then_inc(cols_zeroed, 1)
            link(v.memset(bvhot[:].rearrange("p a b -> p (a b)"), 0.0))
            v.memset(place[:].rearrange("p a n -> p (a n)").bitcast(F32), 0.0).then_inc(placed, 1)
            dve.wait_ge(placed, 1)
            dve.wait_ge(consts, 1)
            for i, (lo, hi, by) in enumerate(((0, 2, 1), (2, 4, 1), (0, 4, 2), (1, 4, 2))):
                v.tensor_copy(place[:, i, :].rearrange("p (a j d) -> p a j d", a=8, j=4)[:, :, lo:hi:by, :],
                              ident[:].rearrange("p (a d) -> p a d", d=16).unsqueeze(2).broadcast_to([P, 8, 2, 16])
                              ).then_inc(placed, 1)
            v.memset(qhot[:].rearrange("p r i n -> p (r i n)").bitcast(F32), 0.0).then_inc(placed, 1)
            dve.wait_ge(load["masks"], 48)
            link(v.tensor_scalar(mask0[:].rearrange("p b k -> p (b k)"), mask0i, 0, NEG0, ALU.is_equal, ALU.mult))
            link(v.tensor_scalar(mask3[:].rearrange("p b k -> p (b k)"), mask3i, 0, NEG3, ALU.is_equal, ALU.mult))

            def side0_copy(job, b):
                if job[0] in ("proj", "kpair"):
                    return
                key = (job, b)
                dve.wait_ge(*narrow.full(key))
                ps = narrow_ps[:, narrow.slot(key), :]
                done = narrow.drained[narrow.slot(key)]
                if job[0] in ("q", "k"):
                    parts, n = (qparts, S) if job[0] == "q" else (kparts, KEYS0)
                    chunks = range(NC) if job[0] == "q" else job[1:]
                    _, drained = narrow.empty(key)
                    dve.wait_ge(narrow.drained[narrow.slot(key)], drained - len(chunks))
                    for i, c in enumerate(chunks):
                        v.scalar_tensor_tensor(out=parts[:, 1, c, :], in0=ps[:, i * n:(i + 1) * n],
                                               scalar=column(f"L0_{job[0]}_b", c),
                                               in1=parts[:, 0, c, :].bitcast(F32), op0=ALU.add, op1=ALU.subtract
                                               ).then_inc(done, 1)
                    return
                if job[0] == "qhot":
                    v.tensor_copy(qhot[0:64, 2 * job[1]:2 * job[1] + 2, 0, :],
                                  ps[0:64, :].rearrange("p (r n) -> p r n", r=2)).then_inc(done, 1)
                    return
                if b < 2 and job[1] == 0:
                    dve.wait_ge(vzero, b + 1)
                vp = vpad0[b % 2]
                for kb in range(2 if job[1] == 0 else 0):
                    v.tensor_copy(diagonal(vp, kb * 1024, [(256, 4), (64 + 16, 4), (1, 16)]), ps[:, kb * 256:(kb + 1) * 256].rearrange("p (a h d) -> p a h d", a=4, h=4)
                                  ).then_inc(done, 1)
                for i in range(2 if job[1] == 1 else 0):
                    dst = diagonal(vp, 2048 + 16 * i, [(128, 4), (64 + 32, 2), (1, 16)])
                    src = ps[:, 0:D].rearrange("p (a j two d) -> p a j two d", a=4, two=2, d=16)[:, :, :, i, :]
                    v.tensor_copy(dst[64 * i:64 * i + 64], src[64 * i:64 * i + 64]).then_inc(done, 1)

            def front0(u):
                b, r, q = units0[u]
                key = ("S", u)
                dve.wait_ge(*wide.full(key))
                ps = wide_ps[:, wide.slot(key), :].rearrange("p (i n) -> p i n", i=2)
                link(v.tensor_tensor(ps[:, :, S:KEYS0], ps[:, :, S:KEYS0],
                                     mask0[:, b, :].unsqueeze(1).broadcast_to([P, 2, T]), ALU.add))
                if u >= 3:
                    dve.wait_ge(*wide.empty(("S", u - 3)))
                link(v.tensor_reduce(mx[:, u % 3, 4:6], ps[:, :, 0:KEYS0], AX, ALU.max))
                v.tensor_scalar(mx[:, u % 3, 0:2], mx[:, u % 3, 4:6], -1.0 / 16, None, ALU.mult).then_inc(max_ready, 1)

            def middle0(u):
                dve.wait_ge(*wide.empty(("S", u)))
                v.reciprocal(rcp[:, u % 3, 0:2], sums[:, u % 3, 0:2]).then_inc(rcp_ready, 1)

            dve.wait_ge(*wide.empty("cols0"))
            for job in START0[0]:
                side0_copy(job, 0)
            n0 = len(units0)
            for step in range(-2, n0 + 5):
                if step == 0:
                    for job in START0[1]:
                        side0_copy(job, 0)
                if step + 2 < n0:
                    front0(step + 2)
                if 0 <= step + 1 < n0:
                    middle0(step + 1)
                job, b = side0(step - 1)
                if job:
                    side0_copy(job, b)
                if step in (22, 38):
                    weights_low(0, step // 38)
                q = done0(step)
                stream_norm(0, q, done0(step - 1), ("proj", 0, q), xB, 0)
            dve.wait_ge(*wide.empty("cols"))
            mlp(0, 0, lambda q: add_residual(("down", 0, q), xA, q, 1))

            def kv_low(a, h):
                dve.wait_ge(kv_high, a * H2 + h + 1)
                loaded, high, low = kv_weights(a, h)
                for m in range(2):
                    ins = v.tensor_tensor(low[:, m], loaded[:, m], high[:, m].bitcast(F32), ALU.subtract)
                ins.then_inc(kv_split, 1)

            def split_operands(a):
                dve.wait_ge(prob_ready, probcount[base["2a" if a == 0 else "2b"]])
                link(v.tensor_copy(cparts[:, 0], ctxT[:]))
                v.tensor_tensor(cparts[:, 1], ctxT[:], cparts[:, 0].bitcast(F32), ALU.subtract).then_inc(ctx_split, 1)
                for h in range(2):
                    kv_low(a, h)

            def spread_bias_values(a):
                v.tensor_copy(diagonal(bvhot, 0, [(17, 16)], 256),
                              colrange(f"L2_bias_v{a + 1}")).then_inc(hot_ready, 1)

            spread_bias_values(0)
            dve.wait_ge(*wide.full(("v", 1)))
            dve.wait_ge(vzero, 3)
            ps = wide_ps[:, wide.slot(("v", 1)), :]
            for b in range(B):
                for c in range(NC):
                    for i in range(2):
                        dst = diagonal(region, b * 512 + c * 256 + 8 * i, [(64, 4), (48, 2), (1, 8)])
                        src = ps[:, b * 64 + c * 32:b * 64 + (c + 1) * 32].rearrange("p (k d) -> p k d", d=8).unsqueeze(2).broadcast_to([P, 4, 2, 8])
                        v.tensor_copy(dst[64 * i:64 * i + 64], src[64 * i:64 * i + 64]
                                      ).then_inc(wide.drained[wide.slot(("v", 1))], 1)
            n1 = len(units1)
            for step in range(-2, n1 + 4):
                if 0 <= step < n1:
                    middle(base["1"] + step, T)
                if step + 2 < n1:
                    q, c = units1[step + 2]
                    front(base["1"] + step + 2, 1024, 8 ** -0.5,
                          mask1[:, q, :].unsqueeze(1).broadcast_to([P, 16, T]), T)
                if step == n1 + 1:
                    split_operands(0)
                q = done1(step)
                stream_norm(1, q, done1(step - 1), ("proj", 1, q), xA, 2)

            def head2(a, h):
                key = ("kvq", a, h)
                dve.wait_ge(*wide.full(key))
                ps = wide_ps[:, wide.slot(key), :]
                v.tensor_copy(heads[:, h % 2, 513:769], ps[:, 512:768]).then_inc(wide.drained[wide.slot(key)], 1)
                v.tensor_tensor(vwb[:, :], ps[0:16, 768:1024], vwb[:, :], ALU.add
                                ).then_inc(wide.drained[wide.slot(key)], 1)

            def precompute2(a):
                link(v.memset(vwb[:], 0.0))
                head2(a, 0)
                for h in range(H2):
                    if h + 2 < H2:
                        kv_low(a, h + 2)
                    if h + 1 < H2:
                        dve.wait_ge(*wide.empty(("kvq", a, h)))
                        head2(a, h + 1)
                    key = ("G", a, h)
                    dve.wait_ge(*wide.full(key))
                    v.tensor_copy(G[:, :, h, :], wide_ps[:, wide.slot(key), :].rearrange("p (c n) -> p c n", c=NC)[:, :, 0:NK2]
                                  ).then_inc(wide.drained[wide.slot(key)], 1)
                    if a == 0 and 3 <= h < 3 + NQ:
                        dve.wait_ge(x2_ready, h - 2)
                        stat(2, h - 3)
                    if a == 0 and 4 <= h < 4 + NQ:
                        norm(2, h - 4)

            def attend2(a, rows_before):
                u0 = base["2a" if a == 0 else "2b"]
                for step in range(-2, NQ + 3):
                    if step == -2:
                        for h in range(H2 - 2, H2):
                            dve.wait_ge(*narrow.empty(("cB", a, h)))
                    if 0 <= step < NQ:
                        middle(u0 + step, 65)
                    if step - 1 < NQ:
                        key = ("X", a, step - 1)
                        dve.wait_ge(*narrow.full(key))
                        ps = narrow_ps[:, narrow.slot(key), :]
                        if step + 2 < NQ:
                            u = u0 + step + 2
                            dve.wait_ge(prob_ready, probcount[u - 2])
                            v.scalar_tensor_tensor(out=scoresb[:, u % 3, 0:16 * 65].rearrange("p (h k) -> p h k", h=16)[:, :, T],
                                                   in0=ps[:, 0:16], scalar=DH2 ** -0.5, in1=cB[:, :, NK2 - 1],
                                                   op0=ALU.mult, op1=ALU.add).then_inc(narrow.drained[narrow.slot(key)], 1)
                        if step - 1 >= 0:
                            v.tensor_copy(probsbT[:, (u0 + step - 1) % 2, :], ps[0:16, P:2 * P]
                                          ).then_inc(narrow.drained[narrow.slot(key)], 1)
                    if step + 2 < NQ:
                        q = step + 2
                        b = q // 2
                        front(u0 + q, 1024, DH2 ** -0.5, cB[:, :, b * T:(b + 1) * T], 65, ("X", a, step - 1))
                    if a == 1 and 3 <= step < 7:
                        weights_low(1, step - 3)
                    q = done2(step)
                    stream_norm(3 + a, q, done2(step - 1), ("proj", 2 + a, q), xB, rows_before)
                    if a == 0 and step == NQ:
                        split_operands(1)

            precompute2(0)
            spread_bias_values(1)
            attend2(0, 3)
            precompute2(1)
            attend2(1, 4)

            dve.wait_ge(*wide.full(("v", 3)))
            dve.wait_ge(vzero, 4)
            ps = wide_ps[:, wide.slot(("v", 3)), :]
            for b in range(B):
                for i in range(2):
                    dst = diagonal(region, 12288 + b * 256 + 16 * i, [(P, NC), (32, 4), (1, 16)])
                    src = ps[:, b * 256:(b + 1) * 256].rearrange("p (c j two d) -> p c j two d", c=NC, two=2, d=16)[:, :, :, i, :]
                    v.tensor_copy(dst[64 * i:64 * i + 64], src[64 * i:64 * i + 64]
                                  ).then_inc(wide.drained[wide.slot(("v", 3))], 1)
            mlp(1, 4, lambda q: stream_norm(5, q, q - 1 if q else None, ("down", 1, q), xB, 5))
            norm(5, NQ - 1)
            for step in range(-2, NQ + 4):
                if 0 <= step < NQ:
                    middle(base["3"] + step, T)
                if step + 2 < NQ:
                    q = step + 2
                    front(base["3"] + q, 1024, 0.25, mask3[:, q // 2, :].unsqueeze(1).broadcast_to([P, 16, T]), T)
                if 5 <= step < 7:
                    weights_low(2, step - 5)
                q = done3(step)
                stream_norm(6, q, done3(step - 1), ("proj", 4, q), xB, 6)
            mlp(2, 6, lambda q: add_residual(("down", 2, q), xB, q, 7))

        @block.gpsimd
        def _(pool):
            g = nc.gpsimd
            chain = [0]

            def link(ins):
                chain[0] += 1
                ins.then_inc(link_pool, 1)
                pool.wait_ge(link_pool, chain[0])

            def head_mask(tile, width, heads_):
                link(g.memset(tile[:], 1.0))
                link(g.affine_select(out=tile[:], in_=tile[:], compare_op=ALU.is_ge, fill=0.0, base=0,
                                     pattern=[[-width, heads_]], channel_multiplier=1))
                link(g.affine_select(out=tile[:], in_=tile[:], compare_op=ALU.is_ge, fill=0.0, base=width - 1,
                                     pattern=[[width, heads_]], channel_multiplier=-1))

            def add_row(q, dst, src, name):
                g.tensor_tensor(dst[:, q, :], src[:, q, :], row(name), ALU.add).then_inc(row_added, 1)

            def rstd_of(k, q):
                pool.wait_ge(stat_ready, k * NQ + q + 1)
                g.tensor_tensor(rstd[:, q:q + 1], veps[:, q:q + 1], mhalf[:], ALU.pow).then_inc(rstd_ready, 1)

            def stream_norm(k, q, before, name):
                if q is not None:
                    rstd_of(k, q)
                if before is not None and name:
                    pool.wait_ge(xn_ready, k * NQ + before + 1)
                    add_row(before, xB, xB, name)

            def shift(u, n_scores):
                pool.wait_ge(max_ready, u + 1)
                s3 = scoresb[:, u % 3, 0:16 * n_scores].rearrange("p (h k) -> p h k", h=16)
                first = DIRECT if n_scores == T else 0
                g.tensor_tensor(s3[:, first:], s3[:, first:],
                                mx[:, u % 3, first:].unsqueeze(2).broadcast_to([P, 16 - first, n_scores]), ALU.subtract
                                ).then_inc(shifted, 1)

            def normalize(u, n_scores):
                pool.wait_ge(rcp_ready, u + 1)
                pool.wait_ge(*wide.full(("T", u - 2)))
                s3 = scoresb[:, u % 3, 0:16 * n_scores].rearrange("p (h k) -> p h k", h=16)
                g.tensor_tensor(probs[:, u % 2, :].rearrange("p (h k) -> p h k", h=16), s3[:, :, 0:T],
                                rcp[:, u % 3, :].unsqueeze(2).broadcast_to([P, 16, T]), ALU.mult).then_inc(prob_ready, 1)
                if n_scores > T:
                    g.tensor_tensor(probsb[:, u % 2, :], s3[:, :, T], rcp[:, u % 3, :], ALU.mult).then_inc(prob_ready, 1)

            def normalize0(u):
                pool.wait_ge(rcp_ready, u + 1)
                if u >= 2:
                    pool.wait_ge(*wide.full(("T", u - 2)))
                s3 = scoresb[:, u % 3, 0:2 * KEYS0].rearrange("p (i k) -> p i k", i=2)
                for lo, hi, o in ((0, S, 0), (S, KEYS0, 2 * S)):
                    n = hi - lo
                    g.tensor_tensor(probs[:, u % 2, o:o + 2 * n].rearrange("p (i k) -> p i k", i=2), s3[:, :, lo:hi],
                                    rcp[:, u % 3, 0:2].unsqueeze(2).broadcast_to([P, 2, n]), ALU.mult).then_inc(prob_ready, 1)

            def spread_keys(layer, kbd, mask, heads_):
                pool.wait_ge(*wide.empty(("k", layer)))
                for c in range(NC):
                    g.tensor_tensor(kbd[:, c],
                                    kT2[:, c, :].rearrange("p (b k) -> p b k", b=B).unsqueeze(2).broadcast_to([P, B, heads_, T]),
                                    mask[:].unsqueeze(1).unsqueeze(3).broadcast_to([P, B, heads_, T]), ALU.mult
                                    ).then_inc(kbd_ready, 1)

            link(g.memset(ident[:], 0.0))
            g.affine_select(out=ident[:], in_=ident[:], compare_op=ALU.not_equal, fill=1.0, base=0,
                            pattern=[[-1, P]], channel_multiplier=1).then_inc(consts, 1)
            link(g.memset(mhalf[:], -0.5))
            head_mask(head16, 16, 8)
            head_mask(head8, 8, 16)
            pool.wait_ge(*wide.empty("ctxT"))
            g.tensor_copy(ctxD[:].rearrange("p c b a k -> p (c b) a k"),
                          ctxT[:].rearrange("p c (b k) -> p (c b) k", b=B).unsqueeze(2).broadcast_to([P, NC * B, 2, T])
                          ).then_inc(ctxd_ready, 1)
            for i in range(2):
                g.memset(vpad0[i], 0.0).then_inc(vzero, 1)
            pool.wait_ge(load["rows"], 16 * len(ROWS))
            pool.wait_ge(load["x"], 16)
            for q in range(NQ):
                add_row(q, xB, xA, "L0_out_b")
            for step in range(len(units0) + 5):
                if step < len(units0):
                    normalize0(step)
                if step == 4:
                    pool.wait_ge(*wide.full(("x0T", 1)))
                    pool.wait_ge(row_added, NQ)
                if 4 <= step < 4 + NQ:
                    add_row(step - 4, xA, xA, "L0_mlp_b2")
                if step == 4 + NQ:
                    pool.wait_ge(load["w1"], 64)
                    for kc in range(NC):
                        g.tensor_copy(wkrep[:, kc].rearrange("p c (k r d) -> p (c k) r d", r=4, d=8),
                                      k_w1[:, kc].rearrange("p (k d) -> p k d", d=8).unsqueeze(2).broadcast_to([P, 8, 4, 8])
                                      ).then_inc(wk_ready, 1)
                stream_norm(0, done0(step), None, None)
            spread_keys(1, kbd1, head8, 16)
            pool.wait_ge(*narrow.full(("down", 0, NQ - 1)))
            g.memset(region[:, 0:2048], 0.0).then_inc(vzero, 1)
            pool.wait_ge(*wide.full(("x1T", 1)))
            for q in range(NQ):
                add_row(q, xA, xA, "L1_bo")

            def attend(first, n, n_scores, k, done, name):
                for step in range(-2, n + 4):
                    if 0 <= step < n:
                        normalize(first + step, n_scores)
                    if step + 2 < n:
                        shift(first + step + 2, n_scores)
                    stream_norm(k, done(step), done(step - 1), name)

            attend(base["1"], len(units1), T, 1, done1, None)
            for q in range(NQ):
                pool.wait_ge(xn_ready, NQ + q + 1)
                link(g.tensor_tensor(xn[:, q, :], xn[:, q, :], row("L1_gamma"), ALU.mult))
                g.tensor_tensor(xB[:, q, :], xn[:, q, :], row("L1_beta"), ALU.add).then_inc(x2_ready, 1)
            for q in range(NQ + 1):
                stream_norm(2, q if q < NQ else None, q - 1 if q else None, "L2_bo1")
            attend(base["2a"], NQ, 65, 3, done2, "L2_bo2")
            attend(base["2b"], NQ, 65, 4, done2, "L2_b_fc2")
            pool.wait_ge(*narrow.full(("proj", 3, NQ - 1)))
            g.memset(region[:, 12288:13312], 0.0).then_inc(vzero, 1)
            spread_keys(3, kbd3, head16, 8)
            for q in range(NQ + 1):
                stream_norm(5, q if q < NQ else None, q - 1 if q else None, "L3_cproj_b")
            attend(base["3"], NQ, T, 6, done3, "L3_proj_b")


def kernel(**inputs):
    import numpy as np
    import concourse.bacc as bacc
    from concourse.bass_utils import run_bass_kernel_spmd

    nc = bacc.Bacc("TRN2", target_bir_lowering=False, num_devices=1)
    arrays, args = {}, {}
    for name, value in inputs.items():
        a = np.ascontiguousarray(value)
        if a.dtype == np.bool_:
            a = a.view(np.uint8)
        arrays["in_" + name] = a
        args[name] = nc.dram_tensor("in_" + name, a.shape, mybir.dt.from_np(a.dtype), kind="ExternalInput").ap()
    out = nc.dram_tensor("out", (B, S, D), F32, kind="ExternalOutput").ap()
    build(nc, args, out)
    r = run_bass_kernel_spmd(nc, [arrays], core_ids=[0])
    return r.results[0]["out"]
```
